# Optimizing a Trainium2 kernel written in Bass

```python
import numpy as np
import jax
import jax.numpy as jnp

def _softmax(x, axis=-1):
    return jax.nn.softmax(x, axis=axis)

def _gelu(x):
    return jax.nn.gelu(x, approximate=True)

def _silu(x):
    return jax.nn.silu(x)

def _sigmoid(x):
    return jax.nn.sigmoid(x)

def _layernorm(x, axis=-1, eps=1e-05):
    m = jnp.mean(x, axis=axis, keepdims=True)
    v = jnp.var(x, axis=axis, keepdims=True)
    return (x - m) / jnp.sqrt(v + eps)

def _scatter_add(tgt, idx, src, axis=0):
    return tgt.at[idx].add(src)

def _segment_sum(src, seg, n):
    return jax.ops.segment_sum(src, seg, n)
kernel_name = 'mk_decoder_preln_d1_seqx_r4_f63696'

def setup_inputs(seed: int=0):
    np.random.seed(seed)
    _w = jnp.asarray

    def _rec_inputs():
        import jax
        import jax.numpy as jnp
        _rk = jax.random.key(seed)
        x = -0.0002928 + 1 * jax.random.normal(jax.random.fold_in(_rk, 1), (2, 1024, 256), jnp.float32)
        _lenS = 1024 - jax.random.randint(jax.random.fold_in(_rk, 7), (2,), 0, max(1, 1024 // 4) + 1, jnp.int32)
        _lenS2 = 77 - jax.random.randint(jax.random.fold_in(_rk, 8), (2,), 0, max(1, 77 // 4) + 1, jnp.int32)
        _ctx_1024P = jax.random.normal(jax.random.fold_in(_rk, 11), (2, 16, 256), jnp.float32)
        _ctx_1024c = jax.random.dirichlet(jax.random.fold_in(_rk, 511), 0.3 * jnp.ones((16,), jnp.float32), (2, 77))
        _ctx_1024t = jnp.einsum('bsk,bkd->bsd', _ctx_1024c, _ctx_1024P)
        _ctx_1024t = _ctx_1024t * jax.lax.rsqrt(jnp.mean(jnp.square(_ctx_1024t)) + 1e-12) * 0.953939
        ctx_1024 = -1.39393e-06 + 0.999914 * (_ctx_1024t + 0.3 * jax.random.normal(jax.random.fold_in(_rk, 611), (2, 77, 256), jnp.float32))
        _validS = jnp.arange(1024)[None, :] < _lenS[:, None]
        _validS2 = jnp.arange(77)[None, :] < _lenS2[:, None]
        _causal = jnp.tril(jnp.ones((1024, 1024), dtype=bool))
        mask_BxSxS2_bk1 = jnp.broadcast_to(_validS2[:, None, :], (2, 1024, 77))
        return (x, ctx_1024, mask_BxSxS2_bk1)
    x, ctx_1024, mask_BxSxS2_bk1 = _rec_inputs()

    def _L0_attn_setup():
        import jax, jax.numpy as jnp
        import numpy as np
        HEADS = 16
        HEAD_DIM = 64
        DIM = 256
        INNER = HEADS * HEAD_DIM

        def rotate_half(t):
            x1, x2 = jnp.split(t, 2, axis=-1)
            return jnp.concatenate((-x2, x1), axis=-1)

        def rope_table(n, head_dim, dtype):
            inv_freq = 1.0 / 10000.0 ** (jnp.arange(0, head_dim, 2, dtype=jnp.float32) / head_dim)
            freqs = jnp.arange(n, dtype=jnp.float32)[:, None] * inv_freq[None, :]
            return jnp.concatenate((freqs, freqs), axis=-1).astype(dtype)
        key = jax.random.key(seed)
        k1, k2, k3, k4 = jax.random.split(key, 4)
        x = jax.random.normal(k1, (1, 1024, DIM), dtype=jnp.float32)
        s = 0.02
        W_qkv = jax.random.normal(k2, (DIM, 3 * INNER), dtype=jnp.float32) * s
        W_o1 = jax.random.normal(k3, (INNER, DIM), dtype=jnp.float32) * s
        W_o2 = jax.random.normal(k4, (DIM, DIM), dtype=jnp.float32) * s
        gamma = jnp.ones((DIM,), dtype=jnp.float32)
        return {'x': x, 'W_qkv': W_qkv, 'W_o1': W_o1, 'W_o2': W_o2, 'gamma': gamma}
    _L0_attn_all = _L0_attn_setup()
    _L0_attn_in = {k: v for k, v in _L0_attn_all.items() if k in ('W_qkv', 'W_o1', 'W_o2', 'gamma')}
    del _L0_attn_all

    def _L0_xattn_setup():
        import jax, jax.numpy as jnp
        import numpy as np
        B, TQ, TK, D, H = (2, 512, 512, 256, 16)
        key = jax.random.key(seed)
        ks = jax.random.split(key, 8)
        s = 1.0 / np.sqrt(D)
        x_q = jax.random.normal(ks[0], (B, TQ, D), jnp.float32)
        x_k = jax.random.normal(ks[1], (B, TK, D), jnp.float32)
        x_v = jax.random.normal(ks[2], (B, TK, D), jnp.float32)
        causal = jnp.triu(jnp.ones((TQ, TK), jnp.bool_), k=1)
        attn_mask = jnp.broadcast_to(causal, (B, TQ, TK))
        Wq = jax.random.normal(ks[3], (D, D), jnp.float32) * s
        Wk = jax.random.normal(ks[4], (D, D), jnp.float32) * s
        Wv = jax.random.normal(ks[5], (D, D), jnp.float32) * s
        Wo = jax.random.normal(ks[6], (D, D), jnp.float32) * s
        z = jnp.zeros((D,), jnp.float32)
        return {'x_q': x_q, 'x_k': x_k, 'x_v': x_v, 'attn_mask': attn_mask, 'Wq': Wq, 'bq': z, 'Wk': Wk, 'bk': z, 'Wv': Wv, 'bv': z, 'Wo': Wo, 'bo': z, 'n_heads': H}
    _L0_xattn_all = _L0_xattn_setup()
    _L0_xattn_in = {k: v for k, v in _L0_xattn_all.items() if k in ('Wq', 'bq', 'Wk', 'bk', 'Wv', 'bv', 'Wo', 'bo')}
    del _L0_xattn_all

    def _L0_ffn_setup():
        import jax, jax.numpy as jnp
        import numpy as np
        N_HEADS = 4
        key = jax.random.key(seed)
        k1, k2, k3, k4 = jax.random.split(key, 4)
        dmodel, n_experts, expert_size = (256, 64, 128)
        B, S = (4, 512)
        x = jax.random.normal(k1, (B, S, dmodel), dtype=jnp.float32)
        expert_sel = jax.random.normal(k2, (n_experts, dmodel), dtype=jnp.float32) * dmodel ** (-0.5)
        keys = jax.random.normal(k3, (n_experts, dmodel, expert_size), dtype=jnp.float32) * dmodel ** (-0.5)
        values = jax.random.normal(k4, (n_experts, expert_size, dmodel), dtype=jnp.float32) * (n_experts * expert_size) ** (-0.5)
        return {'x': x, 'expert_sel': expert_sel, 'keys': keys, 'values': values}
    _L0_ffn_all = _L0_ffn_setup()
    _L0_ffn_in = {k: v for k, v in _L0_ffn_all.items() if k in ('expert_sel', 'keys', 'values')}
    del _L0_ffn_all
    return {'x': x, 'ctx_1024': ctx_1024, 'mask_BxSxS2_bk1': mask_BxSxS2_bk1, 'L0_attn_W_qkv': _L0_attn_in['W_qkv'], 'L0_attn_W_o1': _L0_attn_in['W_o1'], 'L0_attn_W_o2': _L0_attn_in['W_o2'], 'L0_attn_gamma': _L0_attn_in['gamma'], 'L0_xattn_Wq': _L0_xattn_in['Wq'], 'L0_xattn_bq': _L0_xattn_in['bq'], 'L0_xattn_Wk': _L0_xattn_in['Wk'], 'L0_xattn_bk': _L0_xattn_in['bk'], 'L0_xattn_Wv': _L0_xattn_in['Wv'], 'L0_xattn_bv': _L0_xattn_in['bv'], 'L0_xattn_Wo': _L0_xattn_in['Wo'], 'L0_xattn_bo': _L0_xattn_in['bo'], 'L0_ffn_expert_sel': _L0_ffn_in['expert_sel'], 'L0_ffn_keys': _L0_ffn_in['keys'], 'L0_ffn_values': _L0_ffn_in['values']}

def reference(x, ctx_1024, mask_BxSxS2_bk1, L0_attn_W_qkv, L0_attn_W_o1, L0_attn_W_o2, L0_attn_gamma, L0_xattn_Wq, L0_xattn_bq, L0_xattn_Wk, L0_xattn_bk, L0_xattn_Wv, L0_xattn_bv, L0_xattn_Wo, L0_xattn_bo, L0_ffn_expert_sel, L0_ffn_keys, L0_ffn_values):
    import jax
    import jax.numpy as jnp

    def _L0_attn_ref(x, W_qkv, W_o1, W_o2, gamma):
        import jax, jax.numpy as jnp
        import numpy as np
        HEADS = 16
        HEAD_DIM = 64
        DIM = 256
        INNER = HEADS * HEAD_DIM

        def rotate_half(t):
            x1, x2 = jnp.split(t, 2, axis=-1)
            return jnp.concatenate((-x2, x1), axis=-1)

        def rope_table(n, head_dim, dtype):
            inv_freq = 1.0 / 10000.0 ** (jnp.arange(0, head_dim, 2, dtype=jnp.float32) / head_dim)
            freqs = jnp.arange(n, dtype=jnp.float32)[:, None] * inv_freq[None, :]
            return jnp.concatenate((freqs, freqs), axis=-1).astype(dtype)
        b, n, _ = x.shape
        scale = HEAD_DIM ** (-0.5)
        qkv = x @ W_qkv
        q, k, v = jnp.split(qkv, 3, axis=-1)
        to_heads = lambda t: t.reshape(b, n, HEADS, HEAD_DIM).transpose(0, 2, 1, 3)
        q, k, v = (to_heads(q), to_heads(k), to_heads(v))
        pos = rope_table(n, HEAD_DIM, x.dtype)
        cos, sin = (jnp.cos(pos), jnp.sin(pos))
        apply_rope = lambda t: t * cos + rotate_half(t) * sin
        q, k = (apply_rope(q), apply_rope(k))
        dots = jnp.einsum('bhid,bhjd->bhij', q, k) * scale
        causal = jnp.triu(jnp.ones((n, n), dtype=bool), 1)
        neg = -jnp.finfo(dots.dtype).max
        dots = jnp.where(causal, neg, dots)
        attn = jax.nn.softmax(dots, axis=-1)
        out = jnp.einsum('bhij,bhjd->bhid', attn, v)
        out = out.transpose(0, 2, 1, 3).reshape(b, n, INNER)
        out = jax.nn.relu(out @ W_o1) @ W_o2
        mean = jnp.mean(out, axis=-1, keepdims=True)
        var = jnp.var(out, axis=-1, keepdims=True)
        out = (out - mean) * jax.lax.rsqrt(var + 1e-05) * gamma
        return out

    def _L0_xattn_ref(x_q, x_k, x_v, attn_mask, Wq, bq, Wk, bk, Wv, bv, Wo, bo, n_heads):
        import jax, jax.numpy as jnp
        import numpy as np
        B, TQ, TK, D, H = (2, 512, 512, 256, 16)
        Bv, Tq, Dm = x_q.shape
        Tk = x_k.shape[1]
        dh = Dm // n_heads
        Q = (jnp.einsum('btd,od->bto', x_q, Wq) + bq).reshape(Bv, Tq, n_heads, dh).transpose(0, 2, 1, 3)
        K = (jnp.einsum('btd,od->bto', x_k, Wk) + bk).reshape(Bv, Tk, n_heads, dh).transpose(0, 2, 1, 3)
        V = (jnp.einsum('btd,od->bto', x_v, Wv) + bv).reshape(Bv, Tk, n_heads, dh).transpose(0, 2, 1, 3)
        scale = 1.0 / np.sqrt(dh).astype(np.float32)
        scores = jnp.einsum('bhqd,bhkd->bhqk', Q, K) * scale
        scores = jnp.where(attn_mask[:, None, :, :], -jnp.inf, scores)
        A = jax.nn.softmax(scores, axis=-1)
        out = jnp.einsum('bhqk,bhkd->bhqd', A, V)
        out = out.transpose(0, 2, 1, 3).reshape(Bv, Tq, Dm)
        return jnp.einsum('btd,od->bto', out, Wo) + bo

    def _L0_ffn_ref(x, expert_sel, keys, values):
        import jax, jax.numpy as jnp
        import numpy as np
        N_HEADS = 4
        B, S, d = x.shape
        n_experts = keys.shape[0]
        xf = x.reshape(-1, d)
        N = xf.shape[0]
        logits = xf @ expert_sel.T
        sel = jax.nn.sigmoid(logits)
        sel_val, sel_idx = jax.lax.top_k(sel, N_HEADS)
        gates = jnp.zeros((N, n_experts), dtype=x.dtype)
        gates = gates.at[jnp.arange(N)[:, None], sel_idx].set(sel_val)
        h = jnp.einsum('nd,kde->nke', xf, keys)
        scores = jax.nn.relu(h) * gates[:, :, None]
        out = jnp.einsum('nke,kev->nv', scores, values)
        return out.reshape(B, S, -1)
    x = x + _L0_attn_ref(_layernorm(x, axis=-1), L0_attn_W_qkv, L0_attn_W_o1, L0_attn_W_o2, L0_attn_gamma)
    x = x + _L0_xattn_ref(_layernorm(x, axis=-1), ctx_1024, ctx_1024, mask_BxSxS2_bk1, L0_xattn_Wq, L0_xattn_bq, L0_xattn_Wk, L0_xattn_bk, L0_xattn_Wv, L0_xattn_bv, L0_xattn_Wo, L0_xattn_bo, 16)
    x = x + _L0_ffn_ref(_layernorm(x, axis=-1), L0_ffn_expert_sel, L0_ffn_keys, L0_ffn_values)
    return x

_drawn_inputs = setup_inputs


def setup_inputs(seed=0):
    import zlib

    import numpy as np

    out = dict(_drawn_inputs(seed))
    spreads = {'L0_attn_gamma': (1.0, 0.2),
     'L0_xattn_bq': (0.0, 0.1),
     'L0_xattn_bk': (0.0, 0.1),
     'L0_xattn_bv': (0.0, 0.1),
     'L0_xattn_bo': (0.0, 0.1)}
    factors = {}
    for name, (base, spread) in spreads.items():
        noise = np.random.default_rng([zlib.crc32(name.encode()), seed]).standard_normal(out[name].shape)
        drawn = base * np.exp(spread * noise) if base else spread * noise
        out[name] = jnp.asarray(drawn.astype(out[name].dtype))
    for name, factor in factors.items():
        out[name] = (out[name] * factor).astype(out[name].dtype)
    return out
```

```python
from contextlib import ExitStack

import numpy as np

import concourse.bass as bass
from concourse import mybir

F32 = mybir.dt.float32
F32R = mybir.dt.float32r
BF16 = mybir.dt.bfloat16
U32 = mybir.dt.uint32
I32 = mybir.dt.int32
U8 = mybir.dt.uint8
ALU = mybir.AluOpType
ACT = mybir.ActivationFunctionType
AX = mybir.AxisListType.X

P = 128
BATCH, SEQ, DIM = 2, 1024, 256
HEADS, DH = 16, 64
PAIRS = HEADS // 2
KT = DIM // P
TT = SEQ // P
HALF = 512
EPS = 1e-5
SK = 77
NEG = -3.0e38

DX = DIM // HEADS
CHUNK = 4
CHUNKS_X = BATCH * TT // CHUNK
TILES_IN = BATCH * TT
EXPERTS, TOPK = 64, 4
HID = 128
PLACES = BATCH * SEQ
MOE_TILES = BATCH * SEQ * TOPK // P + EXPERTS
RING = 8

UNITS = 2 * TT
LAG = 2
STEPS = UNITS + LAG
PROJ_AT = {1: 0, 3: 1, 5: 2, 9: 3, 13: 4, 17: 5}
GROUP_END = {UNITS // 2 - 1 + LAG: 0, STEPS - 1: 1}


def unit(n):
    return n // TT, n // 2, n % 2


def score_chunks(qi):
    w = (qi + 1) * P
    return [(c, max(256, min(HALF, w - c))) for c in range(0, w, HALF)]


def transpose_chunks():
    out, seen = [], {"dve": 0, "act": 0}
    for g in range(2):
        for n in range(g * TT, (g + 1) * TT):
            qi = unit(n)[1]
            for c in range(0, qi + 1, 4):
                eng = "dve" if len(out) % 2 == 0 else "act"
                seen[eng] += 1
                out.append((n, c, min(4, qi + 1 - c), eng, seen[eng]))
        seen["act"] += 1
        out.append(("sums", g, 4, "act", seen["act"]))
    return out, seen


CHUNKS, EVACS = transpose_chunks()


def build_program(nc, t):
    ctx = ExitStack()
    with ctx:
        def sem(name):
            return ctx.enter_context(nc.semaphore(name))

        def sb_in(c, name, shape, dt=F32):
            return c.enter_context(nc.sbuf_tensor(name, shape, dt))

        ps = [ctx.enter_context(nc.psum_tensor(f"bank{i}", [P, HALF], F32)) for i in range(4, 8)]
        sc = ctx.enter_context(nc.psum_tensor("scores", [P, 4, HALF], F32))
        tb, ob, pj = ps[0:2], ps[2], ps[3]

        ident = sb_in(ctx, "ident", [P, P])
        ident_b = sb_in(ctx, "ident_b", [P, P], BF16)
        causal_b = sb_in(ctx, "causal_b", [P, P], BF16)
        stats = sb_in(ctx, "stats", [P, TT, 6])
        mv = sb_in(ctx, "mv", [P, TT, 2])
        veps = sb_in(ctx, "veps", [P, TT])
        std = sb_in(ctx, "std", [P, TT])
        rstd = sb_in(ctx, "rstd", [P, TT])

        m1 = ExitStack()
        stk = sb_in(m1, "stk", [P, 2, 2, 3, SEQ], F32R)
        qk_hi = sb_in(m1, "qk_hi", [P, 2, SEQ], F32R)
        qk_lo = sb_in(m1, "qk_lo", [P, 2, SEQ], F32R)
        v = sb_in(m1, "v", [P, 2, TT, P])
        wbuf = sb_in(m1, "wbuf", [P, 2, KT, 3 * P])
        pt = sb_in(m1, "pt", [P, 2, TT, HALF])
        probs = sb_in(m1, "probs", [P, 2, SEQ])
        oT = sb_in(m1, "oT", [P, PAIRS, SEQ])
        xT = sb_in(m1, "xT", [P, KT, SEQ])
        cos_t = sb_in(m1, "cos_t", [P, SEQ])
        sin_t = sb_in(m1, "sin_t", [P, SEQ])
        t1 = sb_in(m1, "t1", [P, 2, HALF])
        t2 = sb_in(m1, "t2", [P, 2, HALF])
        rot = sb_in(m1, "rot", [P, 2, HALF])
        rs = sb_in(m1, "rs", [P, UNITS])
        rsi = sb_in(m1, "rsi", [P, TT])
        rinv = sb_in(m1, "rinv", [P, TT, DH])
        nmax = sb_in(m1, "nmax", [P, UNITS])
        inv_b = sb_in(m1, "inv_b", [P, HALF])
        xb = sb_in(m1, "xb", [P, TT, DIM])
        wo1 = sb_in(m1, "wo1", [P, PAIRS, DIM])
        wo2 = sb_in(m1, "wo2", [P, KT, DIM])
        gamma = sb_in(m1, "gamma", [P, DIM])
        m1.close()
        xn = probs[:, :, :].rearrange("p a b -> p (a b)").rearrange("p (t d) -> p t d", t=TT)
        h1T = pt[:, 0, 0:4, :].rearrange("p a b -> p (a b)").rearrange("p (m s) -> p m s", m=KT)

        ctx2 = ExitStack()
        s_const = sem("s_const")
        s_apart = sem("s_apart")
        s_x = sem("s_x")
        s_w = [sem("s_w0"), sem("s_w1")]
        s_wq = sem("s_wq")
        s_var = sem("s_var"); s_std = sem("s_std")
        s_lnv = sem("s_lnv")
        s_xn = sem("s_xn")
        s_xt = sem("s_xt")
        s_xtv = sem("s_xtv"); s_xta = sem("s_xta")
        s_pj = sem("s_pj")
        s_rope = sem("s_rope")
        s_rot = sem("s_rot")
        s_hi = sem("s_hi"); s_lo = sem("s_lo")
        s_v = sem("s_v")
        s_stk = [sem("s_stk0"), sem("s_stk1")]
        s_s = sem("s_s"); s_mx = sem("s_mx"); s_exp = sem("s_exp")
        s_t = sem("s_t")
        s_ev = {"dve": sem("s_evv"), "act": sem("s_eva")}
        s_rsi = sem("s_rsi"); s_rinv = sem("s_rinv"); s_pv = sem("s_pv"); s_ot = sem("s_ot")
        s_h1 = sem("s_h1"); s_h1a = sem("s_h1a"); s_o2 = sem("s_o2")
        s_x1 = sem("s_x1"); s_st = sem("s_st")

        x2 = sb_in(ctx2, "x2", [P, TILES_IN, DIM])
        keys = sb_in(ctx2, "keys", [P, EXPERTS, KT * HID])
        chose = sb_in(ctx2, "chose", [P, TILES_IN * TOPK, EXPERTS], BF16)
        expert = sb_in(ctx2, "expert", [P, TILES_IN * TOPK])
        rank = sb_in(ctx2, "rank", [P, TILES_IN * TOPK])
        gate = sb_in(ctx2, "gate", [P, TILES_IN * TOPK])
        macc = sb_in(ctx2, "macc", [P, EXPERTS], BF16)
        tri_b = sb_in(ctx2, "tri_b", [P, P], BF16)
        ones_b = sb_in(ctx2, "ones_b", [P, P], BF16)
        iota_e = sb_in(ctx2, "iota_e", [P, EXPERTS])
        rowidx = sb_in(ctx2, "rowidx", [P, MOE_TILES], U32)
        etile = sb_in(ctx2, "etile", [P, MOE_TILES], I32)
        yslot = sb_in(ctx2, "yslot", [P, TILES_IN * TOPK], U32)
        m2 = ExitStack()
        x1c = sb_in(m2, "x1c", [P, CHUNK, DIM])
        maskc = sb_in(m2, "maskc", [P, CHUNK, SK], U8)
        mbias = sb_in(m2, "mbias", [P, CHUNK, SK])
        xnc = sb_in(m2, "xnc", [P, CHUNK, DIM])
        xTc = sb_in(m2, "xTc", [P, KT, HALF])
        qT = sb_in(m2, "qT", [P, KT, HALF])
        sx = sb_in(m2, "sx", [P, 2, HEADS, SK])
        mx = sb_in(m2, "mx", [P, 2, HEADS])
        sums = sb_in(m2, "sums", [P, 2, HEADS])
        inv = sb_in(m2, "inv", [P, 2, HEADS])
        ptx = sb_in(m2, "ptx", [SK, HEADS, HALF])
        oTc = sb_in(m2, "oTc", [P, KT, HALF])
        wx = sb_in(m2, "wx", [P, 4, KT, DIM])
        sel_w = sb_in(m2, "sel_w", [P, KT, EXPERTS])
        bqk = sb_in(m2, "bqk", [P, 2, KT])
        bvo = sb_in(m2, "bvo", [P, 2, DIM])
        ctxT = sb_in(m2, "ctxT", [P, KT, SK])
        headm = sb_in(m2, "headm", [P, HEADS // 2])
        kT = sb_in(m2, "kT", [P, KT, SK])
        kblk = sb_in(m2, "kblk", [P, KT, HEADS // 2, SK])
        vz = sb_in(m2, "vz", [SK, HEADS, 2 * DX])
        x3 = sb_in(m2, "x3", [P, CHUNK, DIM])
        el = sb_in(m2, "el", [P, CHUNK, EXPERTS])
        sel = sb_in(m2, "sel", [P, CHUNK, EXPERTS])
        top = sb_in(m2, "top", [P, CHUNK, 8])
        topi = sb_in(m2, "topi", [P, CHUNK, 8], U32)
        mch = sb_in(m2, "mch", [P, CHUNK, EXPERTS], BF16)
        msum = sb_in(m2, "msum", [P, EXPERTS])
        prod = sb_in(m2, "prod", [P, CHUNK * TOPK, EXPERTS])
        slotf = sb_in(m2, "slotf", [P, CHUNK * TOPK])
        slots = sb_in(m2, "slots", [P, CHUNK * TOPK], U32)
        tokid = sb_in(m2, "tokid", [P, TILES_IN])
        tokens = sb_in(m2, "tokens", [P, CHUNK])
        zeros = sb_in(m2, "zeros", [P, EXPERTS * PLACES // P])
        m2.close()
        m3 = ExitStack()
        vals = sb_in(m3, "vals", [P, EXPERTS, DIM])
        prod3 = sb_in(m3, "prod3", [P, CHUNK * TOPK, EXPERTS])
        iota_t = sb_in(m3, "iota_t", [EXPERTS, MOE_TILES])
        iota_pt = sb_in(m3, "iota_pt", [P, MOE_TILES])
        iota_ee = sb_in(m3, "iota_ee", [EXPERTS, P])
        cnt = sb_in(m3, "cnt", [EXPERTS, P])
        cnti = sb_in(m3, "cnti", [EXPERTS, 2, P], I32)
        tiles_f = sb_in(m3, "tiles_f", [EXPERTS, P])
        tiles_b = sb_in(m3, "tiles_b", [EXPERTS, P], BF16)
        first = sb_in(m3, "first", [EXPERTS, P])
        first_b = sb_in(m3, "first_b", [P, EXPERTS])
        after = sb_in(m3, "after", [EXPERTS, 1])
        begun = sb_in(m3, "begun", [EXPERTS, 2, MOE_TILES])
        owner = sb_in(m3, "owner", [EXPERTS, MOE_TILES])
        blockf = sb_in(m3, "blockf", [EXPERTS, P])
        block_i = sb_in(m3, "block_i", [MOE_TILES, 1], U32)
        table_t = sb_in(m3, "table_t", [MOE_TILES, P])
        ybase = sb_in(m3, "ybase", [P, TILES_IN * TOPK])
        idxb = sb_in(m3, "idxb", [P, RING], U32)
        xin = sb_in(m3, "xin", [P, RING, DIM])
        xgT = sb_in(m3, "xgT", [P, 2, KT * P])
        ksel = sb_in(m3, "ksel", [P, 2, KT * HID])
        hT = sb_in(m3, "hT", [P, 2, P])
        ysb = sb_in(m3, "ysb", [P, 4, DIM])
        m3.close()
        ctx2.close()

        s_c2 = sem("s_c2")
        s_zr = sem("s_zr"); s_zero = sem("s_zero")
        s_keys = sem("s_keys"); s_vals = sem("s_vals")
        s_ctx = sem("s_ctx"); s_x1c = sem("s_x1c"); s_mask = sem("s_mask")
        s_cd = sem("s_cd")
        s_bd = sem("s_bd")
        s_kv = sem("s_kv"); s_kvd = sem("s_kvd")
        s_var2 = sem("s_var2"); s_std2 = sem("s_std2"); s_ln = sem("s_ln")
        s_tr2 = sem("s_tr2"); s_trv = sem("s_trv"); s_tra = sem("s_tra")
        s_q2 = sem("s_q2"); s_qd = sem("s_qd")
        s_sx = sem("s_sx"); s_sub = sem("s_sub"); s_masked = sem("s_masked")
        s_ex = sem("s_ex"); s_inv = sem("s_inv"); s_norm = sem("s_norm")
        s_px = sem("s_px"); s_pxv = sem("s_pxv"); s_pxa = sem("s_pxa")
        s_ov = sem("s_ov"); s_ovv = sem("s_ovv"); s_ova = sem("s_ova")
        s_wox = sem("s_wox"); s_lg = sem("s_lg"); s_el = sem("s_el")
        s_mch = sem("s_mch"); s_rk = sem("s_rk"); s_slot = sem("s_slot"); s_macc = sem("s_macc")
        s_x3d = sem("s_x3d")
        s_scat = sem("s_scat"); s_sent = sem("s_sent")
        s_c3 = sem("s_c3")
        s_md = sem("s_md")
        s_m = sem("s_m"); s_mv = sem("s_mv"); s_map = sem("s_map")
        s_blk = sem("s_blk"); s_tab = sem("s_tab")
        s_idx = sem("s_idx"); s_g = [sem(f"s_g{i}") for i in range(RING)]
        s_t3 = sem("s_t3"); s_xg = sem("s_xg"); s_ks = sem("s_ks")
        s_f1 = sem("s_f1"); s_h = sem("s_h"); s_f2 = sem("s_f2"); s_y = sem("s_y")
        s_ys = [sem(f"s_ys{i}") for i in range(4)]
        s_cg = [sem(f"s_cg{i}") for i in range(RING)]
        s_comb = sem("s_comb"); s_out = sem("s_out")

        block = ctx.enter_context(nc.Block())

        def apart(eng):
            eng.sem_inc(s_apart, 1)

        def pairs(eng, b, body):
            with eng.Fori(0, PAIRS // 2 - 1) as it:
                for u in range(2):
                    body(b * PAIRS + it * 2 + u, it * 2 + u, u, b * (PAIRS // 2) + it, True, True)
            for u in range(2):
                body(b * PAIRS + PAIRS - 2 + u, PAIRS - 2 + u, u, b * (PAIRS // 2) + PAIRS // 2 - 1, u == 0, False)

        def evac_chunks(eng, name, PB, what, copy):
            for idx, (m, c, tiles, who, _) in enumerate(CHUNKS):
                key = (m, c) if m == "sums" else m
                if who != name or key != what:
                    continue
                eng.wait_ge(s_t, PB * len(CHUNKS) + idx + 1)
                if m == "sums":
                    copy(inv_b[:], tb[idx % 2][:]).then_inc(s_ev[name], 1)
                    continue
                g, qi, hh = unit(m)
                if g == 1:
                    eng.wait_ge(s_pv, PB * 2 + 1)
                q0 = (qi - 4 * g) * P
                copy(pt[:, hh, c:c + tiles, q0:q0 + P],
                     tb[idx % 2][:, 0:P * tiles].rearrange("p (k q) -> p k q", k=tiles)).then_inc(s_ev[name], 1)

        @block.sync
        def _(sp):
            for dst, src in ((ident[:], t["ident"]), (ident_b[:], t["ident_b"]), (causal_b[:], t["causal_b"]),
                             (cos_t[:], t["cos"]), (sin_t[:], t["sin"]), (gamma[:], t["gamma"]),
                             (wo1[:], t["wo1"]), (wo2[:], t["wo2"])):
                sp.dma_start(dst, src).then_inc(s_const, 16)

            def load_w(pair, u):
                sp.dma_start(wbuf[:, u], t["wqkv"][bass.ds(pair, 1)].rearrange("o p k n -> p (o k) n")).then_inc(s_w[u], 16)

            def stack(PT, u):
                for which in range(2):
                    sp.wait_ge(s_lo, PT * 4 + 2 * (which + 1))
                    for hh in range(2):
                        for part in range(2):
                            rows = slice(64 * part + 32 * hh, 64 * part + 32 * hh + 32)
                            for buf, hl in ((qk_hi, 0), (qk_lo, 1)):
                                src = buf[rows, which, :].bitcast(F32)
                                if which == 0:
                                    at = 64 * hl + 32 * part
                                    sp.dma_start(stk[at:at + 32, u, hh, 0, :].bitcast(F32), src).then_inc(s_stk[u], 16)
                                else:
                                    for dup in range(2):
                                        at = 64 * dup + 32 * part
                                        sp.dma_start(stk[at:at + 32, u, hh, 1 + hl, :].bitcast(F32), src).then_inc(s_stk[u], 16)

            with sp.Fori(0, BATCH) as b:
                sp.dma_start(xb[:], t["x"][bass.ds(b, 1)].rearrange("o (t p) d -> p (o t) d", p=P)).then_inc(s_x, 16)
                load_w(0, 0)
                load_w(1, 1)
                stack(b * PAIRS, 0)

                def body(PB, pair, u, use, nxt, nxt2):
                    if nxt2:
                        sp.wait_ge(s_pj, (PB + 1) * 6)
                        load_w(pair + 2, u)
                    if nxt:
                        stack(PB + 1, 1 - u)
                pairs(sp, b, body)
                sp.wait_ge(s_x1, b + 1)
                sp.dma_start(t["x1"][bass.ds(b, 1)].rearrange("o (t p) d -> p (o t) d", p=P), xb[:]).then_inc(s_st, 16)
                sp.wait_ge(s_st, (b + 1) * 16)
                apart(sp)

            for dst, src in ((wx[:], t["wx"]), (sel_w[:], t["sel_w"]), (bqk[:], t["bqk"]), (bvo[:], t["bvo"]),
                             (headm[:], t["headm"]), (tri_b[:], t["tri_b"]), (ones_b[:], t["ones_b"]), (iota_e[:], t["iota_e"]), (tokid[:], t["tokid"])):
                sp.dma_start(dst, src).then_inc(s_c2, 16)
            sp.wait_ge(s_zr, 1)
            sp.dma_start(t["table"].rearrange("(p n) o -> p (n o)", p=P), zeros[:]).then_inc(s_zero, 16)
            with sp.Fori(0, BATCH) as b:
                with sp.Fori(0, TT // CHUNK) as c:
                    cc = b * (TT // CHUNK) + c
                    sp.wait_ge(s_slot, cc + 1)
                    sp.dma_start(x1c[:], t["x1"][bass.ds(b, 1), bass.ts(c, CHUNK * P), :]
                                 .rearrange("o (t p) d -> p (o t) d", p=P)).then_inc(s_x1c, 16)
                    sp.dma_start(maskc[:], t["mask"][bass.ds(b, 1), :, bass.ts(c, CHUNK), :]
                                 .rearrange("o p t k -> p (o t) k")).then_inc(s_mask, 16)
                    sp.dma_start(ctxT[:], t["ctxT"][bass.ds(b, 1)].rearrange("o p k s -> p (o k) s")).then_inc(s_ctx, 16)
                    sp.dma_start(keys[:, bass.ts(cc, EXPERTS // CHUNKS_X), :],
                                 t["keys"][:, bass.ts(cc, EXPERTS // CHUNKS_X), :]).then_inc(s_keys, 16)
                    sp.wait_ge(s_ln, cc * 2 + 2)
                    sp.dma_start(t["x3"][bass.ds(cc, 1)].rearrange("o (t p) d -> p (o t) d", p=P), x3[:]).then_inc(s_x3d, 16)
            sp.wait_ge(s_slot, CHUNKS_X + 1)
            sp.wait_ge(s_scat, 16 * TILES_IN * TOPK)
            sp.wait_ge(s_x3d, 16 * CHUNKS_X)
            for dst, src in ((iota_t[:], t["iota_t"]), (iota_pt[:], t["iota_pt"]), (iota_ee[:], t["iota_ee"])):
                sp.dma_start(dst, src).then_inc(s_c3, 16)
            sp.dma_start(vals[:], t["vals"]).then_inc(s_vals, 16)
            with sp.Fori(0, MOE_TILES // 4) as it:
                for i in range(4):
                    sp.wait_ge(s_y, it * 4 + (i + 3))
                    sp.dma_start(t["yg"][bass.ts(it * 4 + i, P), :], ysb[:, i, :]).then_inc(s_ys[i], 16)
            with sp.Fori(0, TILES_IN) as tt:
                sp.wait_ge(s_comb, tt * TOPK + (TOPK + RING))
                sp.dma_start(t["out"][bass.ts(tt, P), :], x2[:, bass.ds(tt, 1), :].rearrange("p o d -> p (o d)")).then_inc(s_out, 16)
            sp.wait_ge(s_out, 16 * TILES_IN)
            for i in range(4):
                sp.wait_ge(s_ys[i], 16 * (MOE_TILES // 4))
            sp.wait_ge(s_st, 16 * BATCH)

        @block.gpsimd
        def _(pool):
            def scale_wq(PT, u, use):
                pool.wait_ge(s_w[u], (use + 1) * 16)
                apart(pool)
                pool.tensor_scalar(wbuf[:, u, :, 0:P], wbuf[:, u, :, 0:P], DH ** -0.5, None, ALU.mult).then_inc(s_wq, 1)

            def rotate(PT):
                for j in range(4):
                    pool.wait_ge(s_rope, PT * 4 + j + 1)
                    if j >= 2:
                        pool.wait_ge(s_hi, PT * 4 + j - 1)
                    pool.tensor_tensor(rot[:, j % 2], t1[:, j % 2], t2[:, j % 2], ALU.add).then_inc(s_rot, 1)
                    pool.wait_ge(s_rot, PT * 4 + j + 1)
                    pool.wait_ge(s_hi, PT * 4 + j + 1)
                    dst = slice(HALF * (j % 2), HALF * (j % 2 + 1))
                    pool.tensor_tensor(qk_lo[:, j // 2, dst], rot[:, j % 2], qk_hi[:, j // 2, dst].bitcast(F32),
                                       ALU.subtract).then_inc(s_lo, 1)

            with pool.Fori(0, BATCH) as b:
                for u in range(2):
                    scale_wq(b * PAIRS + u, u, b * (PAIRS // 2))
                rotate(b * PAIRS)

                def body(PB, pair, u, use, nxt, nxt2):
                    if nxt:
                        rotate(PB + 1)
                    if nxt2:
                        scale_wq(PB + 2, u, use + 1)
                pairs(pool, b, body)

            pool.wait_ge(s_st, 16 * BATCH)
            pool.memset(zeros[:], 0.0).then_inc(s_zr, 1)
            pool.sem_inc(s_sent, 1)
            pool.wait_ge(s_zero, 16)
            with pool.Fori(0, CHUNKS_X) as cc:
                for i in range(CHUNK):
                    pool.wait_ge(s_inv, cc * CHUNK + i + 1)
                    pool.tensor_tensor(sx[:, i % 2], sx[:, i % 2],
                                       inv[:, i % 2, :].unsqueeze(2).to_broadcast([P, HEADS, SK]), ALU.mult).then_inc(s_norm, 1)
                pool.wait_ge(s_slot, cc + 2)
                apart(pool)
                for i in range(CHUNK * TOPK):
                    pool.indirect_dma_start(t["table"], bass.IndirectOffsetOnAxis(ap=slots[:, i:i + 1], axis=0),
                                            tokens[:, i // TOPK:i // TOPK + 1], None).then_inc(s_scat, 16)
                pool.wait_ge(s_scat, cc * (16 * CHUNK * TOPK) + 16 * CHUNK * TOPK)
                pool.wait_ge(s_x3d, cc * 16 + 16)
                pool.sem_inc(s_sent, 1)
            pool.wait_ge(s_scat, 16 * TILES_IN * TOPK)
            pool.wait_ge(s_x3d, 16 * CHUNKS_X)
            pool.wait_ge(s_blk, 1)
            pool.indirect_dma_start(table_t[:], None, t["table"].rearrange("(n p) o -> n (p o)", p=P),
                                    bass.IndirectOffsetOnAxis(ap=block_i[:], axis=0)).then_inc(s_tab, 16)
            pool.wait_ge(s_map, 1)
            with pool.Fori(0, MOE_TILES // RING) as it:
                pool.tensor_copy(idxb[:], rowidx[:, bass.ts(it, RING)]).then_inc(s_idx, 1)
                pool.wait_ge(s_idx, it + 1)
                for i in range(RING):
                    pool.wait_ge(s_t3, it * RING + i + 1)
                    apart(pool)
                    pool.indirect_dma_start(xin[:, i, :], None, t["x3"].rearrange("c n d -> (c n) d"), bass.IndirectOffsetOnAxis(ap=idxb[:, i:i + 1], axis=0)).then_inc(s_g[i], 16)
                for i in range(RING):
                    pool.wait_ge(s_g[i], it * 16 + 16)
            for i in range(4):
                pool.wait_ge(s_ys[i], 16 * (MOE_TILES // 4))
            with pool.Fori(0, TILES_IN * TOPK // RING) as it:
                pool.tensor_copy(idxb[:], yslot[:, bass.ts(it, RING)]).then_inc(s_idx, 1)
                pool.wait_ge(s_idx, it + MOE_TILES // RING + 1)
                for i in range(RING):
                    pool.wait_ge(s_comb, it * RING + i + 1)
                    apart(pool)
                    pool.indirect_dma_start(xin[:, i, :], None, t["yg"], bass.IndirectOffsetOnAxis(ap=idxb[:, i:i + 1], axis=0)).then_inc(s_cg[i], 16)
                for i in range(RING):
                    pool.wait_ge(s_cg[i], it * 16 + 16)

        @block.tensor
        def _(pe):
            def proj(PT, u, j, first=False):
                if j == 0:
                    pe.wait_ge(s_wq, PT + 1)
                    if not first:
                        pe.wait_ge(s_v, PT * 2)
                elif j < 5:
                    pe.wait_ge(s_rope, PT * 4 + j)
                else:
                    pe.wait_ge(s_v, PT * 2 + 1)
                if j < 4:
                    for k in range(KT):
                        last = pe.matmul(pj[:], wbuf[:, u, k, (j // 2) * P:(j // 2 + 1) * P],
                                         xT[:, k, HALF * (j % 2):HALF * (j % 2 + 1)], start=k == 0, stop=k == KT - 1)
                else:
                    for i in range(4):
                        tt = 4 * (j - 4) + i
                        for k in range(KT):
                            last = pe.matmul(pj[:, P * i:P * (i + 1)], xT[:, k, P * tt:P * (tt + 1)],
                                             wbuf[:, u, k, 2 * P:3 * P], start=k == 0, stop=k == KT - 1)
                last.then_inc(s_pj, 1)

            def scores(PB, u, n):
                _, qi, hh = unit(n)
                if n >= 2:
                    pe.wait_ge(s_exp, PB * UNITS + n - 1)
                q = stk[:, u, hh, 0, qi * P:(qi + 1) * P]
                for c, w in score_chunks(qi):
                    out = sc[:, 2 * (n % 2) + c // HALF, 0:w]
                    diag = c <= qi * P < c + HALF
                    pe.matmul(out, q, stk[:, u, hh, 1, c:c + w], start=True, stop=False)
                    last = pe.matmul(out, q, stk[:, u, hh, 2, c:c + w], start=False, stop=not diag)
                    if diag:
                        o = qi * P - c
                        last = pe.matmul(sc[:, 2 * (n % 2) + c // HALF, o:o + P], ident_b[:], causal_b[:],
                                         start=False, stop=True)
                last.then_inc(s_s, 1)

            def reuse(PB, idx):
                if idx >= 2:
                    eng, count = CHUNKS[idx - 2][3:]
                    pe.wait_ge(s_ev[eng], PB * EVACS[eng] + count)

            def transposes(PB, n):
                pe.wait_ge(s_exp, PB * UNITS + n + 1)
                for idx, (m, c, tiles, _, _) in enumerate(CHUNKS):
                    if m == n:
                        reuse(PB, idx)
                        for i in range(tiles):
                            last = pe.transpose(tb[idx % 2][:, P * i:P * (i + 1)],
                                                probs[:, n % 2, (c + i) * P:(c + i + 1) * P], ident[:])
                        last.then_inc(s_t, 1)

            def finish_group(PB, u, g):
                idx = next(i for i, ch in enumerate(CHUNKS) if ch[0] == "sums" and ch[1] == g)
                reuse(PB, idx)
                pe.wait_ge(s_rinv, PB * 2 + g + 1)
                for i in range(4):
                    last = pe.transpose(tb[idx % 2][:, P * i:P * (i + 1)],
                                        rinv[:, 2 * i:2 * i + 2, :].rearrange("p h d -> p (h d)"), ident[:])
                last.then_inc(s_t, 1)
                for eng in ("dve", "act"):
                    pe.wait_ge(s_ev[eng], PB * EVACS[eng] + max(c[4] for c in CHUNKS[:idx] if c[3] == eng))
                pe.wait_ge(s_v, (PB + 1) * 2)
                tiles = 4 * (g + 1)
                for kt in range(tiles):
                    q0 = max(0, kt - 4 * g) * P
                    for hh in range(2):
                        last = pe.matmul(ob[DH * hh:DH * (hh + 1), q0:HALF], v[:, u, kt, DH * hh:DH * (hh + 1)],
                                         pt[:, hh, kt, q0:HALF], start=kt == 0, stop=kt == tiles - 1)
                last.then_inc(s_pv, 1)

            pe.wait_ge(s_const, 16 * 8)
            with pe.Fori(0, BATCH) as b:
                pe.wait_ge(s_xn, b + 1)
                for c in range(4):
                    k, half = c // 2, c % 2
                    for i in range(4):
                        last = pe.transpose(sc[:, c, P * i:P * (i + 1)], xn[:, 4 * half + i, P * k:P * (k + 1)], ident[:])
                    last.then_inc(s_xt, 1)
                pe.wait_ge(s_xtv, (b + 1) * 2)
                pe.wait_ge(s_xta, (b + 1) * 2)
                for j in range(6):
                    proj(b * PAIRS, 0, j, first=True)

                def body(PB, pair, u, use, nxt, nxt2):
                    pe.wait_ge(s_stk[u], (use + 1) * (24 * 16))
                    for k in range(STEPS):
                        if k < UNITS:
                            scores(PB, u, k)
                        late = k in GROUP_END
                        if late:
                            transposes(PB, k - LAG)
                        if nxt and k in PROJ_AT:
                            proj(PB + 1, 1 - u, PROJ_AT[k])
                        if k >= LAG and not late:
                            transposes(PB, k - LAG)
                        if late:
                            finish_group(PB, u, GROUP_END[k])
                pairs(pe, b, body)
                pe.wait_ge(s_ot, (b + 1) * (2 * PAIRS))
                for m in range(KT):
                    for c in range(2):
                        for k in range(PAIRS):
                            last = pe.matmul(sc[:, 2 * m + c, :], wo1[:, k, P * m:P * (m + 1)],
                                             oT[:, k, HALF * c:HALF * (c + 1)], start=k == 0, stop=k == PAIRS - 1)
                        last.then_inc(s_h1, 1)
                pe.wait_ge(s_h1a, (b + 1) * 4)
                for i in range(TT):
                    for k in range(KT):
                        last = pe.matmul(ps[i // 2][:, DIM * (i % 2):DIM * (i % 2 + 1)], h1T[:, k, P * i:P * (i + 1)],
                                         wo2[:, k, :], start=k == 0, stop=k == KT - 1)
                    last.then_inc(s_o2, 1)

            pe.wait_ge(s_c2, 16 * 9)

            def transpose_chunk(cc, k, src):
                pe.wait_ge(s_ln, cc * 2 + k)
                for kt in range(KT):
                    for i in range(CHUNK):
                        last = pe.transpose(tb[kt][:, P * i:P * (i + 1)], src[:, i, P * kt:P * (kt + 1)], ident[:])
                    last.then_inc(s_tr2, 1)
                pe.wait_ge(s_trv, cc * 2 + k)
                pe.wait_ge(s_tra, cc * 2 + k)

            with pe.Fori(0, CHUNKS_X) as cc:
                pe.wait_ge(s_slot, cc + 1)
                pe.wait_ge(s_ctx, cc * 16 + 16)
                for m in range(KT):
                    for k in range(KT):
                        last = pe.matmul(tb[m][:, 0:SK], wx[:, 1, k, P * m:P * (m + 1)], ctxT[:, k, :], start=k == 0, stop=k == KT - 1)
                for k in range(KT):
                    last = pe.matmul(ob[0:SK, 0:DIM], ctxT[:, k, :], wx[:, 2, k, :], start=k == 0, stop=k == KT - 1)
                last.then_inc(s_kv, 1)
                pe.wait_ge(s_kvd, cc + 1)
                transpose_chunk(cc, 1, xnc)
                for m in range(KT):
                    for k in range(KT):
                        last = pe.matmul(ps[2 + m][:], wx[:, 0, k, P * m:P * (m + 1)], xTc[:, k, :], start=k == 0, stop=k == KT - 1)
                    last.then_inc(s_q2, 1)
                pe.wait_ge(s_qd, cc * 2 + 2)

                def probs_T(i):
                    pe.wait_ge(s_norm, cc * CHUNK + i + 1)
                    for j in range(4):
                        n = 4 * i + j
                        if n >= 2:
                            pe.wait_ge(s_pxv if n % 2 == 0 else s_pxa, cc * (2 * CHUNK) + n // 2)
                        for h in range(4):
                            last = pe.transpose(tb[j % 2][0:SK, P * h:P * (h + 1)], sx[:, i % 2, 4 * j + h, :], ident[:])
                        last.then_inc(s_px, 1)

                for i in range(CHUNK + 1):
                    if i < CHUNK:
                        if i >= 1:
                            pe.wait_ge(s_masked, cc * CHUNK + i)
                        for j in range(4):
                            last = pe.matmul(sc[:, j, 0:4 * SK], qT[:, j // 2, P * i:P * (i + 1)],
                                             kblk[:, j // 2, 4 * (j % 2):4 * (j % 2) + 4, :].rearrange("p h s -> p (h s)"),
                                             start=True, stop=True)
                        last.then_inc(s_sx, 1)
                    if i >= 1:
                        probs_T(i - 1)
                pe.wait_ge(s_pxv, cc * (2 * CHUNK) + 2 * CHUNK)
                pe.wait_ge(s_pxa, cc * (2 * CHUNK) + 2 * CHUNK)
                for m in range(KT):
                    for odd in range(2):
                        for g in range(4):
                            h = 8 * m + 2 * g + odd
                            last = pe.matmul(ps[2 + m][32 * g:32 * (g + 1), :], vz[:, h, :], ptx[:, h, :],
                                             start=odd == 0, stop=odd == 1)
                    last.then_inc(s_ov, 1)
                pe.wait_ge(s_ovv, cc + 1)
                pe.wait_ge(s_ova, cc + 1)
                for i in range(CHUNK):
                    for k in range(KT):
                        last = pe.matmul(tb[i // 2][:, DIM * (i % 2):DIM * (i % 2 + 1)], oTc[:, k, P * i:P * (i + 1)],
                                         wx[:, 3, k, :], start=k == 0, stop=k == KT - 1)
                last.then_inc(s_wox, 1)
                transpose_chunk(cc, 2, x3)
                for i in range(CHUNK):
                    for k in range(KT):
                        last = pe.matmul(ob[:, EXPERTS * i:EXPERTS * (i + 1)], xTc[:, k, P * i:P * (i + 1)], sel_w[:, k, :],
                                         start=k == 0, stop=k == KT - 1)
                last.then_inc(s_lg, 1)
                pe.wait_ge(s_mch, cc + 1)
                for i in range(CHUNK):
                    out = pj[:, EXPERTS * i:EXPERTS * (i + 1)]
                    pe.matmul(out, tri_b[:], mch[:, i, :], start=True, stop=False)
                    for j in range(i):
                        pe.matmul(out, ones_b[:], mch[:, j, :], start=False, stop=False)
                    last = pe.matmul(out, ones_b[:], macc[:], start=False, stop=True)
                last.then_inc(s_rk, 1)

            pe.wait_ge(s_slot, CHUNKS_X + 1)
            pe.matmul(tb[0][0:EXPERTS, 0:P], macc[:], ones_b[:], start=True, stop=True).then_inc(s_m, 1)
            pe.wait_ge(s_mv, 1)
            pe.matmul(tb[1][0:EXPERTS, 0:P], tri_b[0:EXPERTS, 0:EXPERTS], tiles_b[:], start=True, stop=True)
            pe.matmul(ob[:, 0:EXPERTS], tiles_b[:], tri_b[0:EXPERTS, 0:EXPERTS], start=True, stop=True).then_inc(s_m, 1)
            pe.wait_ge(s_mv, 2)
            pe.matmul(sc[:, 0, 0:P], owner[:], blockf[:], start=True, stop=True)
            pe.matmul(sc[:, 1, 0:MOE_TILES], iota_ee[:], owner[:], start=True, stop=True).then_inc(s_m, 1)
            pe.wait_ge(s_tab, 16)
            pe.transpose(sc[:, 2, 0:MOE_TILES], table_t[:], ident[:]).then_inc(s_m, 1)

            pe.sem_inc(s_t3, RING)
            pe.sem_inc(s_f1, 2)
            pe.sem_inc(s_f2, 2)
            pe.wait_ge(s_map, 1)
            pe.wait_ge(s_vals, 16)

            def tile_T(n, s, use):
                pe.wait_ge(s_g[s % RING], use * 16 + 16)
                pe.wait_ge(s_xg, n + 1)
                for k in range(KT):
                    last = pe.transpose(tb[s % 2][:, P * k:P * (k + 1)], xin[:, s % RING, P * k:P * (k + 1)], ident[:])
                last.then_inc(s_t3, 1)

            def tile_keys(n, s):
                pe.wait_ge(s_xg, n + 3)
                pe.wait_ge(s_ks, n + 3)
                pe.wait_ge(s_h, n + 1)
                for k in range(KT):
                    last = pe.matmul(sc[:, s % 2, 0:P], ksel[:, s % 2, HID * k:HID * (k + 1)], xgT[:, s % 2, P * k:P * (k + 1)],
                                     start=k == 0, stop=k == KT - 1)
                last.then_inc(s_f1, 1)

            def tile_values(n, s):
                e = pe.value_load(etile[0:1, bass.ds(n, 1)], min_val=0, max_val=EXPERTS - 1)
                pe.wait_ge(s_h, n + 3)
                pe.wait_ge(s_y, n + 1)
                pe.matmul(sc[:, 2 + s % 2, 0:DIM], hT[:, s % 2, :], vals[:, bass.ds(e, 1), :].rearrange("p o d -> p (o d)"),
                          start=True, stop=True).then_inc(s_f2, 1)

            tile_T(0, 0, 0)
            tile_T(1, 1, 0)
            tile_keys(0, 0)
            with pe.Fori(0, MOE_TILES // RING - 1) as it:
                for i in range(RING):
                    s = i + 2
                    n = it * RING + s
                    tile_T(n, s, it + s // RING)
                    tile_keys(n - 1, s - 1)
                    tile_values(n - 2, s - 2)
            for n in range(MOE_TILES - RING + 2, MOE_TILES + 2):
                if n < MOE_TILES:
                    tile_T(n, n, n // RING)
                if n - 1 < MOE_TILES:
                    tile_keys(n - 1, n - 1)
                tile_values(n - 2, n - 2)

        @block.scalar
        def _(act):
            def exps(PB, n):
                _, qi, _ = unit(n)
                act.wait_ge(s_mx, PB * UNITS + n + 1)
                if n >= 2:
                    done = sum(1 for c in CHUNKS if c[0] != "sums" and c[0] <= n - 2 or c[0] == "sums" and n - 2 >= TT * (c[1] + 1))
                    act.wait_ge(s_t, PB * len(CHUNKS) + done)
                w = (qi + 1) * P
                src = sc[:, 2 * (n % 2):2 * (n % 2) + 2, :].rearrange("p a b -> p (a b)")[:, 0:w]
                act.activation(probs[:, n % 2, 0:w], src, ACT.Exp, bias=nmax[:, n:n + 1],
                               accum_out=rs[:, n:n + 1]).then_inc(s_exp, 1)

            def evac(PB, what):
                evac_chunks(act, "act", PB, what, lambda o, i: act.activation(o, i, ACT.Copy))

            def hi(PT, j):
                act.wait_ge(s_rot, PT * 4 + j + 1)
                act.activation(qk_hi[:, j // 2, HALF * (j % 2):HALF * (j % 2 + 1)], rot[:, j % 2], ACT.Copy).then_inc(s_hi, 1)

            def v_out(PT, u, j):
                act.wait_ge(s_pj, PT * 6 + j + 1)
                act.activation(v[:, u, 4 * (j - 4):4 * (j - 3), :], pj[:].rearrange("p (t d) -> p t d", t=4), ACT.Copy).then_inc(s_v, 1)

            with act.Fori(0, BATCH) as b:
                act.wait_ge(s_var, b * 2 + 1)
                act.activation(std[:], veps[:], ACT.Sqrt).then_inc(s_std, 1)
                for c in (2, 3):
                    act.wait_ge(s_xt, b * 4 + c + 1)
                    act.activation(xT[:, 1, HALF * (c % 2):HALF * (c % 2 + 1)], sc[:, c, :], ACT.Copy).then_inc(s_xta, 1)
                for j in range(4):
                    hi(b * PAIRS, j)
                for j in (4, 5):
                    v_out(b * PAIRS, 0, j)

                def body(PB, pair, u, use, nxt, nxt2):
                    for k in range(STEPS):
                        if k < UNITS:
                            exps(PB, k)
                        if nxt and PROJ_AT.get(k - 1, 9) < 4:
                            hi(PB + 1, PROJ_AT[k - 1])
                        if k >= LAG:
                            evac(PB, k - LAG)
                        if nxt and PROJ_AT.get(k, 0) >= 4:
                            v_out(PB + 1, 1 - u, PROJ_AT[k])
                        if k in GROUP_END:
                            evac(PB, ("sums", GROUP_END[k]))
                pairs(act, b, body)
                for m in range(KT):
                    for c in range(2):
                        act.wait_ge(s_h1, b * 4 + 2 * m + c + 1)
                        act.activation(h1T[:, m, HALF * c:HALF * (c + 1)], sc[:, 2 * m + c, :], ACT.Relu).then_inc(s_h1a, 1)
                act.wait_ge(s_var, b * 2 + 2)
                act.activation(std[:], veps[:], ACT.Sqrt).then_inc(s_std, 1)

            def ln_and_transposes(cc, k):
                act.wait_ge(s_var2, cc * 2 + k)
                act.activation(std[:, 0:CHUNK], veps[:, 0:CHUNK], ACT.Sqrt).then_inc(s_std2, 1)
                act.wait_ge(s_tr2, cc * 4 + 2 * k)
                act.activation(xTc[:, 1, :], tb[1][:], ACT.Copy).then_inc(s_tra, 1)

            with act.Fori(0, CHUNKS_X) as cc:
                ln_and_transposes(cc, 1)
                for i in range(CHUNK):
                    act.wait_ge(s_sub, cc * CHUNK + i + 1)
                    act.activation(sx[:, i % 2], sx[:, i % 2], ACT.Exp).then_inc(s_ex, 1)
                    for j in (1, 3):
                        act.wait_ge(s_px, cc * (4 * CHUNK) + 4 * i + j + 1)
                        act.activation(ptx[:, 4 * j:4 * j + 4, P * i:P * (i + 1)],
                                       tb[1][0:SK, :].rearrange("s (h q) -> s h q", h=4), ACT.Copy).then_inc(s_pxa, 1)
                act.wait_ge(s_ov, cc * 2 + 2)
                act.activation(oTc[:, 1, :], ps[3][:], ACT.Copy).then_inc(s_ova, 1)
                ln_and_transposes(cc, 2)
                act.wait_ge(s_lg, cc + 1)
                act.activation(el[:], ob[:, 0:CHUNK * EXPERTS].rearrange("p (t e) -> p t e", t=CHUNK), ACT.Exp, scale=-1.0).then_inc(s_el, 1)

            act.sem_inc(s_xg, 2)
            act.sem_inc(s_ks, 2)
            act.wait_ge(s_map, 1)
            act.wait_ge(s_keys, 16 * CHUNKS_X)
            with act.Fori(0, MOE_TILES // 2) as it:
                for i in range(2):
                    n = it * 2 + i
                    e = act.value_load(etile[0:1, bass.ds(n, 1)], min_val=0, max_val=EXPERTS - 1)
                    act.wait_ge(s_f1, n + 1)
                    act.activation(ksel[:, i, :], keys[:, bass.ds(e, 1), :].rearrange("p o d -> p (o d)"), ACT.Copy).then_inc(s_ks, 1)
                    act.wait_ge(s_t3, n + RING + 1)
                    act.activation(xgT[:, i, :], tb[i][:, 0:KT * P], ACT.Copy).then_inc(s_xg, 1)

        @block.vector
        def _(dve):
            LN_STEPS = 30
            chain = [0]

            def link(ins, b):
                chain[0] += 1
                ins.then_inc(s_lnv, 1)
                dve.wait_ge(s_lnv, b * chain[1] + chain[0])
                apart(dve)

            def ln_stats(b, src, k):
                for i in range(TT):
                    last = dve.bn_stats(stats[:, i, :], src(i))
                link(last, b)
                for i in range(TT):
                    last = dve.bn_aggr(mv[:, i, :], stats[:, i, :])
                link(last, b)
                dve.tensor_scalar(veps[:], mv[:, :, 1], EPS, None, ALU.add).then_inc(s_var, 1)
                dve.wait_ge(s_std, b * 2 + k)
                link(dve.reciprocal(rstd[:], std[:]), b)

            def rope(PT, j):
                dve.wait_ge(s_pj, PT * 6 + j + 1)
                if j >= 2:
                    dve.wait_ge(s_rot, PT * 4 + j - 1)
                cols = slice(HALF * (j % 2), HALF * (j % 2 + 1))
                dve.tensor_tensor(t1[:, j % 2], pj[:], cos_t[:, cols], ALU.mult)
                dve.tensor_tensor(t2[0:64, j % 2], pj[64:128, :], sin_t[64:128, cols], ALU.mult)
                dve.tensor_tensor(t2[64:128, j % 2], pj[0:64, :], sin_t[0:64, cols], ALU.mult).then_inc(s_rope, 1)

            def row_max(PB, n):
                _, qi, _ = unit(n)
                w = (qi + 1) * P
                dve.wait_ge(s_s, PB * UNITS + n + 1)
                src = sc[:, 2 * (n % 2):2 * (n % 2) + 2, :].rearrange("p a b -> p (a b)")[:, 0:w]
                dve.tensor_reduce(nmax[:, n:n + 1], src, axis=AX, op=ALU.max, negate=True).then_inc(s_mx, 1)

            def inverse_sums(PB, g):
                dve.wait_ge(s_exp, PB * UNITS + TT * (g + 1))
                dve.reciprocal(rsi[:], rs[:, TT * g:TT * (g + 1)]).then_inc(s_rsi, 1)
                dve.wait_ge(s_rsi, PB * 2 + g + 1)
                dve.tensor_copy(rinv[:], rsi[:, :].unsqueeze(2).to_broadcast([P, TT, DH])).then_inc(s_rinv, 1)

            def out_T(PB, pair, g):
                dve.wait_ge(s_pv, PB * 2 + g + 1)
                count = next(c[4] for c in CHUNKS if c[0] == "sums" and c[1] == g)
                dve.wait_ge(s_ev["act"], PB * EVACS["act"] + count)
                dst = oT[:, bass.ds(pair, 1), HALF * g:HALF * (g + 1)].rearrange("p o s -> p (o s)")
                dve.tensor_tensor(dst, ob[:], inv_b[:], ALU.mult).then_inc(s_ot, 1)

            chain.append(0)
            chain[1] = CHAIN_PER_BATCH
            dve.wait_ge(s_const, 16 * 8)
            with dve.Fori(0, BATCH) as b:
                dve.wait_ge(s_x, (b + 1) * 16)
                apart(dve)
                ln_stats(b, lambda i: xb[:, i, :], 1)
                for i in range(TT):
                    last = dve.tensor_scalar(xn[:, i, :], xb[:, i, :], mv[:, i, 0:1], rstd[:, i:i + 1], ALU.subtract, ALU.mult)
                last.then_inc(s_xn, 1)
                for c in (0, 1):
                    dve.wait_ge(s_xt, b * 4 + c + 1)
                    dve.tensor_copy(xT[:, 0, HALF * c:HALF * (c + 1)], sc[:, c, :]).then_inc(s_xtv, 1)
                for j in range(4):
                    rope(b * PAIRS, j)

                def body(PB, pair, u, use, nxt, nxt2):
                    for k in range(STEPS):
                        if k < UNITS:
                            row_max(PB, k)
                        late = k in GROUP_END
                        if late:
                            inverse_sums(PB, GROUP_END[k])
                            evac_chunks(dve, "dve", PB, k - LAG, dve.tensor_copy)
                        if nxt and PROJ_AT.get(k, 9) < 4:
                            rope(PB + 1, PROJ_AT[k])
                        if k >= LAG and not late:
                            evac_chunks(dve, "dve", PB, k - LAG, dve.tensor_copy)
                        if k == 11:
                            out_T(PB, pair, 0)
                    out_T(PB, pair, 1)
                pairs(dve, b, body)
                dve.wait_ge(s_o2, (b + 1) * TT)
                apart(dve)
                o2 = lambda i: ps[i // 2][:, DIM * (i % 2):DIM * (i % 2 + 1)]
                ln_stats(b, o2, 2)
                for i in range(TT):
                    last = dve.tensor_scalar(xn[:, i, :], o2(i), mv[:, i, 0:1], rstd[:, i:i + 1], ALU.subtract, ALU.mult)
                link(last, b)
                link(dve.tensor_tensor(xn, xn, gamma[:, :].unsqueeze(1).to_broadcast([P, TT, DIM]), ALU.mult), b)
                dve.tensor_tensor(xb[:], xb[:], xn, ALU.add).then_inc(s_x1, 1)
                assert chain[0] == CHAIN_PER_BATCH, chain

            steps = [0]

            def then(ins, cc):
                steps[0] += 1
                ins.then_inc(s_cd, 1)
                dve.wait_ge(s_cd, cc * CHAIN_PER_CHUNK + steps[0])
                apart(dve)

            def layer_norm(cc, k, src, dst):
                for i in range(CHUNK):
                    last = dve.bn_stats(stats[:, i, :], src(i))
                then(last, cc)
                for i in range(CHUNK):
                    last = dve.bn_aggr(mv[:, i, :], stats[:, i, :])
                then(last, cc)
                dve.tensor_scalar(veps[:, 0:CHUNK], mv[:, 0:CHUNK, 1], EPS, None, ALU.add).then_inc(s_var2, 1)
                dve.wait_ge(s_std2, cc * 2 + k)
                then(dve.reciprocal(rstd[:, 0:CHUNK], std[:, 0:CHUNK]), cc)
                for i in range(CHUNK):
                    last = dve.tensor_scalar(dst[:, i, :], src(i), mv[:, i, 0:1], rstd[:, i:i + 1], ALU.subtract, ALU.mult)
                last.then_inc(s_ln, 1)
                dve.wait_ge(s_tr2, cc * 4 + 2 * k - 1)
                dve.tensor_copy(xTc[:, 0, :], tb[0][:]).then_inc(s_trv, 1)

            dve.wait_ge(s_c2, 16 * 9)
            dve.memset(vz[:], 0.0)
            dve.memset(macc[:], 0.0).then_inc(s_slot, 1)
            with dve.Fori(0, CHUNKS_X) as cc:
                steps[0] = 0
                dve.wait_ge(s_kv, cc + 1)
                for m in range(KT):
                    last = dve.tensor_scalar(kT[:, m, :], tb[m][:, 0:SK], bqk[:, 1, m:m + 1], None, ALU.add)
                then(last, cc)
                for m in range(KT):
                    dve.tensor_tensor(kblk[:, m], kT[:, m, :].unsqueeze(1).to_broadcast([P, HEADS // 2, SK]),
                                      headm[:, :].unsqueeze(2).to_broadcast([P, HEADS // 2, SK]), ALU.mult)
                for odd in range(2):
                    last = dve.tensor_tensor(vz[:].rearrange("s (g o) d -> s g o d", o=2)[:, :, odd, DX * odd:DX * (odd + 1)],
                                             ob[0:SK, 0:DIM].rearrange("s (g o d) -> s g o d", o=2, d=DX)[:, :, odd, :],
                                             bvo[0:SK, 0, :].rearrange("s (g o d) -> s g o d", o=2, d=DX)[:, :, odd, :], ALU.add)
                last.then_inc(s_kvd, 1)
                dve.wait_ge(s_x1c, cc * 16 + 16)
                apart(dve)
                layer_norm(cc, 1, lambda i: x1c[:, i, :], xnc)
                dve.wait_ge(s_mask, cc * 16 + 16)
                dve.tensor_scalar(mbias[:], maskc[:], NEG, None, ALU.mult)
                then(dve.tensor_tensor(x1c[:], x1c[:], bvo[:, 1, :].unsqueeze(1).to_broadcast([P, CHUNK, DIM]), ALU.add), cc)
                for m in range(KT):
                    dve.wait_ge(s_q2, cc * 2 + m + 1)
                    dve.tensor_scalar(qT[:, m, :], ps[2 + m][:], bqk[:, 0, m:m + 1], DX ** -0.5, ALU.add, ALU.mult).then_inc(s_qd, 1)

                def scores_in(i):
                    s = sx[:, i % 2]
                    dve.wait_ge(s_sx, cc * CHUNK + i + 1)
                    if i >= 2:
                        dve.wait_ge(s_px, cc * (4 * CHUNK) + 4 * (i - 1))
                    dve.tensor_tensor(s.rearrange("p (j h) k -> p j h k", j=4),
                                      sc[:, :, 0:4 * SK].rearrange("p j (h k) -> p j h k", h=4),
                                      mbias[:, i, :].unsqueeze(1).unsqueeze(1).to_broadcast([P, 4, 4, SK]), ALU.add).then_inc(s_masked, 1)
                    dve.wait_ge(s_masked, cc * CHUNK + i + 1)
                    then(dve.tensor_reduce(mx[:, i % 2, :], s, axis=AX, op=ALU.max), cc)
                    dve.tensor_tensor(s, s, mx[:, i % 2, :].unsqueeze(2).to_broadcast([P, HEADS, SK]), ALU.subtract).then_inc(s_sub, 1)

                def probs_sum(i):
                    dve.wait_ge(s_ex, cc * CHUNK + i + 1)
                    then(dve.tensor_reduce(sums[:, i % 2, :], sx[:, i % 2], axis=AX, op=ALU.add), cc)
                    dve.reciprocal(inv[:, i % 2, :], sums[:, i % 2, :]).then_inc(s_inv, 1)

                def probs_out(i):
                    for j in (0, 2):
                        dve.wait_ge(s_px, cc * (4 * CHUNK) + 4 * i + j + 1)
                        dve.tensor_copy(ptx[:, 4 * j:4 * j + 4, P * i:P * (i + 1)],
                                        tb[0][0:SK, :].rearrange("s (h q) -> s h q", h=4)).then_inc(s_pxv, 1)

                for i in range(CHUNK):
                    scores_in(i)
                    if i >= 1:
                        probs_out(i - 1)
                    probs_sum(i)
                probs_out(CHUNK - 1)
                dve.wait_ge(s_ov, cc * 2 + 1)
                dve.tensor_copy(oTc[:, 0, :], ps[2][:]).then_inc(s_ovv, 1)
                dve.wait_ge(s_wox, cc + 1)
                for i in range(2):
                    last = dve.tensor_tensor(x2[:, bass.ds(cc * CHUNK + 2 * i, 2), :], tb[i][:].rearrange("p (t d) -> p t d", t=2),
                                             x1c[:, 2 * i:2 * i + 2, :], ALU.add)
                then(last, cc)
                dve.wait_ge(s_sent, cc + 1)
                apart(dve)
                layer_norm(cc, 2, lambda i: x2[:, bass.ds(cc * CHUNK + i, 1), :].rearrange("p o d -> p (o d)"), x3)
                dve.wait_ge(s_el, cc + 1)
                then(dve.tensor_scalar(el[:], el[:], 1.0, None, ALU.add), cc)
                then(dve.reciprocal(sel[:], el[:]), cc)
                for i in range(CHUNK):
                    last = dve.max(top[:, i, :], sel[:, i, :])
                then(last, cc)
                for i in range(CHUNK):
                    last = dve.max_index(topi[:, i, :], top[:, i, :], sel[:, i, :])
                then(last, cc)
                cols = bass.ds(cc * (CHUNK * TOPK), CHUNK * TOPK)
                dve.tensor_copy(gate[:, cols].rearrange("p (t j) -> p t j", t=CHUNK), top[:, :, 0:TOPK])
                then(dve.tensor_copy(expert[:, cols].rearrange("p (t j) -> p t j", t=CHUNK), topi[:, :, 0:TOPK]), cc)
                then(dve.tensor_tensor(chose[:, cols, :], iota_e[:, :].unsqueeze(1).to_broadcast([P, CHUNK * TOPK, EXPERTS]),
                                       expert[:, cols].unsqueeze(2).to_broadcast([P, CHUNK * TOPK, EXPERTS]), ALU.is_equal), cc)
                with nc.allow_low_precision(reason="sums of zeros and ones, exact in bfloat16"):
                    dve.tensor_reduce(mch[:], chose[:, cols, :].rearrange("p (t j) e -> p t e j", t=CHUNK), axis=AX, op=ALU.add).then_inc(s_mch, 1)
                dve.wait_ge(s_rk, cc + 1)
                for i in range(CHUNK):
                    last = dve.tensor_tensor(prod[:, TOPK * i:TOPK * (i + 1), :], chose[:, bass.ds(cc * (CHUNK * TOPK) + TOPK * i, TOPK), :],
                                             pj[:, EXPERTS * i:EXPERTS * (i + 1)].unsqueeze(1).to_broadcast([P, TOPK, EXPERTS]), ALU.mult)
                then(last, cc)
                dve.tensor_reduce(msum[:], mch[:].rearrange("p t e -> p e t"), axis=AX, op=ALU.add)
                then(dve.tensor_reduce(rank[:, cols], prod[:], axis=AX, op=ALU.add), cc)
                dve.tensor_tensor(macc[:], macc[:], msum[:], ALU.add)
                then(dve.scalar_tensor_tensor(slotf[:], expert[:, cols], float(PLACES), rank[:, cols], ALU.mult, ALU.add), cc)
                dve.tensor_copy(tokens[:], tokid[:, bass.ts(cc, CHUNK)])
                dve.tensor_copy(slots[:], slotf[:]).then_inc(s_slot, 1)
            assert steps[0] == CHAIN_PER_CHUNK, steps

            made = [0]

            def do(ins):
                made[0] += 1
                ins.then_inc(s_md, 1)
                dve.wait_ge(s_md, made[0])

            dve.wait_ge(s_c3, 16 * 3)
            dve.wait_ge(s_m, 1)
            do(dve.tensor_copy(cnt[:], tb[0][0:EXPERTS, 0:P]))
            do(dve.tensor_scalar(cnti[:, 0], cnt[:], float(P - 1), None, ALU.add))
            do(dve.tensor_scalar(cnti[:, 1], cnti[:, 0], P.bit_length() - 1, None, ALU.arith_shift_right))
            dve.tensor_copy(tiles_f[:], cnti[:, 1])
            dve.tensor_copy(tiles_b[:], cnti[:, 1]).then_inc(s_mv, 1)
            dve.wait_ge(s_m, 2)
            dve.tensor_copy(first_b[:], ob[:, 0:EXPERTS])
            do(dve.tensor_copy(first[:], tb[1][0:EXPERTS, 0:P]))
            do(dve.tensor_tensor(after[:], first[:, 0:1], tiles_f[:, 0:1], ALU.add))
            dve.tensor_scalar(begun[:, 0], iota_t[:], first[:, 0:1], None, ALU.is_ge)
            do(dve.tensor_scalar(begun[:, 1], iota_t[:], after[:, 0:1], None, ALU.is_ge))
            do(dve.scalar_tensor_tensor(blockf[:], iota_ee[:], float(PLACES // P), first[:], ALU.mult, ALU.subtract))
            dve.tensor_tensor(owner[:], begun[:, 0], begun[:, 1], ALU.subtract).then_inc(s_mv, 1)
            dve.wait_ge(s_m, 3)
            dve.tensor_tensor(block_i[:], sc[:, 0, 0:1], iota_pt[:, 0:1], ALU.add).then_inc(s_blk, 1)
            dve.tensor_copy(etile[:], sc[:, 1, 0:MOE_TILES])
            dve.wait_ge(s_m, 4)
            do(dve.tensor_copy(rowidx[:], sc[:, 2, 0:MOE_TILES]))
            dve.sem_inc(s_map, 1)
            for q in range(CHUNKS_X):
                cols = slice(CHUNK * TOPK * q, CHUNK * TOPK * (q + 1))
                do(dve.tensor_tensor(prod3[:], chose[:, cols, :], first_b[:, :].unsqueeze(1).to_broadcast([P, CHUNK * TOPK, EXPERTS]), ALU.mult))
                do(dve.tensor_reduce(ybase[:, cols], prod3[:], axis=AX, op=ALU.add))
            do(dve.scalar_tensor_tensor(ybase[:], ybase[:], float(P), rank[:], ALU.mult, ALU.add))
            do(dve.tensor_copy(yslot[:], ybase[:]))

            dve.sem_inc(s_h, 2)
            dve.sem_inc(s_y, 2)

            def hidden(n, s):
                dve.wait_ge(s_f1, n + 3)
                dve.wait_ge(s_f2, n + 1)
                dve.tensor_scalar(hT[:, s % 2, :], sc[:, s % 2, 0:P], 0.0, None, ALU.max).then_inc(s_h, 1)

            def result(n, s):
                dve.wait_ge(s_f2, n + 3)
                if not isinstance(n, int) or n >= 4:
                    dve.wait_ge(s_ys[s % 4], (n - s % 4) * 4)
                dve.tensor_copy(ysb[:, s % 4, :], sc[:, 2 + s % 2, 0:DIM]).then_inc(s_y, 1)

            for n in range(5):
                hidden(n, n)
                if n >= 1:
                    result(n - 1, n - 1)
            with dve.Fori(0, (MOE_TILES - 8) // 4) as it:
                for i in range(4):
                    hidden(it * 4 + 5 + i, 5 + i)
                    result(it * 4 + 4 + i, i)
            for n in range(MOE_TILES - 3, MOE_TILES + 1):
                if n < MOE_TILES:
                    hidden(n, n)
                result(n - 1, n - 1)
            dve.sem_inc(s_comb, RING)
            with dve.Fori(0, TILES_IN * TOPK // RING) as it:
                for i in range(RING):
                    dve.wait_ge(s_cg[i], it * 16 + 16)
                    row = x2[:, bass.ds(it * (RING // TOPK) + i // TOPK, 1), :].rearrange("p o d -> p (o d)")
                    dve.scalar_tensor_tensor(row, xin[:, i, :], gate[:, bass.ds(it * RING + i, 1)], row, ALU.mult, ALU.add).then_inc(s_comb, 1)
                    dve.wait_ge(s_comb, it * RING + (i + 1 + RING))

CHAIN_PER_BATCH = 8
CHAIN_PER_CHUNK = 26


def constants():
    inv = (1.0 / 10000.0 ** (np.arange(0, DH, 2, dtype=np.float32) / DH)).astype(np.float32)
    ang = np.arange(SEQ, dtype=np.float32)[:, None] * inv[None, :]
    cos, sin = np.cos(ang).T.astype(np.float32), np.sin(ang).T.astype(np.float32)
    bf = np.dtype("bfloat16")
    eye = np.eye(P, dtype=np.float32)
    i = np.arange(P)
    return {
        "cos": np.ascontiguousarray(np.tile(cos, (4, 1))),
        "sin": np.ascontiguousarray(np.concatenate([sin, sin, -sin, -sin])),
        "ident": eye,
        "tri_b": (i[:, None] < i[None, :]).astype(bf),
        "ones_b": np.ones((P, P), bf),
        "tokid": (P * np.arange(TILES_IN)[None, :] + i[:, None]).astype(np.float32),
        "headm": (i[:, None] // DX == np.arange(HEADS // 2)[None, :]).astype(np.float32),
        "iota_e": np.tile(np.arange(EXPERTS, dtype=np.float32), (P, 1)),
        "iota_t": np.tile(np.arange(MOE_TILES, dtype=np.float32), (EXPERTS, 1)),
        "iota_ee": np.tile(np.arange(EXPERTS, dtype=np.float32)[:, None], (1, P)),
        "iota_pt": (P * np.arange(MOE_TILES)[None, :] + i[:, None]).astype(np.float32),
        "ident_b": eye.astype(bf),
        "causal_b": np.where(i[None, :] > i[:, None], np.float32(NEG), np.float32(0)).astype(bf),
    }


def layout(inputs):
    a = {k: np.asarray(v) for k, v in inputs.items()}
    out = dict(constants())
    out["x"] = a["x"]
    w = a["L0_attn_W_qkv"].reshape(KT, P, 3, PAIRS, 2, 2, DH // 2)
    q, k, v = w[:, :, 0], w[:, :, 1], w[:, :, 2]
    perm = lambda z: z.transpose(2, 1, 0, 4, 3, 5).reshape(PAIRS, P, KT, P)
    out["wqkv"] = np.concatenate([perm(q), perm(k), v.transpose(2, 1, 0, 3, 4, 5).reshape(PAIRS, P, KT, P)], axis=3)
    out["wo1"] = a["L0_attn_W_o1"].reshape(PAIRS, P, DIM).transpose(1, 0, 2)
    out["wo2"] = a["L0_attn_W_o2"].reshape(KT, P, DIM).transpose(1, 0, 2)
    out["gamma"] = np.broadcast_to(a["L0_attn_gamma"], (P, DIM))
    lay = lambda w: w.T.reshape(KT, P, -1).transpose(1, 0, 2)
    out["wx"] = np.stack([lay(a["L0_xattn_" + n]) for n in ("Wq", "Wk", "Wv", "Wo")], axis=1)
    out["bqk"] = np.stack([a["L0_xattn_" + n].reshape(KT, P).T for n in ("bq", "bk")], axis=1)
    out["bvo"] = np.stack([np.broadcast_to(a["L0_xattn_" + n], (P, DIM)) for n in ("bv", "bo")], axis=1)
    out["ctxT"] = a["ctx_1024"].reshape(BATCH, SK, KT, P).transpose(0, 3, 2, 1)
    out["mask"] = a["mask_BxSxS2_bk1"].reshape(BATCH, TT, P, SK).transpose(0, 2, 1, 3)
    out["sel_w"] = lay(a["L0_ffn_expert_sel"])
    out["keys"] = a["L0_ffn_keys"].reshape(EXPERTS, KT, P, HID).transpose(2, 0, 1, 3).reshape(P, EXPERTS, KT * HID)
    out["vals"] = a["L0_ffn_values"].transpose(1, 0, 2)
    return {k: np.ascontiguousarray(v) for k, v in out.items()}


def make(nc, arrays):
    t = {}
    for name, arr in arrays.items():
        t[name] = nc.dram_tensor("in_" + name, arr.shape, mybir.dt.from_np(arr.dtype), kind="ExternalInput").ap()
    t["x1"] = nc.dram_tensor("x1", (BATCH, SEQ, DIM), F32, kind="Internal").ap()
    t["x3"] = nc.dram_tensor("x3_rows", (CHUNKS_X, CHUNK * P, DIM), F32, kind="Internal").ap()
    t["table"] = nc.dram_tensor("table", (EXPERTS * PLACES, 1), F32, kind="Internal").ap()
    t["yg"] = nc.dram_tensor("yg", (MOE_TILES * P, DIM), F32, kind="Internal").ap()
    t["out"] = nc.dram_tensor("out", (BATCH * SEQ, DIM), F32, kind="ExternalOutput").ap()
    build_program(nc, t)


def kernel(**inputs):
    import concourse.bacc as bacc
    from concourse.bass_utils import run_bass_kernel_spmd

    nc = bacc.Bacc("TRN2", target_bir_lowering=False, num_devices=1)
    arrays = layout(inputs)
    make(nc, arrays)
    result = run_bass_kernel_spmd(nc, [{"in_" + k: v for k, v in arrays.items()}], core_ids=[0])
    return result.results[0]["out"].reshape(BATCH, SEQ, DIM)
```

```python
from contextlib import ExitStack

import numpy as np

import concourse.bass as bass
from concourse import mybir

F32 = mybir.dt.float32
F32R = mybir.dt.float32r
BF16 = mybir.dt.bfloat16
U32 = mybir.dt.uint32
I32 = mybir.dt.int32
U8 = mybir.dt.uint8
ALU = mybir.AluOpType
ACT = mybir.ActivationFunctionType
AX = mybir.AxisListType.X

P = 128
BATCH, SEQ, DIM = 2, 1024, 256
HEADS, DH = 16, 64
PAIRS = HEADS // 2
KT = DIM // P
TT = SEQ // P
HALF = 512
EPS = 1e-5
SK = 77
NEG = -3.0e38

DX = DIM // HEADS
CHUNK = 4
SXBUFS = 4
UX = 2 * TT
HEADS_OUT_AT = {9: (0, 0), 11: (0, 1), 17: (1, 0)}
NORMALISED_AT = {10: 0, 12: 1, 17: 2}


def last_unit(half, m):
    return 2 * (CHUNK * (half + 1) - 1) + m


TILES_IN = BATCH * TT
EXPERTS, TOPK = 64, 4
NOTES = TT * TOPK
HID = 128
PLACES = BATCH * SEQ
MOE_TILES = BATCH * SEQ * TOPK // P + EXPERTS
RING = 8

UNITS = 2 * TT
PROBS = 3
LAG = 2
STEPS = UNITS + LAG
PROJ_AT = {1: 0, 3: 1, 5: 2, 9: 3, 13: 4, 17: 5}
GROUP_END = {UNITS // 2 - 1 + LAG: 0, STEPS - 1: 1}


def unit(n):
    return n // TT, n // 2, n % 2


def score_chunks(qi):
    w = (qi + 1) * P
    return [(c, max(256, min(HALF, w - c))) for c in range(0, w, HALF)]


def transpose_chunks():
    out, seen = [], {"dve": 0, "act": 0}
    for g in range(2):
        for n in range(g * TT, (g + 1) * TT):
            qi = unit(n)[1]
            for c in range(0, qi + 1, 4):
                eng = "dve" if len(out) % 2 == 0 else "act"
                seen[eng] += 1
                out.append((n, c, min(4, qi + 1 - c), eng, seen[eng]))
        seen["act"] += 1
        out.append(("sums", g, 4, "act", seen["act"]))
    return out, seen


CHUNKS, EVACS = transpose_chunks()


def build_program(nc, t):
    ctx = ExitStack()
    with ctx:
        def sem(name):
            return ctx.enter_context(nc.semaphore(name))

        def sb_in(c, name, shape, dt=F32):
            return c.enter_context(nc.sbuf_tensor(name, shape, dt))

        ps = [ctx.enter_context(nc.psum_tensor(f"bank{i}", [P, HALF], F32)) for i in range(4, 8)]
        sc = ctx.enter_context(nc.psum_tensor("scores", [P, 4, HALF], F32))
        tb, ob, pj = ps[0:2], ps[2], ps[3]

        ident = sb_in(ctx, "ident", [P, P])
        ident_b = sb_in(ctx, "ident_b", [P, P], BF16)
        causal_b = sb_in(ctx, "causal_b", [P, P], BF16)
        stats = sb_in(ctx, "stats", [P, TT, 6])
        mv = sb_in(ctx, "mv", [P, TT, 2])
        veps = sb_in(ctx, "veps", [P, TT])
        std = sb_in(ctx, "std", [P, TT])
        rstd = sb_in(ctx, "rstd", [P, TT])

        m1 = ExitStack()
        stk = sb_in(m1, "stk", [P, 2, 2, 3, SEQ], F32R)
        qk_hi = sb_in(m1, "qk_hi", [P, 2, SEQ], F32R)
        qk_lo = sb_in(m1, "qk_lo", [P, 2, SEQ], F32R)
        v = sb_in(m1, "v", [P, 2, TT, P])
        wbuf = sb_in(m1, "wbuf", [P, 2, KT, 3 * P])
        pt = sb_in(m1, "pt", [P, 2, TT, HALF])
        probs = sb_in(m1, "probs", [P, PROBS, SEQ])
        oT = sb_in(m1, "oT", [P, PAIRS, SEQ])
        xT = sb_in(m1, "xT", [P, KT, SEQ])
        cos_t = sb_in(m1, "cos_t", [P, SEQ])
        sin_t = sb_in(m1, "sin_t", [P, SEQ])
        t1 = sb_in(m1, "t1", [P, 2, HALF])
        t2 = sb_in(m1, "t2", [P, 2, HALF])
        rot = sb_in(m1, "rot", [P, 2, HALF])
        rs = sb_in(m1, "rs", [P, UNITS])
        rsi = sb_in(m1, "rsi", [P, TT])
        rinv = sb_in(m1, "rinv", [P, TT, DH])
        nmax = sb_in(m1, "nmax", [P, UNITS])
        inv_b = sb_in(m1, "inv_b", [P, HALF])
        xb = sb_in(m1, "xb", [P, TT, DIM])
        wo1 = sb_in(m1, "wo1", [P, PAIRS, DIM])
        wo2 = sb_in(m1, "wo2", [P, KT, DIM])
        gamma = sb_in(m1, "gamma", [P, DIM])
        m1.close()
        xn = probs[:, 0:2, :].rearrange("p a b -> p (a b)").rearrange("p (t d) -> p t d", t=TT)
        h1T = pt[:, 0, 0:4, :].rearrange("p a b -> p (a b)").rearrange("p (m s) -> p m s", m=KT)

        ctx2 = ExitStack()
        s_const = sem("s_const")
        s_apart = sem("s_apart")
        s_x = sem("s_x")
        s_w = [sem("s_w0"), sem("s_w1")]
        s_wq = sem("s_wq")
        s_var = sem("s_var"); s_std = sem("s_std")
        s_lnv = sem("s_lnv")
        s_xn = sem("s_xn")
        s_xt = sem("s_xt")
        s_xtv = sem("s_xtv"); s_xta = sem("s_xta")
        s_pj = sem("s_pj")
        s_rope = sem("s_rope")
        s_rot = sem("s_rot")
        s_hi = sem("s_hi"); s_lo = sem("s_lo")
        s_v = sem("s_v")
        s_stk = [sem("s_stk0"), sem("s_stk1")]
        s_s = sem("s_s"); s_mx = sem("s_mx"); s_exp = sem("s_exp")
        s_t = sem("s_t")
        s_ev = {"dve": sem("s_evv"), "act": sem("s_eva")}
        s_rsi = sem("s_rsi"); s_rinv = sem("s_rinv"); s_pv = sem("s_pv"); s_ot = sem("s_ot")
        s_h1 = sem("s_h1"); s_h1a = sem("s_h1a"); s_o2 = sem("s_o2")
        s_x1 = sem("s_x1"); s_st = sem("s_st")

        x2 = sb_in(ctx2, "x2", [P, TILES_IN, DIM])
        keys = sb_in(ctx2, "keys", [P, EXPERTS, KT * HID])
        chose = sb_in(ctx2, "chose", [P, TILES_IN * TOPK, EXPERTS], BF16)
        expert = sb_in(ctx2, "expert", [P, TILES_IN * TOPK])
        rank = sb_in(ctx2, "rank", [P, TILES_IN * TOPK])
        gate = sb_in(ctx2, "gate", [P, TILES_IN * TOPK])
        macc = sb_in(ctx2, "macc", [P, EXPERTS], BF16)
        tri_b = sb_in(ctx2, "tri_b", [P, P], BF16)
        ones_b = sb_in(ctx2, "ones_b", [P, P], BF16)
        iota_e = sb_in(ctx2, "iota_e", [P, EXPERTS])
        rowidx = sb_in(ctx2, "rowidx", [P, MOE_TILES], U32)
        etile = sb_in(ctx2, "etile", [P, MOE_TILES], I32)
        yslot = sb_in(ctx2, "yslot", [P, TILES_IN * TOPK], U32)
        slots = sb_in(ctx2, "slots", [P, NOTES], U32)
        tokid = sb_in(ctx2, "tokid", [P, TILES_IN])
        tokens = sb_in(ctx2, "tokens", [P, TT])
        m2 = ExitStack()
        x1c = sb_in(m2, "x1c", [P, TT, DIM])
        x3 = sb_in(m2, "x3", [P, TT, DIM])
        maskc = sb_in(m2, "maskc", [P, TT, SK], U8)
        mbias = sb_in(m2, "mbias", [P, TT, SK], BF16)
        xTc = sb_in(m2, "xTc", [P, KT, SEQ])
        qT = sb_in(m2, "qT", [P, KT, SEQ])
        sx = sb_in(m2, "sx", [P, SXBUFS, HEADS // 2, SK])
        mx = sb_in(m2, "mx", [P, 2, HEADS // 2])
        ptx = sb_in(m2, "ptx", [P, HEADS, HALF])
        wx = sb_in(m2, "wx", [P, 4, KT, DIM])
        sel_w = sb_in(m2, "sel_w", [P, KT, EXPERTS])
        bqk = sb_in(m2, "bqk", [P, 2, KT])
        bvo = sb_in(m2, "bvo", [P, 2, DIM])
        ctxT = sb_in(m2, "ctxT", [P, KT, SK])
        headm = sb_in(m2, "headm", [P, HEADS // 2])
        kT = sb_in(m2, "kT", [P, KT, SK])
        kblk = sb_in(m2, "kblk", [P, KT, HEADS // 2, SK])
        vz = sb_in(m2, "vz", [SK, HEADS, 2 * DX])
        onez = sb_in(m2, "onez", [SK, 2, 2 * DX])
        itotal = sb_in(m2, "itotal", [P, 2, HALF])
        el = sb_in(m2, "el", [P, TT, EXPERTS])
        sel = sb_in(m2, "sel", [P, TT, EXPERTS])
        top = sb_in(m2, "top", [P, TT, 8])
        topi = sb_in(m2, "topi", [P, TT, 8], U32)
        mch = sb_in(m2, "mch", [P, TT, EXPERTS], BF16)
        msum = sb_in(m2, "msum", [P, EXPERTS])
        slotf = sb_in(m2, "slotf", [P, NOTES])
        zeros = sb_in(m2, "zeros", [P, EXPERTS * PLACES // P])
        m2.close()
        q_bank = [ob, pj, tb[0], tb[1]]
        oTc = xTc
        prod = ptx[:, 0:NOTES * EXPERTS // HALF, :].rearrange("p a b -> p (a b)").rearrange("p (n e) -> p n e", n=NOTES)
        m3 = ExitStack()
        vals = sb_in(m3, "vals", [P, EXPERTS, DIM])
        prod3 = sb_in(m3, "prod3", [P, NOTES, EXPERTS])
        iota_t = sb_in(m3, "iota_t", [EXPERTS, MOE_TILES])
        iota_pt = sb_in(m3, "iota_pt", [P, MOE_TILES])
        iota_ee = sb_in(m3, "iota_ee", [EXPERTS, P])
        cnt = sb_in(m3, "cnt", [EXPERTS, P])
        cnti = sb_in(m3, "cnti", [EXPERTS, 2, P], I32)
        tiles_f = sb_in(m3, "tiles_f", [EXPERTS, P])
        tiles_b = sb_in(m3, "tiles_b", [EXPERTS, P], BF16)
        first = sb_in(m3, "first", [EXPERTS, P])
        first_b = sb_in(m3, "first_b", [P, EXPERTS])
        after = sb_in(m3, "after", [EXPERTS, 1])
        begun = sb_in(m3, "begun", [EXPERTS, 2, MOE_TILES])
        owner = sb_in(m3, "owner", [EXPERTS, MOE_TILES])
        blockf = sb_in(m3, "blockf", [EXPERTS, P])
        block_i = sb_in(m3, "block_i", [MOE_TILES, 1], U32)
        table_t = sb_in(m3, "table_t", [MOE_TILES, P])
        ybase = sb_in(m3, "ybase", [P, TILES_IN * TOPK])
        idxb = sb_in(m3, "idxb", [P, RING], U32)
        xin = sb_in(m3, "xin", [P, RING, DIM])
        xgT = sb_in(m3, "xgT", [P, 2, KT * P])
        ksel = sb_in(m3, "ksel", [P, 2, KT * HID])
        hT = sb_in(m3, "hT", [P, 2, P])
        ysb = sb_in(m3, "ysb", [P, 4, DIM])
        m3.close()
        ctx2.close()

        s_c2 = sem("s_c2")
        s_zr = sem("s_zr"); s_zero = sem("s_zero")
        s_keys = sem("s_keys"); s_vals = sem("s_vals")
        s_x1c = sem("s_x1c"); s_mask = sem("s_mask"); s_ctx = sem("s_ctx")
        s_cd = sem("s_cd")
        s_kv = sem("s_kv"); s_kvd = sem("s_kvd")
        s_var2 = sem("s_var2"); s_std2 = sem("s_std2"); s_ln = sem("s_ln")
        s_tr2 = sem("s_tr2"); s_trv = sem("s_trv"); s_tra = sem("s_tra")
        s_q2 = sem("s_q2"); s_qd = sem("s_qd")
        s_sx = sem("s_sx"); s_mxx = sem("s_mxx"); s_sub = sem("s_sub"); s_ex = sem("s_ex")
        s_px = sem("s_px"); s_pxv = sem("s_pxv"); s_pxa = sem("s_pxa")
        s_ov = sem("s_ov"); s_tot = sem("s_tot"); s_ovd = sem("s_ovd")
        s_bo = sem("s_bo"); s_wox = sem("s_wox"); s_x2 = sem("s_x2")
        s_lg = sem("s_lg"); s_el = sem("s_el")
        s_mch = sem("s_mch"); s_rk = sem("s_rk"); s_slot = sem("s_slot")
        s_x3d = sem("s_x3d"); s_scat = sem("s_scat")
        s_c3 = sem("s_c3")
        s_md = sem("s_md")
        s_m = sem("s_m"); s_mv = sem("s_mv"); s_map = sem("s_map")
        s_blk = sem("s_blk"); s_tab = sem("s_tab")
        s_idx = sem("s_idx"); s_g = [sem(f"s_g{i}") for i in range(RING)]
        s_t3 = sem("s_t3"); s_xg = sem("s_xg"); s_ks = sem("s_ks")
        s_f1 = sem("s_f1"); s_h = sem("s_h"); s_f2 = sem("s_f2"); s_y = sem("s_y")
        s_ys = [sem(f"s_ys{i}") for i in range(4)]
        s_cg = [sem(f"s_cg{i}") for i in range(RING)]
        s_comb = sem("s_comb"); s_out = sem("s_out")

        block = ctx.enter_context(nc.Block())

        def apart(eng):
            eng.sem_inc(s_apart, 1)

        def pairs(eng, b, body):
            with eng.Fori(0, PAIRS // 2 - 1) as it:
                for u in range(2):
                    body(b * PAIRS + it * 2 + u, it * 2 + u, u, b * (PAIRS // 2) + it, True, True)
            for u in range(2):
                body(b * PAIRS + PAIRS - 2 + u, PAIRS - 2 + u, u, b * (PAIRS // 2) + PAIRS // 2 - 1, u == 0, False)

        def evac_chunks(eng, name, PB, what, copy):
            for idx, (m, c, tiles, who, _) in enumerate(CHUNKS):
                key = (m, c) if m == "sums" else m
                if who != name or key != what:
                    continue
                eng.wait_ge(s_t, PB * len(CHUNKS) + idx + 1)
                if m == "sums":
                    copy(inv_b[:], tb[idx % 2][:]).then_inc(s_ev[name], 1)
                    continue
                g, qi, hh = unit(m)
                if g == 1:
                    eng.wait_ge(s_pv, PB * 2 + 1)
                q0 = (qi - 4 * g) * P
                copy(pt[:, hh, c:c + tiles, q0:q0 + P],
                     tb[idx % 2][:, 0:P * tiles].rearrange("p (k q) -> p k q", k=tiles)).then_inc(s_ev[name], 1)

        def taken(eng, name, b, u):
            i, m = u // 2, u % 2
            j = 0 if name == "dve" else 1
            if i == CHUNK:
                eng.wait_ge(s_ov, b * 4 + m + 1)
            eng.wait_ge(s_px, b * (2 * UX) + 2 * u + j + 1)
            at = P * (i % CHUNK)
            dst = ptx[0:SK, 8 * m + 4 * j:8 * m + 4 * j + 4, at:at + P]
            src = tb[j][0:SK, :].rearrange("s (h q) -> s h q", h=4)
            if name == "dve":
                eng.tensor_copy(dst, src).then_inc(s_pxv, 1)
            else:
                eng.activation(dst, src, ACT.Copy).then_inc(s_pxa, 1)

        @block.sync
        def _(sp):
            for dst, src in ((ident[:], t["ident"]), (ident_b[:], t["ident_b"]), (causal_b[:], t["causal_b"]),
                             (cos_t[:], t["cos"]), (sin_t[:], t["sin"]), (gamma[:], t["gamma"]),
                             (wo1[:], t["wo1"]), (wo2[:], t["wo2"])):
                sp.dma_start(dst, src).then_inc(s_const, 16)

            def load_w(pair, u):
                sp.dma_start(wbuf[:, u], t["wqkv"][bass.ds(pair, 1)].rearrange("o p k n -> p (o k) n")).then_inc(s_w[u], 16)

            def stack(PT, u):
                for which in range(2):
                    sp.wait_ge(s_lo, PT * 4 + 2 * (which + 1))
                    for hh in range(2):
                        for part in range(2):
                            rows = slice(64 * part + 32 * hh, 64 * part + 32 * hh + 32)
                            for buf, hl in ((qk_hi, 0), (qk_lo, 1)):
                                src = buf[rows, which, :].bitcast(F32)
                                if which == 0:
                                    at = 64 * hl + 32 * part
                                    sp.dma_start(stk[at:at + 32, u, hh, 0, :].bitcast(F32), src).then_inc(s_stk[u], 16)
                                else:
                                    for dup in range(2):
                                        at = 64 * dup + 32 * part
                                        sp.dma_start(stk[at:at + 32, u, hh, 1 + hl, :].bitcast(F32), src).then_inc(s_stk[u], 16)

            with sp.Fori(0, BATCH) as b:
                sp.dma_start(xb[:], t["x"][bass.ds(b, 1)].rearrange("o (t p) d -> p (o t) d", p=P)).then_inc(s_x, 16)
                load_w(0, 0)
                load_w(1, 1)
                stack(b * PAIRS, 0)

                def body(PB, pair, u, use, nxt, nxt2):
                    if nxt2:
                        sp.wait_ge(s_pj, (PB + 1) * 6)
                        load_w(pair + 2, u)
                    if nxt:
                        stack(PB + 1, 1 - u)
                pairs(sp, b, body)
                sp.wait_ge(s_x1, b + 1)
                sp.dma_start(t["x1"][bass.ds(b, 1)].rearrange("o (t p) d -> p (o t) d", p=P), xb[:]).then_inc(s_st, 16)
                sp.wait_ge(s_st, (b + 1) * 16)
                apart(sp)

            for dst, src in ((wx[:], t["wx"]), (sel_w[:], t["sel_w"]), (bqk[:], t["bqk"]), (bvo[:], t["bvo"]),
                             (headm[:], t["headm"]), (tri_b[:], t["tri_b"]), (ones_b[:], t["ones_b"]), (iota_e[:], t["iota_e"]),
                             (tokid[:], t["tokid"])):
                sp.dma_start(dst, src).then_inc(s_c2, 16)
            sp.wait_ge(s_zr, 1)
            sp.dma_start(t["table"].rearrange("(p n) o -> p (n o)", p=P), zeros[:]).then_inc(s_zero, 16)
            with sp.Fori(0, BATCH) as b:
                sp.wait_ge(s_x2, b + 1)
                sp.dma_start(x1c[:], t["x1"][bass.ds(b, 1)].rearrange("o (t p) d -> p (o t) d", p=P)).then_inc(s_x1c, 16)
                sp.dma_start(maskc[:], t["mask"][bass.ds(b, 1)].rearrange("o p t k -> p (o t) k")).then_inc(s_mask, 16)
                sp.dma_start(ctxT[:], t["ctxT"][bass.ds(b, 1)].rearrange("o p k s -> p (o k) s")).then_inc(s_ctx, 16)
                sp.dma_start(keys[:, bass.ts(b, EXPERTS // BATCH), :],
                             t["keys"][:, bass.ts(b, EXPERTS // BATCH), :]).then_inc(s_keys, 16)
                sp.wait_ge(s_ln, b * 2 + 2)
                sp.dma_start(t["x3"][bass.ds(b, 1)].rearrange("o (t p) d -> p (o t) d", p=P), x3[:]).then_inc(s_x3d, 16)
                sp.wait_ge(s_x3d, b * 16 + 16)
                apart(sp)
            sp.wait_ge(s_slot, BATCH + 1)
            sp.wait_ge(s_x3d, 16 * BATCH)
            for dst, src in ((iota_t[:], t["iota_t"]), (iota_pt[:], t["iota_pt"]), (iota_ee[:], t["iota_ee"])):
                sp.dma_start(dst, src).then_inc(s_c3, 16)
            sp.dma_start(vals[:], t["vals"]).then_inc(s_vals, 16)
            with sp.Fori(0, MOE_TILES // 4) as it:
                for i in range(4):
                    sp.wait_ge(s_y, it * 4 + (i + 3))
                    sp.dma_start(t["yg"][bass.ts(it * 4 + i, P), :], ysb[:, i, :]).then_inc(s_ys[i], 16)
            with sp.Fori(0, TILES_IN) as tt:
                sp.wait_ge(s_comb, tt * TOPK + (TOPK + RING))
                sp.dma_start(t["out"][bass.ts(tt, P), :], x2[:, bass.ds(tt, 1), :].rearrange("p o d -> p (o d)")).then_inc(s_out, 16)
            sp.wait_ge(s_out, 16 * TILES_IN)
            for i in range(4):
                sp.wait_ge(s_ys[i], 16 * (MOE_TILES // 4))
            sp.wait_ge(s_st, 16 * BATCH)

        @block.gpsimd
        def _(pool):
            def scale_wq(PT, u, use):
                pool.wait_ge(s_w[u], (use + 1) * 16)
                apart(pool)
                pool.tensor_scalar(wbuf[:, u, :, 0:P], wbuf[:, u, :, 0:P], DH ** -0.5, None, ALU.mult).then_inc(s_wq, 1)

            def rotate(PT):
                for j in range(4):
                    pool.wait_ge(s_rope, PT * 4 + j + 1)
                    if j >= 2:
                        pool.wait_ge(s_hi, PT * 4 + j - 1)
                    pool.tensor_tensor(rot[:, j % 2], t1[:, j % 2], t2[:, j % 2], ALU.add).then_inc(s_rot, 1)
                    pool.wait_ge(s_rot, PT * 4 + j + 1)
                    pool.wait_ge(s_hi, PT * 4 + j + 1)
                    dst = slice(HALF * (j % 2), HALF * (j % 2 + 1))
                    pool.tensor_tensor(qk_lo[:, j // 2, dst], rot[:, j % 2], qk_hi[:, j // 2, dst].bitcast(F32),
                                       ALU.subtract).then_inc(s_lo, 1)

            with pool.Fori(0, BATCH) as b:
                for u in range(2):
                    scale_wq(b * PAIRS + u, u, b * (PAIRS // 2))
                rotate(b * PAIRS)

                def body(PB, pair, u, use, nxt, nxt2):
                    if nxt:
                        rotate(PB + 1)
                    if nxt2:
                        scale_wq(PB + 2, u, use + 1)
                pairs(pool, b, body)

            pool.wait_ge(s_st, 16 * BATCH)
            pool.memset(zeros[:], 0.0).then_inc(s_zr, 1)
            with pool.Fori(0, BATCH) as b:
                pool.wait_ge(s_ln, b * 2 + 1)
                apart(pool)
                pool.tensor_tensor(x1c[:], x1c[:], bvo[:, 1, :].unsqueeze(1).to_broadcast([P, TT, DIM]), ALU.add).then_inc(s_bo, 1)
                pool.wait_ge(s_zero, 16)
                pool.wait_ge(s_slot, b + 2)
                apart(pool)
                for i in range(NOTES):
                    pool.indirect_dma_start(t["table"], bass.IndirectOffsetOnAxis(ap=slots[:, i:i + 1], axis=0),
                                            tokens[:, i // TOPK:i // TOPK + 1], None).then_inc(s_scat, 16)
                pool.wait_ge(s_scat, b * (16 * NOTES) + 16 * NOTES)
            pool.wait_ge(s_scat, 16 * TILES_IN * TOPK)
            pool.wait_ge(s_x3d, 16 * BATCH)
            pool.wait_ge(s_blk, 1)
            pool.indirect_dma_start(table_t[:], None, t["table"].rearrange("(n p) o -> n (p o)", p=P),
                                    bass.IndirectOffsetOnAxis(ap=block_i[:], axis=0)).then_inc(s_tab, 16)
            pool.wait_ge(s_map, 1)
            with pool.Fori(0, MOE_TILES // RING) as it:
                pool.tensor_copy(idxb[:], rowidx[:, bass.ts(it, RING)]).then_inc(s_idx, 1)
                pool.wait_ge(s_idx, it + 1)
                for i in range(RING):
                    pool.wait_ge(s_t3, it * RING + i + 1)
                    apart(pool)
                    pool.indirect_dma_start(xin[:, i, :], None, t["x3"].rearrange("c n d -> (c n) d"), bass.IndirectOffsetOnAxis(ap=idxb[:, i:i + 1], axis=0)).then_inc(s_g[i], 16)
                for i in range(RING):
                    pool.wait_ge(s_g[i], it * 16 + 16)
            for i in range(4):
                pool.wait_ge(s_ys[i], 16 * (MOE_TILES // 4))
            with pool.Fori(0, TILES_IN * TOPK // RING) as it:
                pool.tensor_copy(idxb[:], yslot[:, bass.ts(it, RING)]).then_inc(s_idx, 1)
                pool.wait_ge(s_idx, it + MOE_TILES // RING + 1)
                for i in range(RING):
                    pool.wait_ge(s_comb, it * RING + i + 1)
                    apart(pool)
                    pool.indirect_dma_start(xin[:, i, :], None, t["yg"], bass.IndirectOffsetOnAxis(ap=idxb[:, i:i + 1], axis=0)).then_inc(s_cg[i], 16)
                for i in range(RING):
                    pool.wait_ge(s_cg[i], it * 16 + 16)

        @block.tensor
        def _(pe):
            def proj(PT, u, j, first=False):
                if j == 0:
                    pe.wait_ge(s_wq, PT + 1)
                    if not first:
                        pe.wait_ge(s_v, PT * 2)
                elif j < 5:
                    pe.wait_ge(s_rope, PT * 4 + j)
                else:
                    pe.wait_ge(s_v, PT * 2 + 1)
                if j < 4:
                    for k in range(KT):
                        last = pe.matmul(pj[:], wbuf[:, u, k, (j // 2) * P:(j // 2 + 1) * P],
                                         xT[:, k, HALF * (j % 2):HALF * (j % 2 + 1)], start=k == 0, stop=k == KT - 1)
                else:
                    for i in range(4):
                        tt = 4 * (j - 4) + i
                        for k in range(KT):
                            last = pe.matmul(pj[:, P * i:P * (i + 1)], xT[:, k, P * tt:P * (tt + 1)],
                                             wbuf[:, u, k, 2 * P:3 * P], start=k == 0, stop=k == KT - 1)
                last.then_inc(s_pj, 1)

            def scores(PB, u, n):
                _, qi, hh = unit(n)
                if n >= 2:
                    pe.wait_ge(s_exp, PB * UNITS + n - 1)
                q = stk[:, u, hh, 0, qi * P:(qi + 1) * P]
                for c, w in score_chunks(qi):
                    out = sc[:, 2 * (n % 2) + c // HALF, 0:w]
                    diag = c <= qi * P < c + HALF
                    pe.matmul(out, q, stk[:, u, hh, 1, c:c + w], start=True, stop=False)
                    last = pe.matmul(out, q, stk[:, u, hh, 2, c:c + w], start=False, stop=not diag)
                    if diag:
                        o = qi * P - c
                        last = pe.matmul(sc[:, 2 * (n % 2) + c // HALF, o:o + P], ident_b[:], causal_b[:],
                                         start=False, stop=True)
                last.then_inc(s_s, 1)

            def reuse(PB, idx):
                if idx >= 2:
                    eng, count = CHUNKS[idx - 2][3:]
                    pe.wait_ge(s_ev[eng], PB * EVACS[eng] + count)

            def transposes(PB, n):
                pe.wait_ge(s_exp, PB * UNITS + n + 1)
                for idx, (m, c, tiles, _, _) in enumerate(CHUNKS):
                    if m == n:
                        reuse(PB, idx)
                        for i in range(tiles):
                            last = pe.transpose(tb[idx % 2][:, P * i:P * (i + 1)],
                                                probs[:, n % PROBS, (c + i) * P:(c + i + 1) * P], ident[:])
                        last.then_inc(s_t, 1)

            def finish_group(PB, u, g):
                idx = next(i for i, ch in enumerate(CHUNKS) if ch[0] == "sums" and ch[1] == g)
                reuse(PB, idx)
                pe.wait_ge(s_rinv, PB * 2 + g + 1)
                for i in range(4):
                    last = pe.transpose(tb[idx % 2][:, P * i:P * (i + 1)],
                                        rinv[:, 2 * i:2 * i + 2, :].rearrange("p h d -> p (h d)"), ident[:])
                last.then_inc(s_t, 1)
                for eng in ("dve", "act"):
                    pe.wait_ge(s_ev[eng], PB * EVACS[eng] + max(c[4] for c in CHUNKS[:idx] if c[3] == eng))
                pe.wait_ge(s_v, (PB + 1) * 2)
                tiles = 4 * (g + 1)
                for kt in range(tiles):
                    q0 = max(0, kt - 4 * g) * P
                    for hh in range(2):
                        last = pe.matmul(ob[DH * hh:DH * (hh + 1), q0:HALF], v[:, u, kt, DH * hh:DH * (hh + 1)],
                                         pt[:, hh, kt, q0:HALF], start=kt == 0, stop=kt == tiles - 1)
                last.then_inc(s_pv, 1)

            pe.wait_ge(s_const, 16 * 8)
            with pe.Fori(0, BATCH) as b:
                pe.wait_ge(s_xn, b + 1)
                for c in range(4):
                    k, half = c // 2, c % 2
                    for i in range(4):
                        last = pe.transpose(sc[:, c, P * i:P * (i + 1)], xn[:, 4 * half + i, P * k:P * (k + 1)], ident[:])
                    last.then_inc(s_xt, 1)
                pe.wait_ge(s_xtv, (b + 1) * 2)
                pe.wait_ge(s_xta, (b + 1) * 2)
                for j in range(6):
                    proj(b * PAIRS, 0, j, first=True)

                def body(PB, pair, u, use, nxt, nxt2):
                    pe.wait_ge(s_stk[u], (use + 1) * (24 * 16))
                    for k in range(STEPS):
                        if k < UNITS:
                            scores(PB, u, k)
                        late = k in GROUP_END
                        if late:
                            transposes(PB, k - LAG)
                        if nxt and k in PROJ_AT:
                            proj(PB + 1, 1 - u, PROJ_AT[k])
                        if k >= LAG and not late:
                            transposes(PB, k - LAG)
                        if late:
                            finish_group(PB, u, GROUP_END[k])
                pairs(pe, b, body)
                pe.wait_ge(s_ot, (b + 1) * (2 * PAIRS))
                for m in range(KT):
                    for c in range(2):
                        for k in range(PAIRS):
                            last = pe.matmul(sc[:, 2 * m + c, :], wo1[:, k, P * m:P * (m + 1)],
                                             oT[:, k, HALF * c:HALF * (c + 1)], start=k == 0, stop=k == PAIRS - 1)
                        last.then_inc(s_h1, 1)
                pe.wait_ge(s_h1a, (b + 1) * 4)
                for i in range(TT):
                    for k in range(KT):
                        last = pe.matmul(ps[i // 2][:, DIM * (i % 2):DIM * (i % 2 + 1)], h1T[:, k, P * i:P * (i + 1)],
                                         wo2[:, k, :], start=k == 0, stop=k == KT - 1)
                    last.then_inc(s_o2, 1)

            pe.wait_ge(s_c2, 16 * 9)

            def transpose_sequence(b, k):
                pe.wait_ge(s_ln, b * 2 + k)
                for h in range(2):
                    for kt in range(KT):
                        for i in range(CHUNK):
                            last = pe.transpose(sc[:, 2 * h + kt, P * i:P * (i + 1)],
                                                x3[:, CHUNK * h + i, P * kt:P * (kt + 1)], ident[:])
                        last.then_inc(s_tr2, 1)
                pe.wait_ge(s_trv, b * 4 + 2 * k)
                pe.wait_ge(s_tra, b * 4 + 2 * k)

            with pe.Fori(0, BATCH) as b:
                pe.wait_ge(s_slot, b + 1)
                pe.wait_ge(s_ctx, b * 16 + 16)
                for m in range(KT):
                    for k in range(KT):
                        pe.matmul(tb[0][:, SK * m:SK * (m + 1)], wx[:, 1, k, P * m:P * (m + 1)], ctxT[:, k, :], start=k == 0, stop=k == KT - 1)
                for k in range(KT):
                    last = pe.matmul(tb[1][0:SK, 0:DIM], ctxT[:, k, :], wx[:, 2, k, :], start=k == 0, stop=k == KT - 1)
                last.then_inc(s_kv, 1)
                transpose_sequence(b, 1)
                for h in range(2):
                    if h == 1:
                        pe.wait_ge(s_kvd, b + 1)
                    for m in range(KT):
                        for k in range(KT):
                            last = pe.matmul(q_bank[2 * h + m][:], wx[:, 0, k, P * m:P * (m + 1)], xTc[:, k, HALF * h:HALF * (h + 1)],
                                             start=k == 0, stop=k == KT - 1)
                        last.then_inc(s_q2, 1)
                pe.wait_ge(s_qd, b * 4 + 4)

                def head_scores(u):
                    i, m = u // 2, u % 2
                    if u >= 2:
                        pe.wait_ge(s_sub, b * UX + u - 1)
                    for j in range(2):
                        out = sc[:, 2 * m + j, 0:4 * SK]
                        pe.matmul(out, qT[:, m, P * i:P * (i + 1)],
                                  kblk[:, m, 4 * j:4 * j + 4, :].rearrange("p h s -> p (h s)"), start=True, stop=False)
                        last = pe.matmul(out, ident_b[:], mbias[:, i, :].unsqueeze(1).to_broadcast([P, 4, SK]),
                                         start=False, stop=True)
                    last.then_inc(s_sx, 1)

                def probs_T(u):
                    pe.wait_ge(s_ex, b * UX + u + 1)
                    for j in range(2):
                        if u >= 1:
                            pe.wait_ge(s_pxa if j else s_pxv, b * UX + u)
                        for h in range(4):
                            last = pe.transpose(tb[j][0:SK, P * h:P * (h + 1)], sx[:, u % SXBUFS, 4 * j + h, :], ident[:])
                        last.then_inc(s_px, 1)

                def head_out(h, m, out, total):
                    pe.wait_ge(s_pxv, b * UX + last_unit(h, m) + 1)
                    pe.wait_ge(s_pxa, b * UX + last_unit(h, m) + 1)
                    if (h, m) in ((0, 1), (1, 0)):
                        pe.wait_ge(s_ovd, b * 4 + 2 * h + m)
                    for odd in range(2):
                        for g in range(4):
                            head = 8 * m + 2 * g + odd
                            rows = slice(32 * g, 32 * (g + 1))
                            pe.matmul(out[rows, :], vz[:, head, :], ptx[0:SK, head, :], start=odd == 0, stop=odd == 1)
                    for odd in range(2):
                        for g in range(4):
                            head = 8 * m + 2 * g + odd
                            rows = slice(32 * g, 32 * (g + 1))
                            last = pe.matmul(total[rows, :], onez[:, odd, :], ptx[0:SK, head, :], start=odd == 0, stop=odd == 1)
                    last.then_inc(s_ov, 1)

                def project(h):
                    pe.wait_ge(s_ovd, b * 4 + 2 * (h + 1))
                    for i in range(CHUNK * h, CHUNK * (h + 1)):
                        for k in range(KT):
                            last = pe.matmul(sc[:, i // 2, DIM * (i % 2):DIM * (i % 2 + 1)], oTc[:, k, P * i:P * (i + 1)],
                                             wx[:, 3, k, :], start=k == 0, stop=k == KT - 1)
                    last.then_inc(s_wox, 1)

                for u in range(UX + LAG):
                    if u < UX:
                        head_scores(u)
                    if u >= LAG:
                        probs_T(u - LAG)
                    if u in HEADS_OUT_AT:
                        head_out(*HEADS_OUT_AT[u], ob, pj)
                pe.wait_ge(s_sub, b * UX + UX)
                project(0)
                head_out(1, 1, tb[0], tb[1])
                project(1)
                transpose_sequence(b, 2)
                for i in range(TT):
                    for k in range(KT):
                        last = pe.matmul(ob[:, EXPERTS * i:EXPERTS * (i + 1)], xTc[:, k, P * i:P * (i + 1)], sel_w[:, k, :],
                                         start=k == 0, stop=k == KT - 1)
                last.then_inc(s_lg, 1)
                pe.wait_ge(s_mch, b + 1)
                for i in range(TT):
                    out = pj[:, EXPERTS * i:EXPERTS * (i + 1)]
                    pe.matmul(out, tri_b[:], mch[:, i, :], start=True, stop=False)
                    for j in range(i):
                        pe.matmul(out, ones_b[:], mch[:, j, :], start=False, stop=False)
                    last = pe.matmul(out, ones_b[:], macc[:], start=False, stop=True)
                last.then_inc(s_rk, 1)

            pe.wait_ge(s_slot, BATCH + 1)
            pe.matmul(tb[0][0:EXPERTS, 0:P], macc[:], ones_b[:], start=True, stop=True).then_inc(s_m, 1)
            pe.wait_ge(s_mv, 1)
            pe.matmul(tb[1][0:EXPERTS, 0:P], tri_b[0:EXPERTS, 0:EXPERTS], tiles_b[:], start=True, stop=True)
            pe.matmul(ob[:, 0:EXPERTS], tiles_b[:], tri_b[0:EXPERTS, 0:EXPERTS], start=True, stop=True).then_inc(s_m, 1)
            pe.wait_ge(s_mv, 2)
            pe.matmul(sc[:, 0, 0:P], owner[:], blockf[:], start=True, stop=True)
            pe.matmul(sc[:, 1, 0:MOE_TILES], iota_ee[:], owner[:], start=True, stop=True).then_inc(s_m, 1)
            pe.wait_ge(s_tab, 16)
            pe.transpose(sc[:, 2, 0:MOE_TILES], table_t[:], ident[:]).then_inc(s_m, 1)

            pe.sem_inc(s_t3, RING)
            pe.sem_inc(s_f1, 2)
            pe.sem_inc(s_f2, 2)
            pe.wait_ge(s_map, 1)
            pe.wait_ge(s_vals, 16)

            def tile_T(n, s, use):
                pe.wait_ge(s_g[s % RING], use * 16 + 16)
                pe.wait_ge(s_xg, n + 1)
                for k in range(KT):
                    last = pe.transpose(tb[s % 2][:, P * k:P * (k + 1)], xin[:, s % RING, P * k:P * (k + 1)], ident[:])
                last.then_inc(s_t3, 1)

            def tile_keys(n, s):
                pe.wait_ge(s_xg, n + 3)
                pe.wait_ge(s_ks, n + 3)
                pe.wait_ge(s_h, n + 1)
                for k in range(KT):
                    last = pe.matmul(sc[:, s % 2, 0:P], ksel[:, s % 2, HID * k:HID * (k + 1)], xgT[:, s % 2, P * k:P * (k + 1)],
                                     start=k == 0, stop=k == KT - 1)
                last.then_inc(s_f1, 1)

            def tile_values(n, s):
                e = pe.value_load(etile[0:1, bass.ds(n, 1)], min_val=0, max_val=EXPERTS - 1)
                pe.wait_ge(s_h, n + 3)
                pe.wait_ge(s_y, n + 1)
                pe.matmul(sc[:, 2 + s % 2, 0:DIM], hT[:, s % 2, :], vals[:, bass.ds(e, 1), :].rearrange("p o d -> p (o d)"),
                          start=True, stop=True).then_inc(s_f2, 1)

            tile_T(0, 0, 0)
            tile_T(1, 1, 0)
            tile_keys(0, 0)
            with pe.Fori(0, MOE_TILES // RING - 1) as it:
                for i in range(RING):
                    s = i + 2
                    n = it * RING + s
                    tile_T(n, s, it + s // RING)
                    tile_keys(n - 1, s - 1)
                    tile_values(n - 2, s - 2)
            for n in range(MOE_TILES - RING + 2, MOE_TILES + 2):
                if n < MOE_TILES:
                    tile_T(n, n, n // RING)
                if n - 1 < MOE_TILES:
                    tile_keys(n - 1, n - 1)
                tile_values(n - 2, n - 2)

        @block.scalar
        def _(act):
            def exps(PB, n):
                _, qi, _ = unit(n)
                act.wait_ge(s_mx, PB * UNITS + n + 1)
                if n >= PROBS:
                    done = sum(1 for c in CHUNKS if c[0] != "sums" and c[0] <= n - PROBS or c[0] == "sums" and n - PROBS >= TT * (c[1] + 1))
                    act.wait_ge(s_t, PB * len(CHUNKS) + done)
                w = (qi + 1) * P
                src = sc[:, 2 * (n % 2):2 * (n % 2) + 2, :].rearrange("p a b -> p (a b)")[:, 0:w]
                act.activation(probs[:, n % PROBS, 0:w], src, ACT.Exp, bias=nmax[:, n:n + 1],
                               accum_out=rs[:, n:n + 1]).then_inc(s_exp, 1)

            def evac(PB, what):
                evac_chunks(act, "act", PB, what, lambda o, i: act.activation(o, i, ACT.Copy))

            def hi(PT, j):
                act.wait_ge(s_rot, PT * 4 + j + 1)
                act.activation(qk_hi[:, j // 2, HALF * (j % 2):HALF * (j % 2 + 1)], rot[:, j % 2], ACT.Copy).then_inc(s_hi, 1)

            def v_out(PT, u, j):
                act.wait_ge(s_pj, PT * 6 + j + 1)
                act.activation(v[:, u, 4 * (j - 4):4 * (j - 3), :], pj[:].rearrange("p (t d) -> p t d", t=4), ACT.Copy).then_inc(s_v, 1)

            with act.Fori(0, BATCH) as b:
                act.wait_ge(s_var, b * 2 + 1)
                act.activation(std[:], veps[:], ACT.Sqrt).then_inc(s_std, 1)
                for c in (2, 3):
                    act.wait_ge(s_xt, b * 4 + c + 1)
                    act.activation(xT[:, 1, HALF * (c % 2):HALF * (c % 2 + 1)], sc[:, c, :], ACT.Copy).then_inc(s_xta, 1)
                for j in range(4):
                    hi(b * PAIRS, j)
                for j in (4, 5):
                    v_out(b * PAIRS, 0, j)

                def body(PB, pair, u, use, nxt, nxt2):
                    for k in range(STEPS):
                        if k < UNITS:
                            exps(PB, k)
                        if nxt and PROJ_AT.get(k - 1, 9) < 4:
                            hi(PB + 1, PROJ_AT[k - 1])
                        if k >= LAG:
                            evac(PB, k - LAG)
                        if nxt and PROJ_AT.get(k, 0) >= 4:
                            v_out(PB + 1, 1 - u, PROJ_AT[k])
                        if k in GROUP_END:
                            evac(PB, ("sums", GROUP_END[k]))
                pairs(act, b, body)
                for m in range(KT):
                    for c in range(2):
                        act.wait_ge(s_h1, b * 4 + 2 * m + c + 1)
                        act.activation(h1T[:, m, HALF * c:HALF * (c + 1)], sc[:, 2 * m + c, :], ACT.Relu).then_inc(s_h1a, 1)
                act.wait_ge(s_var, b * 2 + 2)
                act.activation(std[:], veps[:], ACT.Sqrt).then_inc(s_std, 1)

            def ln_and_transposes(b, k):
                act.wait_ge(s_var2, b * 2 + k)
                act.activation(std[:], veps[:], ACT.Sqrt).then_inc(s_std2, 1)
                for h in range(2):
                    act.wait_ge(s_tr2, b * 8 + 4 * (k - 1) + 2 * h + 2)
                    act.activation(xTc[:, 1, HALF * h:HALF * (h + 1)], sc[:, 2 * h + 1, :], ACT.Copy).then_inc(s_tra, 1)

            with act.Fori(0, BATCH) as b:
                ln_and_transposes(b, 1)
                for u in range(UX + LAG):
                    if u < UX:
                        act.wait_ge(s_sub, b * UX + u + 1)
                        act.activation(sx[:, u % SXBUFS], sx[:, u % SXBUFS], ACT.Exp).then_inc(s_ex, 1)
                    if u >= LAG:
                        taken(act, "act", b, u - LAG)
                ln_and_transposes(b, 2)
                act.wait_ge(s_lg, b + 1)
                act.activation(el[:], ob[:].rearrange("p (t e) -> p t e", t=TT), ACT.Exp, scale=-1.0).then_inc(s_el, 1)

            act.sem_inc(s_xg, 2)
            act.sem_inc(s_ks, 2)
            act.wait_ge(s_map, 1)
            act.wait_ge(s_keys, 16 * BATCH)
            with act.Fori(0, MOE_TILES // 2) as it:
                for i in range(2):
                    n = it * 2 + i
                    e = act.value_load(etile[0:1, bass.ds(n, 1)], min_val=0, max_val=EXPERTS - 1)
                    act.wait_ge(s_f1, n + 1)
                    act.activation(ksel[:, i, :], keys[:, bass.ds(e, 1), :].rearrange("p o d -> p (o d)"), ACT.Copy).then_inc(s_ks, 1)
                    act.wait_ge(s_t3, n + RING + 1)
                    act.activation(xgT[:, i, :], tb[i][:, 0:KT * P], ACT.Copy).then_inc(s_xg, 1)

        @block.vector
        def _(dve):
            LN_STEPS = 30
            chain = [0]

            def link(ins, b):
                chain[0] += 1
                ins.then_inc(s_lnv, 1)
                dve.wait_ge(s_lnv, b * chain[1] + chain[0])
                apart(dve)

            def ln_stats(b, src, k):
                for i in range(TT):
                    last = dve.bn_stats(stats[:, i, :], src(i))
                link(last, b)
                for i in range(TT):
                    last = dve.bn_aggr(mv[:, i, :], stats[:, i, :])
                link(last, b)
                dve.tensor_scalar(veps[:], mv[:, :, 1], EPS, None, ALU.add).then_inc(s_var, 1)
                dve.wait_ge(s_std, b * 2 + k)
                link(dve.reciprocal(rstd[:], std[:]), b)

            def rope(PT, j):
                dve.wait_ge(s_pj, PT * 6 + j + 1)
                if j >= 2:
                    dve.wait_ge(s_rot, PT * 4 + j - 1)
                cols = slice(HALF * (j % 2), HALF * (j % 2 + 1))
                dve.tensor_tensor(t1[:, j % 2], pj[:], cos_t[:, cols], ALU.mult)
                dve.tensor_tensor(t2[0:64, j % 2], pj[64:128, :], sin_t[64:128, cols], ALU.mult)
                dve.tensor_tensor(t2[64:128, j % 2], pj[0:64, :], sin_t[0:64, cols], ALU.mult).then_inc(s_rope, 1)

            def row_max(PB, n):
                _, qi, _ = unit(n)
                w = (qi + 1) * P
                dve.wait_ge(s_s, PB * UNITS + n + 1)
                src = sc[:, 2 * (n % 2):2 * (n % 2) + 2, :].rearrange("p a b -> p (a b)")[:, 0:w]
                dve.tensor_reduce(nmax[:, n:n + 1], src, axis=AX, op=ALU.max, negate=True).then_inc(s_mx, 1)

            def inverse_sums(PB, g):
                dve.wait_ge(s_exp, PB * UNITS + TT * (g + 1))
                dve.reciprocal(rsi[:], rs[:, TT * g:TT * (g + 1)]).then_inc(s_rsi, 1)
                dve.wait_ge(s_rsi, PB * 2 + g + 1)
                dve.tensor_copy(rinv[:], rsi[:, :].unsqueeze(2).to_broadcast([P, TT, DH])).then_inc(s_rinv, 1)

            def out_T(PB, pair, g):
                dve.wait_ge(s_pv, PB * 2 + g + 1)
                count = next(c[4] for c in CHUNKS if c[0] == "sums" and c[1] == g)
                dve.wait_ge(s_ev["act"], PB * EVACS["act"] + count)
                dst = oT[:, bass.ds(pair, 1), HALF * g:HALF * (g + 1)].rearrange("p o s -> p (o s)")
                dve.tensor_tensor(dst, ob[:], inv_b[:], ALU.mult).then_inc(s_ot, 1)

            chain.append(0)
            chain[1] = CHAIN_PER_BATCH
            dve.wait_ge(s_const, 16 * 8)
            with dve.Fori(0, BATCH) as b:
                dve.wait_ge(s_x, (b + 1) * 16)
                apart(dve)
                ln_stats(b, lambda i: xb[:, i, :], 1)
                for i in range(TT):
                    last = dve.tensor_scalar(xn[:, i, :], xb[:, i, :], mv[:, i, 0:1], rstd[:, i:i + 1], ALU.subtract, ALU.mult)
                last.then_inc(s_xn, 1)
                for c in (0, 1):
                    dve.wait_ge(s_xt, b * 4 + c + 1)
                    dve.tensor_copy(xT[:, 0, HALF * c:HALF * (c + 1)], sc[:, c, :]).then_inc(s_xtv, 1)
                for j in range(4):
                    rope(b * PAIRS, j)

                def body(PB, pair, u, use, nxt, nxt2):
                    for k in range(STEPS):
                        if k < UNITS:
                            row_max(PB, k)
                        late = k in GROUP_END
                        if late:
                            inverse_sums(PB, GROUP_END[k])
                            evac_chunks(dve, "dve", PB, k - LAG, dve.tensor_copy)
                        if nxt and PROJ_AT.get(k, 9) < 4:
                            rope(PB + 1, PROJ_AT[k])
                        if k >= LAG and not late:
                            evac_chunks(dve, "dve", PB, k - LAG, dve.tensor_copy)
                        if k == 11:
                            out_T(PB, pair, 0)
                    out_T(PB, pair, 1)
                pairs(dve, b, body)
                dve.wait_ge(s_o2, (b + 1) * TT)
                apart(dve)
                o2 = lambda i: ps[i // 2][:, DIM * (i % 2):DIM * (i % 2 + 1)]
                ln_stats(b, o2, 2)
                for i in range(TT):
                    last = dve.tensor_scalar(xn[:, i, :], o2(i), mv[:, i, 0:1], rstd[:, i:i + 1], ALU.subtract, ALU.mult)
                link(last, b)
                link(dve.tensor_tensor(xn, xn, gamma[:, :].unsqueeze(1).to_broadcast([P, TT, DIM]), ALU.mult), b)
                dve.tensor_tensor(xb[:], xb[:], xn, ALU.add).then_inc(s_x1, 1)
                assert chain[0] == CHAIN_PER_BATCH, chain

            steps = [0]

            def then(ins, b):
                steps[0] += 1
                ins.then_inc(s_cd, 1)
                dve.wait_ge(s_cd, b * CHAIN_PER_SEQUENCE + steps[0])
                apart(dve)

            def layer_norm(b, k, src):
                for i in range(TT):
                    last = dve.bn_stats(stats[:, i, :], src(i))
                then(last, b)
                for i in range(TT):
                    last = dve.bn_aggr(mv[:, i, :], stats[:, i, :])
                then(last, b)
                dve.tensor_scalar(veps[:], mv[:, :, 1], EPS, None, ALU.add).then_inc(s_var2, 1)
                dve.wait_ge(s_std2, b * 2 + k)
                then(dve.reciprocal(rstd[:], std[:]), b)
                for i in range(TT):
                    last = dve.tensor_scalar(x3[:, i, :], src(i), mv[:, i, 0:1], rstd[:, i:i + 1], ALU.subtract, ALU.mult)
                last.then_inc(s_ln, 1)

            def transposes_out(b, k):
                for h in range(2):
                    dve.wait_ge(s_tr2, b * 8 + 4 * (k - 1) + 2 * h + 1)
                    dve.tensor_copy(xTc[:, 0, HALF * h:HALF * (h + 1)], sc[:, 2 * h, :]).then_inc(s_trv, 1)

            dve.wait_ge(s_c2, 16 * 9)
            dve.memset(vz[:], 0.0)
            for odd in range(2):
                dve.memset(onez[:, odd, DX * odd:DX * (odd + 1)], 1.0)
                dve.memset(onez[:, odd, DX * (1 - odd):DX * (2 - odd)], 0.0)
            dve.sem_inc(s_x2, 1)
            dve.memset(macc[:], 0.0).then_inc(s_slot, 1)
            with dve.Fori(0, BATCH) as b:
                steps[0] = 0
                dve.wait_ge(s_x1c, b * 16 + 16)
                apart(dve)
                layer_norm(b, 1, lambda i: x1c[:, i, :])
                dve.wait_ge(s_mask, b * 16 + 16)
                dve.tensor_scalar(mbias[:], maskc[:], NEG, None, ALU.mult)
                transposes_out(b, 1)
                dve.wait_ge(s_kv, b + 1)
                for m in range(KT):
                    last = dve.tensor_scalar(kT[:, m, :], tb[0][:, SK * m:SK * (m + 1)], bqk[:, 1, m:m + 1], None, ALU.add)
                then(last, b)
                for m in range(KT):
                    dve.tensor_tensor(kblk[:, m], kT[:, m, :].unsqueeze(1).to_broadcast([P, HEADS // 2, SK]),
                                      headm[:, :].unsqueeze(2).to_broadcast([P, HEADS // 2, SK]), ALU.mult)
                for odd in range(2):
                    last = dve.tensor_tensor(vz[:].rearrange("s (g o) d -> s g o d", o=2)[:, :, odd, DX * odd:DX * (odd + 1)],
                                             tb[1][0:SK, 0:DIM].rearrange("s (g o d) -> s g o d", o=2, d=DX)[:, :, odd, :],
                                             bvo[0:SK, 0, :].rearrange("s (g o d) -> s g o d", o=2, d=DX)[:, :, odd, :], ALU.add)
                last.then_inc(s_kvd, 1)
                for n in range(4):
                    h, m = n // 2, n % 2
                    dve.wait_ge(s_q2, b * 4 + n + 1)
                    dve.tensor_scalar(qT[:, m, HALF * h:HALF * (h + 1)], q_bank[n][:], bqk[:, 0, m:m + 1], DX ** -0.5,
                                      ALU.add, ALU.mult).then_inc(s_qd, 1)

                def score_max(u):
                    m = u % 2
                    dve.wait_ge(s_sx, b * UX + u + 1)
                    dve.tensor_reduce(mx[:, m, :].rearrange("p (j h) -> p j h", j=2),
                                      sc[:, 2 * m:2 * m + 2, 0:4 * SK].rearrange("p j (h k) -> p j h k", h=4),
                                      axis=AX, op=ALU.max).then_inc(s_mxx, 1)

                def score_shift(u):
                    m = u % 2
                    if u >= SXBUFS:
                        dve.wait_ge(s_px, b * (2 * UX) + 2 * (u - SXBUFS + 1))
                    dve.wait_ge(s_mxx, b * UX + u + 1)
                    dve.tensor_tensor(sx[:, u % SXBUFS].rearrange("p (j h) k -> p j h k", j=2),
                                      sc[:, 2 * m:2 * m + 2, 0:4 * SK].rearrange("p j (h k) -> p j h k", h=4),
                                      mx[:, m, :].rearrange("p (j h) -> p j h", j=2).unsqueeze(3).to_broadcast([P, 2, 4, SK]),
                                      ALU.subtract).then_inc(s_sub, 1)

                def normalised(n, out, total):
                    dve.wait_ge(s_ov, b * 4 + n + 1)
                    dve.reciprocal(itotal[:, n % 2], total[:]).then_inc(s_tot, 1)
                    dve.wait_ge(s_tot, b * 4 + n + 1)
                    h, m = n // 2, n % 2
                    dve.tensor_tensor(oTc[:, m, HALF * h:HALF * (h + 1)], out[:], itotal[:, n % 2], ALU.mult).then_inc(s_ovd, 1)

                for u in range(UX + LAG):
                    if u < UX:
                        score_max(u)
                        score_shift(u)
                    if u >= LAG:
                        taken(dve, "dve", b, u - LAG)
                    if u in NORMALISED_AT:
                        normalised(NORMALISED_AT[u], ob, pj)
                dve.wait_ge(s_bo, b + 1)
                for i in range(4):
                    if i == 2:
                        normalised(3, tb[0], tb[1])
                    dve.wait_ge(s_wox, b * 2 + i // 2 + 1)
                    last = dve.tensor_tensor(x2[:, bass.ds(b * TT + 2 * i, 2), :], sc[:, i, :].rearrange("p (t d) -> p t d", t=2),
                                             x1c[:, 2 * i:2 * i + 2, :], ALU.add)
                last.then_inc(s_x2, 1)
                dve.wait_ge(s_x2, b + 2)
                apart(dve)
                layer_norm(b, 2, lambda i: x2[:, bass.ds(b * TT + i, 1), :].rearrange("p o d -> p (o d)"))
                transposes_out(b, 2)
                dve.wait_ge(s_el, b + 1)
                then(dve.tensor_scalar(el[:], el[:], 1.0, None, ALU.add), b)
                then(dve.reciprocal(sel[:], el[:]), b)
                for i in range(TT):
                    last = dve.max(top[:, i, :], sel[:, i, :])
                then(last, b)
                for i in range(TT):
                    last = dve.max_index(topi[:, i, :], top[:, i, :], sel[:, i, :])
                then(last, b)
                cols = bass.ts(b, NOTES)
                dve.tensor_copy(gate[:, cols].rearrange("p (t j) -> p t j", t=TT), top[:, :, 0:TOPK])
                then(dve.tensor_copy(expert[:, cols].rearrange("p (t j) -> p t j", t=TT), topi[:, :, 0:TOPK]), b)
                then(dve.tensor_tensor(chose[:, cols, :], iota_e[:, :].unsqueeze(1).to_broadcast([P, NOTES, EXPERTS]),
                                       expert[:, cols].unsqueeze(2).to_broadcast([P, NOTES, EXPERTS]), ALU.is_equal), b)
                with nc.allow_low_precision(reason="sums of zeros and ones, exact in bfloat16"):
                    dve.tensor_reduce(mch[:], chose[:, cols, :].rearrange("p (t j) e -> p t e j", t=TT), axis=AX, op=ALU.add).then_inc(s_mch, 1)
                dve.wait_ge(s_rk, b + 1)
                for i in range(TT):
                    last = dve.tensor_tensor(prod[:, TOPK * i:TOPK * (i + 1), :], chose[:, bass.ds(b * NOTES + TOPK * i, TOPK), :],
                                             pj[:, EXPERTS * i:EXPERTS * (i + 1)].unsqueeze(1).to_broadcast([P, TOPK, EXPERTS]), ALU.mult)
                then(last, b)
                dve.tensor_reduce(msum[:], mch[:].rearrange("p t e -> p e t"), axis=AX, op=ALU.add)
                then(dve.tensor_reduce(rank[:, cols], prod[:], axis=AX, op=ALU.add), b)
                dve.tensor_tensor(macc[:], macc[:], msum[:], ALU.add)
                then(dve.scalar_tensor_tensor(slotf[:], expert[:, cols], float(PLACES), rank[:, cols], ALU.mult, ALU.add), b)
                dve.tensor_copy(tokens[:], tokid[:, bass.ts(b, TT)])
                dve.tensor_copy(slots[:], slotf[:]).then_inc(s_slot, 1)
            assert steps[0] == CHAIN_PER_SEQUENCE, steps

            made = [0]

            def do(ins):
                made[0] += 1
                ins.then_inc(s_md, 1)
                dve.wait_ge(s_md, made[0])

            dve.wait_ge(s_c3, 16 * 3)
            dve.wait_ge(s_m, 1)
            do(dve.tensor_copy(cnt[:], tb[0][0:EXPERTS, 0:P]))
            do(dve.tensor_scalar(cnti[:, 0], cnt[:], float(P - 1), None, ALU.add))
            do(dve.tensor_scalar(cnti[:, 1], cnti[:, 0], P.bit_length() - 1, None, ALU.arith_shift_right))
            dve.tensor_copy(tiles_f[:], cnti[:, 1])
            dve.tensor_copy(tiles_b[:], cnti[:, 1]).then_inc(s_mv, 1)
            dve.wait_ge(s_m, 2)
            dve.tensor_copy(first_b[:], ob[:, 0:EXPERTS])
            do(dve.tensor_copy(first[:], tb[1][0:EXPERTS, 0:P]))
            do(dve.tensor_tensor(after[:], first[:, 0:1], tiles_f[:, 0:1], ALU.add))
            dve.tensor_scalar(begun[:, 0], iota_t[:], first[:, 0:1], None, ALU.is_ge)
            do(dve.tensor_scalar(begun[:, 1], iota_t[:], after[:, 0:1], None, ALU.is_ge))
            do(dve.scalar_tensor_tensor(blockf[:], iota_ee[:], float(PLACES // P), first[:], ALU.mult, ALU.subtract))
            dve.tensor_tensor(owner[:], begun[:, 0], begun[:, 1], ALU.subtract).then_inc(s_mv, 1)
            dve.wait_ge(s_m, 3)
            dve.tensor_tensor(block_i[:], sc[:, 0, 0:1], iota_pt[:, 0:1], ALU.add).then_inc(s_blk, 1)
            dve.tensor_copy(etile[:], sc[:, 1, 0:MOE_TILES])
            for q in range(BATCH):
                cols = slice(NOTES * q, NOTES * (q + 1))
                do(dve.tensor_tensor(prod3[:], chose[:, cols, :], first_b[:, :].unsqueeze(1).to_broadcast([P, NOTES, EXPERTS]), ALU.mult))
                do(dve.tensor_reduce(ybase[:, cols], prod3[:], axis=AX, op=ALU.add))
            do(dve.scalar_tensor_tensor(ybase[:], ybase[:], float(P), rank[:], ALU.mult, ALU.add))
            do(dve.tensor_copy(yslot[:], ybase[:]))
            dve.wait_ge(s_m, 4)
            do(dve.tensor_copy(rowidx[:], sc[:, 2, 0:MOE_TILES]))
            dve.sem_inc(s_map, 1)
            dve.sem_inc(s_h, 2)
            dve.sem_inc(s_y, 2)

            def hidden(n, s):
                dve.wait_ge(s_f1, n + 3)
                dve.wait_ge(s_f2, n + 1)
                dve.tensor_scalar(hT[:, s % 2, :], sc[:, s % 2, 0:P], 0.0, None, ALU.max).then_inc(s_h, 1)

            def result(n, s):
                dve.wait_ge(s_f2, n + 3)
                if not isinstance(n, int) or n >= 4:
                    dve.wait_ge(s_ys[s % 4], (n - s % 4) * 4)
                dve.tensor_copy(ysb[:, s % 4, :], sc[:, 2 + s % 2, 0:DIM]).then_inc(s_y, 1)

            for n in range(5):
                hidden(n, n)
                if n >= 1:
                    result(n - 1, n - 1)
            with dve.Fori(0, (MOE_TILES - 8) // 4) as it:
                for i in range(4):
                    hidden(it * 4 + 5 + i, 5 + i)
                    result(it * 4 + 4 + i, i)
            for n in range(MOE_TILES - 3, MOE_TILES + 1):
                if n < MOE_TILES:
                    hidden(n, n)
                result(n - 1, n - 1)
            dve.sem_inc(s_comb, RING)
            with dve.Fori(0, TILES_IN * TOPK // RING) as it:
                for i in range(RING):
                    dve.wait_ge(s_cg[i], it * 16 + 16)
                    row = x2[:, bass.ds(it * (RING // TOPK) + i // TOPK, 1), :].rearrange("p o d -> p (o d)")
                    dve.scalar_tensor_tensor(row, xin[:, i, :], gate[:, bass.ds(it * RING + i, 1)], row, ALU.mult, ALU.add).then_inc(s_comb, 1)
                    dve.wait_ge(s_comb, it * RING + (i + 1 + RING))

CHAIN_PER_BATCH = 8
CHAIN_PER_SEQUENCE = 16


def constants():
    inv = (1.0 / 10000.0 ** (np.arange(0, DH, 2, dtype=np.float32) / DH)).astype(np.float32)
    ang = np.arange(SEQ, dtype=np.float32)[:, None] * inv[None, :]
    cos, sin = np.cos(ang).T.astype(np.float32), np.sin(ang).T.astype(np.float32)
    bf = np.dtype("bfloat16")
    eye = np.eye(P, dtype=np.float32)
    i = np.arange(P)
    return {
        "cos": np.ascontiguousarray(np.tile(cos, (4, 1))),
        "sin": np.ascontiguousarray(np.concatenate([sin, sin, -sin, -sin])),
        "ident": eye,
        "tri_b": (i[:, None] < i[None, :]).astype(bf),
        "ones_b": np.ones((P, P), bf),
        "tokid": (P * np.arange(TILES_IN)[None, :] + i[:, None]).astype(np.float32),
        "headm": (i[:, None] // DX == np.arange(HEADS // 2)[None, :]).astype(np.float32),
        "iota_e": np.tile(np.arange(EXPERTS, dtype=np.float32), (P, 1)),
        "iota_t": np.tile(np.arange(MOE_TILES, dtype=np.float32), (EXPERTS, 1)),
        "iota_ee": np.tile(np.arange(EXPERTS, dtype=np.float32)[:, None], (1, P)),
        "iota_pt": (P * np.arange(MOE_TILES)[None, :] + i[:, None]).astype(np.float32),
        "ident_b": eye.astype(bf),
        "causal_b": np.where(i[None, :] > i[:, None], np.float32(NEG), np.float32(0)).astype(bf),
    }


def layout(inputs):
    a = {k: np.asarray(v) for k, v in inputs.items()}
    out = dict(constants())
    out["x"] = a["x"]
    w = a["L0_attn_W_qkv"].reshape(KT, P, 3, PAIRS, 2, 2, DH // 2)
    q, k, v = w[:, :, 0], w[:, :, 1], w[:, :, 2]
    perm = lambda z: z.transpose(2, 1, 0, 4, 3, 5).reshape(PAIRS, P, KT, P)
    out["wqkv"] = np.concatenate([perm(q), perm(k), v.transpose(2, 1, 0, 3, 4, 5).reshape(PAIRS, P, KT, P)], axis=3)
    out["wo1"] = a["L0_attn_W_o1"].reshape(PAIRS, P, DIM).transpose(1, 0, 2)
    out["wo2"] = a["L0_attn_W_o2"].reshape(KT, P, DIM).transpose(1, 0, 2)
    out["gamma"] = np.broadcast_to(a["L0_attn_gamma"], (P, DIM))
    lay = lambda w: w.T.reshape(KT, P, -1).transpose(1, 0, 2)
    out["wx"] = np.stack([lay(a["L0_xattn_" + n]) for n in ("Wq", "Wk", "Wv", "Wo")], axis=1)
    out["bqk"] = np.stack([a["L0_xattn_" + n].reshape(KT, P).T for n in ("bq", "bk")], axis=1)
    out["bvo"] = np.stack([np.broadcast_to(a["L0_xattn_" + n], (P, DIM)) for n in ("bv", "bo")], axis=1)
    out["ctxT"] = a["ctx_1024"].reshape(BATCH, SK, KT, P).transpose(0, 3, 2, 1)
    out["mask"] = a["mask_BxSxS2_bk1"].reshape(BATCH, TT, P, SK).transpose(0, 2, 1, 3)
    out["sel_w"] = lay(a["L0_ffn_expert_sel"])
    out["keys"] = a["L0_ffn_keys"].reshape(EXPERTS, KT, P, HID).transpose(2, 0, 1, 3).reshape(P, EXPERTS, KT * HID)
    out["vals"] = a["L0_ffn_values"].transpose(1, 0, 2)
    return {k: np.ascontiguousarray(v) for k, v in out.items()}


def make(nc, arrays):
    t = {}
    for name, arr in arrays.items():
        t[name] = nc.dram_tensor("in_" + name, arr.shape, mybir.dt.from_np(arr.dtype), kind="ExternalInput").ap()
    t["x1"] = nc.dram_tensor("x1", (BATCH, SEQ, DIM), F32, kind="Internal").ap()
    t["x3"] = nc.dram_tensor("x3_rows", (BATCH, SEQ, DIM), F32, kind="Internal").ap()
    t["table"] = nc.dram_tensor("table", (EXPERTS * PLACES, 1), F32, kind="Internal").ap()
    t["yg"] = nc.dram_tensor("yg", (MOE_TILES * P, DIM), F32, kind="Internal").ap()
    t["out"] = nc.dram_tensor("out", (BATCH * SEQ, DIM), F32, kind="ExternalOutput").ap()
    build_program(nc, t)


def kernel(**inputs):
    import concourse.bacc as bacc
    from concourse.bass_utils import run_bass_kernel_spmd

    nc = bacc.Bacc("TRN2", target_bir_lowering=False, num_devices=1)
    arrays = layout(inputs)
    make(nc, arrays)
    result = run_bass_kernel_spmd(nc, [{"in_" + k: v for k, v in arrays.items()}], core_ids=[0])
    return result.results[0]["out"].reshape(BATCH, SEQ, DIM)
```

```python
from contextlib import ExitStack

import numpy as np

import concourse.bass as bass
from concourse import mybir

F32 = mybir.dt.float32
F32R = mybir.dt.float32r
BF16 = mybir.dt.bfloat16
U32 = mybir.dt.uint32
I32 = mybir.dt.int32
U8 = mybir.dt.uint8
ALU = mybir.AluOpType
ACT = mybir.ActivationFunctionType
AX = mybir.AxisListType.X

P = 128
BATCH, SEQ, DIM = 2, 1024, 256
HEADS, DH = 16, 64
PAIRS = HEADS // 2
KT = DIM // P
TT = SEQ // P
HALF = 512
EPS = 1e-5
SK = 77
NEG = -3.0e38

DX = DIM // HEADS
CHUNK = 4
SXBUFS = 4
UX = 2 * TT
HEADS_OUT_AT = {9: (0, 0), 11: (0, 1), 17: (1, 0)}
NORMALISED_AT = {10: 0, 12: 1, 17: 2}


def last_unit(half, m):
    return 2 * (CHUNK * (half + 1) - 1) + m


TILES_IN = BATCH * TT
EXPERTS, TOPK = 64, 4
NOTES = TT * TOPK
HID = 128
PLACES = BATCH * SEQ
MOE_TILES = BATCH * SEQ * TOPK // P + EXPERTS
RING = 8

UNITS = 2 * TT
PROBS = 3
LAG = 2
STEPS = UNITS + LAG
PROJ_AT = {1: 0, 3: 1, 5: 2, 7: 3, 11: 4, 15: 5}
XT_AT = {4: 0, 5: 1, 6: 2, 7: 3}
FIRST_PROJ_AT = {8: 0, 10: 1, 12: 2, 14: 3, 16: 4, 17: 5}
GROUP_END = {UNITS // 2 - 1 + LAG: 0, STEPS - 1: 1}
AHEAD = UNITS // 2 + LAG


def unit(n):
    return n // TT, n // 2, n % 2


def score_chunks(qi):
    w = (qi + 1) * P
    return [(c, max(256, min(HALF, w - c))) for c in range(0, w, HALF)]


def transpose_chunks():
    out, seen = [], {"dve": 0, "act": 0}
    for g in range(2):
        for n in range(g * TT, (g + 1) * TT):
            qi = unit(n)[1]
            for c in range(0, qi + 1, 4):
                eng = "dve" if len(out) % 2 == 0 else "act"
                seen[eng] += 1
                out.append((n, c, min(4, qi + 1 - c), eng, seen[eng]))
        seen["act"] += 1
        out.append(("sums", g, 4, "act", seen["act"]))
    return out, seen


CHUNKS, EVACS = transpose_chunks()


def build_program(nc, t):
    ctx = ExitStack()
    with ctx:
        def sem(name):
            return ctx.enter_context(nc.semaphore(name))

        def sb_in(c, name, shape, dt=F32):
            return c.enter_context(nc.sbuf_tensor(name, shape, dt))

        ps = [ctx.enter_context(nc.psum_tensor(f"bank{i}", [P, HALF], F32)) for i in range(4, 8)]
        sc = ctx.enter_context(nc.psum_tensor("scores", [P, 4, HALF], F32))
        tb, ob, pj = ps[0:2], ps[2], ps[3]

        def proj_bank(j, first):
            return pj[:] if first or j in (0, 3) else sc[:, 2 * j - 1, :]


        ident = sb_in(ctx, "ident", [P, P])
        ident_b = sb_in(ctx, "ident_b", [P, P], BF16)
        causal_b = sb_in(ctx, "causal_b", [P, P], BF16)
        stats = sb_in(ctx, "stats", [P, TT, 6])
        mv = sb_in(ctx, "mv", [P, TT, 2])
        veps = sb_in(ctx, "veps", [P, TT])
        std = sb_in(ctx, "std", [P, TT])
        rstd = sb_in(ctx, "rstd", [P, TT])

        m1 = ExitStack()
        stk = sb_in(m1, "stk", [P, 2, 2, 3, SEQ], F32R)
        qk_hi = sb_in(m1, "qk_hi", [P, 2, SEQ], F32R)
        qk_lo = sb_in(m1, "qk_lo", [P, 2, SEQ], F32R)
        v = sb_in(m1, "v", [P, 2, TT, P])
        wbuf = sb_in(m1, "wbuf", [P, 2, KT, 3 * P])
        pt = sb_in(m1, "pt", [P, 2, TT, HALF])
        probs = sb_in(m1, "probs", [P, PROBS, SEQ])
        oT = sb_in(m1, "oT", [P, PAIRS, SEQ])
        xT = sb_in(m1, "xT", [P, KT, SEQ])
        cos_t = sb_in(m1, "cos_t", [P, SEQ])
        sin_t = sb_in(m1, "sin_t", [P, SEQ])
        t12 = sb_in(m1, "t12", [P, 4, HALF])
        rot = sb_in(m1, "rot", [P, 2, HALF])
        rs = sb_in(m1, "rs", [P, UNITS])
        rsi = sb_in(m1, "rsi", [P, TT])
        rinv = sb_in(m1, "rinv", [P, TT, DH])
        nmax = sb_in(m1, "nmax", [P, UNITS])
        inv_b = sb_in(m1, "inv_b", [P, HALF])
        xb = sb_in(m1, "xb", [P, TT, DIM])
        wo1 = sb_in(m1, "wo1", [P, PAIRS, DIM])
        wo2 = sb_in(m1, "wo2", [P, KT, DIM])
        gamma = sb_in(m1, "gamma", [P, DIM])
        m1.close()
        t1, t2 = t12[:, 0:2], t12[:, 2:4]
        xn = t12[:, :, :].rearrange("p a b -> p (a b)").rearrange("p (t d) -> p t d", t=TT)
        on = pt[:, 1, 4:8, :].rearrange("p a b -> p (a b)").rearrange("p (t d) -> p t d", t=TT)
        h1T = pt[:, 0, 4:8, :].rearrange("p a b -> p (a b)").rearrange("p (m s) -> p m s", m=KT)

        ctx2 = ExitStack()
        s_ident = sem("s_ident"); s_angle = sem("s_angle"); s_wo = sem("s_wo")
        s_apart = sem("s_apart")
        s_x = sem("s_x")
        s_xr = sem("s_xr")
        s_w = [sem("s_w0"), sem("s_w1")]
        s_wq = sem("s_wq")
        s_var = sem("s_var"); s_std = sem("s_std")
        s_lnv = sem("s_lnv")
        s_xn = sem("s_xn")
        s_xt = sem("s_xt")
        s_xtv = sem("s_xtv"); s_xta = sem("s_xta")
        s_pj = sem("s_pj")
        s_rope = sem("s_rope")
        s_rot = sem("s_rot")
        s_hi = sem("s_hi"); s_lo = sem("s_lo")
        s_v = sem("s_v")
        s_stk = [sem("s_stk0"), sem("s_stk1")]
        s_s = sem("s_s"); s_mx = sem("s_mx"); s_exp = sem("s_exp")
        s_t = sem("s_t")
        s_ev = {"dve": sem("s_evv"), "act": sem("s_eva")}
        s_rsi = sem("s_rsi"); s_rinv = sem("s_rinv"); s_pv = sem("s_pv"); s_ot = sem("s_ot")
        s_h1 = sem("s_h1"); s_h1a = sem("s_h1a"); s_o2 = sem("s_o2")
        s_x1 = sem("s_x1"); s_st = sem("s_st")

        x1c = sb_in(ctx2, "x1c", [P, TT, DIM])
        maskc = sb_in(ctx2, "maskc", [P, TT, SK], U8)
        wx = sb_in(ctx2, "wx", [P, 4, KT, DIM])
        sel_w = sb_in(ctx2, "sel_w", [P, KT, EXPERTS])
        bqk = sb_in(ctx2, "bqk", [P, 2, KT])
        bvo = sb_in(ctx2, "bvo", [P, 2, DIM])
        ctxT = sb_in(ctx2, "ctxT", [P, KT, SK])
        headm = sb_in(ctx2, "headm", [P, HEADS // 2])
        x3 = sb_in(ctx2, "x3", [P, TT, DIM])
        vz = sb_in(ctx2, "vz", [SK, HEADS, 2 * DX])
        onez = sb_in(ctx2, "onez", [SK, 2, 2 * DX])
        macc = sb_in(ctx2, "macc", [P, EXPERTS], BF16)
        tri_b = sb_in(ctx2, "tri_b", [P, P], BF16)
        ones_b = sb_in(ctx2, "ones_b", [P, P], BF16)
        iota_e = sb_in(ctx2, "iota_e", [P, EXPERTS])
        tokid = sb_in(ctx2, "tokid", [P, TILES_IN])
        x2 = sb_in(ctx2, "x2", [P, TILES_IN, DIM])
        keys = sb_in(ctx2, "keys", [P, EXPERTS, KT * HID])
        chose = sb_in(ctx2, "chose", [P, TILES_IN * TOPK, EXPERTS], BF16)
        expert = sb_in(ctx2, "expert", [P, TILES_IN * TOPK])
        rank = sb_in(ctx2, "rank", [P, TILES_IN * TOPK])
        gate = sb_in(ctx2, "gate", [P, TILES_IN * TOPK])
        rowidx = sb_in(ctx2, "rowidx", [P, MOE_TILES], U32)
        etile = sb_in(ctx2, "etile", [P, MOE_TILES], I32)
        yslot = sb_in(ctx2, "yslot", [P, TILES_IN * TOPK], U32)
        slots = sb_in(ctx2, "slots", [P, NOTES], U32)
        tokens = sb_in(ctx2, "tokens", [P, TT])
        m2 = ExitStack()
        mbias = sb_in(m2, "mbias", [P, TT, SK], BF16)
        xTc = sb_in(m2, "xTc", [P, KT, SEQ])
        qT = sb_in(m2, "qT", [P, KT, SEQ])
        sx = sb_in(m2, "sx", [P, SXBUFS, HEADS // 2, SK])
        mx = sb_in(m2, "mx", [P, 2, HEADS // 2])
        ptx = sb_in(m2, "ptx", [P, HEADS, HALF])
        kT = sb_in(m2, "kT", [P, KT, SK])
        kblk = sb_in(m2, "kblk", [P, KT, HEADS // 2, SK])
        itotal = sb_in(m2, "itotal", [P, 2, HALF])
        el = sb_in(m2, "el", [P, TT, EXPERTS])
        sel = sb_in(m2, "sel", [P, TT, EXPERTS])
        top = sb_in(m2, "top", [P, TT, 8])
        topi = sb_in(m2, "topi", [P, TT, 8], U32)
        mch = sb_in(m2, "mch", [P, TT, EXPERTS], BF16)
        msum = sb_in(m2, "msum", [P, EXPERTS])
        slotf = sb_in(m2, "slotf", [P, NOTES])
        zeros = sb_in(m2, "zeros", [P, EXPERTS * PLACES // P])
        m2.close()
        q_bank = [ob, pj, tb[0], tb[1]]
        oTc = xTc
        prod = ptx[:, 0:NOTES * EXPERTS // HALF, :].rearrange("p a b -> p (a b)").rearrange("p (n e) -> p n e", n=NOTES)
        m3 = ExitStack()
        vals = sb_in(m3, "vals", [P, EXPERTS, DIM])
        prod3 = x1c[:, :, :].rearrange("p t d -> p (t d)").rearrange("p (n e) -> p n e", n=NOTES)
        iota_t = sb_in(m3, "iota_t", [EXPERTS, MOE_TILES])
        iota_pt = sb_in(m3, "iota_pt", [P, MOE_TILES])
        iota_ee = sb_in(m3, "iota_ee", [EXPERTS, P])
        cnt = sb_in(m3, "cnt", [EXPERTS, P])
        cnti = sb_in(m3, "cnti", [EXPERTS, 2, P], I32)
        tiles_f = sb_in(m3, "tiles_f", [EXPERTS, P])
        tiles_b = sb_in(m3, "tiles_b", [EXPERTS, P], BF16)
        first = sb_in(m3, "first", [EXPERTS, P])
        first_b = sb_in(m3, "first_b", [P, EXPERTS])
        after = sb_in(m3, "after", [EXPERTS, 1])
        begun = sb_in(m3, "begun", [EXPERTS, 2, MOE_TILES])
        owner = sb_in(m3, "owner", [EXPERTS, MOE_TILES])
        blockf = sb_in(m3, "blockf", [EXPERTS, P])
        block_i = sb_in(m3, "block_i", [MOE_TILES, 1], U32)
        table_t = sb_in(m3, "table_t", [MOE_TILES, P])
        ybase = sb_in(m3, "ybase", [P, TILES_IN * TOPK])
        idxb = sb_in(m3, "idxb", [P, 2, RING], U32)
        xin = x3
        xgT = sb_in(m3, "xgT", [P, 2, KT * P])
        ksel = sb_in(m3, "ksel", [P, 4, KT * HID])
        vsel = sb_in(m3, "vsel", [P, 2, DIM])
        hT = sb_in(m3, "hT", [P, 2, P])
        ysb = sb_in(m3, "ysb", [P, 4, DIM])
        m3.close()
        ctx2.close()

        s_c2 = sem("s_c2")
        s_zr = sem("s_zr"); s_zero = sem("s_zero")
        s_keys = sem("s_keys"); s_vals = sem("s_vals")
        s_x1c = sem("s_x1c"); s_mask = sem("s_mask"); s_ctx = sem("s_ctx")
        s_cd = sem("s_cd")
        s_kv = sem("s_kv"); s_kvd = sem("s_kvd")
        s_var2 = sem("s_var2"); s_std2 = sem("s_std2"); s_ln = sem("s_ln")
        s_tr2 = sem("s_tr2"); s_trv = sem("s_trv"); s_tra = sem("s_tra")
        s_q2 = sem("s_q2"); s_qd = sem("s_qd")
        s_sx = sem("s_sx"); s_mxx = sem("s_mxx"); s_sub = sem("s_sub"); s_ex = sem("s_ex")
        s_px = sem("s_px"); s_pxv = sem("s_pxv"); s_pxa = sem("s_pxa")
        s_ov = sem("s_ov"); s_tot = sem("s_tot"); s_ovd = sem("s_ovd")
        s_bo = sem("s_bo"); s_wox = sem("s_wox"); s_x2 = sem("s_x2")
        s_lg = sem("s_lg"); s_el = sem("s_el")
        s_mch = sem("s_mch"); s_rk = sem("s_rk"); s_slot = sem("s_slot")
        s_x3d = sem("s_x3d"); s_scat = sem("s_scat")
        s_c3 = sem("s_c3")
        s_md = sem("s_md")
        s_m = sem("s_m"); s_mv = sem("s_mv"); s_map = sem("s_map")
        s_blk = sem("s_blk"); s_tab = sem("s_tab")
        s_idx = sem("s_idx"); s_g = [sem(f"s_g{i}") for i in range(RING)]
        s_t3 = sem("s_t3"); s_xg = sem("s_xg")
        s_f1 = sem("s_f1"); s_h = sem("s_h"); s_f2 = sem("s_f2"); s_y = sem("s_y")
        s_ys = [sem(f"s_ys{i}") for i in range(4)]
        s_cg = [sem(f"s_cg{i}") for i in range(RING)]
        s_comb = sem("s_comb"); s_out = sem("s_out")

        block = ctx.enter_context(nc.Block())

        def apart(eng):
            eng.sem_inc(s_apart, 1)

        def pairs(eng, b, body):
            again = b < BATCH - 1
            with eng.Fori(0, PAIRS // 2 - 1) as it:
                for u in range(2):
                    body(it * 2 + (b * PAIRS + u), it * 2 + u, it * 2 + (u + 2), u, it + b * (PAIRS // 2), True, True, False)
            for u in range(2):
                pair = PAIRS - 2 + u
                body(b * PAIRS + pair, pair, u, u, b * (PAIRS // 2) + PAIRS // 2 - 1, u == 0 or again, again, u == 1)

        def last_ln(b, h):
            return BATCH + 2 * b + h + 1

        def evac_chunks(eng, name, PB, what, copy):
            for idx, (m, c, tiles, who, _) in enumerate(CHUNKS):
                key = (m, c) if m == "sums" else m
                if who != name or key != what:
                    continue
                eng.wait_ge(s_t, PB * len(CHUNKS) + idx + 1)
                if m == "sums":
                    copy(inv_b[:], tb[idx % 2][:]).then_inc(s_ev[name], 1)
                    continue
                g, qi, hh = unit(m)
                if g == 1:
                    eng.wait_ge(s_pv, PB * 2 + 1)
                q0 = (qi - 4 * g) * P
                copy(pt[:, hh, c:c + tiles, q0:q0 + P],
                     tb[idx % 2][:, 0:P * tiles].rearrange("p (k q) -> p k q", k=tiles)).then_inc(s_ev[name], 1)

        def taken(eng, name, b, u):
            i, m = u // 2, u % 2
            j = 0 if name == "dve" else 1
            if i == CHUNK:
                eng.wait_ge(s_ov, b * 4 + m + 1)
            eng.wait_ge(s_px, b * (2 * UX) + 2 * u + j + 1)
            at = P * (i % CHUNK)
            dst = ptx[0:SK, 8 * m + 4 * j:8 * m + 4 * j + 4, at:at + P]
            src = tb[j][0:SK, :].rearrange("s (h q) -> s h q", h=4)
            if name == "dve":
                eng.tensor_copy(dst, src).then_inc(s_pxv, 1)
            else:
                eng.activation(dst, src, ACT.Copy).then_inc(s_pxa, 1)

        @block.sync
        def _(sp):
            def load(pairs, signal):
                for dst, src in pairs:
                    sp.dma_start(dst, src).then_inc(signal, 16)

            def load_w(pair, u):
                sp.dma_start(wbuf[:, u], t["wqkv"][bass.ds(pair, 1)].rearrange("o p k n -> p (o k) n")).then_inc(s_w[u], 16)

            def stack(PT, u):
                for which in range(2):
                    sp.wait_ge(s_lo, PT * 4 + 2 * (which + 1))
                    for hh in range(2):
                        for part in range(2):
                            rows = slice(64 * part + 32 * hh, 64 * part + 32 * hh + 32)
                            for buf, hl in ((qk_hi, 0), (qk_lo, 1)):
                                src = buf[rows, which, :].bitcast(F32)
                                if which == 0:
                                    at = 64 * hl + 32 * part
                                    sp.dma_start(stk[at:at + 32, u, hh, 0, :].bitcast(F32), src).then_inc(s_stk[u], 16)
                                else:
                                    for dup in range(2):
                                        at = 64 * dup + 32 * part
                                        sp.dma_start(stk[at:at + 32, u, hh, 1 + hl, :].bitcast(F32), src).then_inc(s_stk[u], 16)

            def load_sequence(b):
                load([(x1c[:], t["x1"][b].rearrange("(t p) d -> p t d", p=P))], s_x1c)
                load([(maskc[:], t["mask"][b])], s_mask)
                load([(ctxT[:], t["ctxT"][b])], s_ctx)

            def x_of(b):
                return t["x"][b].rearrange("(t p) d -> p t d", p=P)

            load([(xn, x_of(0))], s_x)
            load([(ident[:], t["ident"])], s_ident)
            load_w(0, 0)
            load([(cos_t[:], t["cos"]), (sin_t[:], t["sin"])], s_angle)
            load([(ident_b[:], t["ident_b"]), (causal_b[:], t["causal_b"])], s_ident)
            load_w(1, 1)
            load([(xb[:], x_of(0))], s_xr)
            stack(0, 0)
            load([(wo1[:], t["wo1"]), (wo2[:], t["wo2"]), (gamma[:], t["gamma"])], s_wo)
            for b in range(BATCH):
                def body(PB, pair, pair2, u, use, nxt, nxt2, first):
                    if nxt2:
                        sp.wait_ge(s_pj, (PB + 1) * 6)
                        load_w(pair2, u)
                    if nxt and first:
                        sp.wait_ge(s_rot, PB * 4 + 4)
                        load([(xn, x_of(b + 1))], s_x)
                    if nxt:
                        stack(PB + 1, 1 - u)
                pairs(sp, b, body)
                if b == BATCH - 1:
                    sp.wait_ge(s_exp, BATCH * PAIRS * UNITS)
                    apart(sp)
                    load([(wx[:], t["wx"]), (sel_w[:], t["sel_w"]), (bqk[:], t["bqk"]), (bvo[:], t["bvo"]),
                          (headm[:], t["headm"]), (tri_b[:], t["tri_b"]), (ones_b[:], t["ones_b"]), (iota_e[:], t["iota_e"]),
                          (tokid[:], t["tokid"])], s_c2)
                    load_sequence(0)
                sp.wait_ge(s_x1, b + 1)
                sp.dma_start(t["x1"][b].rearrange("(t p) d -> p t d", p=P), xb[:]).then_inc(s_st, 16)
                sp.wait_ge(s_st, (b + 1) * 16)
                apart(sp)
                if b < BATCH - 1:
                    load([(xb[:], x_of(b + 1))], s_xr)

            sp.wait_ge(s_zr, 1)
            sp.dma_start(t["table"].rearrange("(p n) o -> p (n o)", p=P), zeros[:]).then_inc(s_zero, 16)
            for b in range(BATCH):
                load([(keys[:, EXPERTS // BATCH * b:EXPERTS // BATCH * (b + 1), :],
                       t["keys"][:, EXPERTS // BATCH * b:EXPERTS // BATCH * (b + 1), :])], s_keys)
                if b >= 1:
                    sp.wait_ge(s_x2, b)
                    load_sequence(b)
                sp.wait_ge(s_ln, b * 2 + 2)
                sp.dma_start(t["x3"][b].rearrange("(t p) d -> p t d", p=P), x3[:]).then_inc(s_x3d, 16)
                sp.wait_ge(s_x3d, b * 16 + 16)
                apart(sp)
            sp.wait_ge(s_slot, BATCH + 1)
            sp.wait_ge(s_x3d, 16 * BATCH)
            for dst, src in ((iota_t[:], t["iota_t"]), (iota_pt[:], t["iota_pt"]), (iota_ee[:], t["iota_ee"])):
                sp.dma_start(dst, src).then_inc(s_c3, 16)
            sp.dma_start(vals[:], t["vals"]).then_inc(s_vals, 16)
            with sp.Fori(0, MOE_TILES // 4) as it:
                for i in range(4):
                    sp.wait_ge(s_y, it * 4 + (i + 1))
                    sp.dma_start(t["yg"][bass.ts(it * 4 + i, P), :], ysb[:, i, :]).then_inc(s_ys[i], 16)
            with sp.Fori(0, TILES_IN) as tt:
                sp.wait_ge(s_comb, tt * TOPK + (TOPK + RING))
                sp.dma_start(t["out"][bass.ts(tt, P), :], x2[:, bass.ds(tt, 1), :].rearrange("p o d -> p (o d)")).then_inc(s_out, 16)
            sp.wait_ge(s_out, 16 * TILES_IN)
            for i in range(4):
                sp.wait_ge(s_ys[i], 16 * (MOE_TILES // 4))
            sp.wait_ge(s_st, 16 * BATCH)

        @block.gpsimd
        def _(pool):
            def scale_wq(PT, u, use):
                pool.wait_ge(s_w[u], (use + 1) * 16)
                apart(pool)
                pool.tensor_scalar(wbuf[:, u, :, 0:P], wbuf[:, u, :, 0:P], DH ** -0.5, None, ALU.mult).then_inc(s_wq, 1)

            def rotate(PT):
                for j in range(4):
                    pool.wait_ge(s_rope, PT * 4 + j + 1)
                    if j >= 2:
                        pool.wait_ge(s_hi, PT * 4 + j - 1)
                    pool.tensor_tensor(rot[:, j % 2], t1[:, j % 2], t2[:, j % 2], ALU.add).then_inc(s_rot, 1)
                    pool.wait_ge(s_rot, PT * 4 + j + 1)
                    pool.wait_ge(s_hi, PT * 4 + j + 1)
                    dst = slice(HALF * (j % 2), HALF * (j % 2 + 1))
                    pool.tensor_tensor(qk_lo[:, j // 2, dst], rot[:, j % 2], qk_hi[:, j // 2, dst].bitcast(F32),
                                       ALU.subtract).then_inc(s_lo, 1)

            for u in range(2):
                scale_wq(u, u, 0)
            rotate(0)
            for b in range(BATCH):
                def body(PB, pair, pair2, u, use, nxt, nxt2, first):
                    if nxt:
                        rotate(PB + 1)
                    if nxt2:
                        scale_wq(PB + 2, u, use + 1)
                pairs(pool, b, body)

            pool.wait_ge(s_st, 16 * BATCH)
            pool.memset(zeros[:], 0.0).then_inc(s_zr, 1)
            with pool.Fori(0, BATCH) as b:
                pool.wait_ge(s_ln, b * 2 + 1)
                apart(pool)
                pool.tensor_tensor(x1c[:], x1c[:], bvo[:, 1, :].unsqueeze(1).to_broadcast([P, TT, DIM]), ALU.add).then_inc(s_bo, 1)
                pool.wait_ge(s_zero, 16)
                pool.wait_ge(s_slot, b + 2)
                apart(pool)
                for i in range(NOTES):
                    pool.indirect_dma_start(t["table"], bass.IndirectOffsetOnAxis(ap=slots[:, i:i + 1], axis=0),
                                            tokens[:, i // TOPK:i // TOPK + 1], None).then_inc(s_scat, 16)
                pool.wait_ge(s_scat, b * (16 * NOTES) + 16 * NOTES)
            pool.wait_ge(s_scat, 16 * TILES_IN * TOPK)
            pool.wait_ge(s_x3d, 16 * BATCH)
            pool.wait_ge(s_blk, 1)
            pool.indirect_dma_start(table_t[:], None, t["table"].rearrange("(n p) o -> n (p o)", p=P),
                                    bass.IndirectOffsetOnAxis(ap=block_i[:], axis=0)).then_inc(s_tab, 16)
            pool.wait_ge(s_map, 1)

            def gather_ring(n, u, indices, src, free, arrived):
                pool.tensor_copy(idxb[:, u], indices[:, bass.ts(n, RING)]).then_inc(s_idx, 1)
                pool.wait_ge(s_idx, n + 1 + (MOE_TILES // RING if src is t["yg"] else 0))
                for i in range(RING):
                    if i % 4 == 0:
                        pool.wait_ge(free, n * RING + i + 4)
                        apart(pool)
                    pool.indirect_dma_start(xin[:, i, :], None, src, bass.IndirectOffsetOnAxis(ap=idxb[:, u, i:i + 1], axis=0)).then_inc(arrived[i], 16)

            with pool.Fori(0, MOE_TILES // (2 * RING)) as it:
                for u in range(2):
                    gather_ring(it * 2 + u, u, rowidx, t["x3"].rearrange("c n d -> (c n) d"), s_t3, s_g)
            for i in range(4):
                pool.wait_ge(s_ys[i], 16 * (MOE_TILES // 4))
            with pool.Fori(0, TILES_IN * TOPK // (2 * RING)) as it:
                for u in range(2):
                    gather_ring(it * 2 + u, u, yslot, t["yg"], s_comb, s_cg)

        @block.tensor
        def _(pe):
            def proj(PT, u, j, first):
                if j == 0:
                    pe.wait_ge(s_wq, PT + 1)
                    if first:
                        pe.wait_ge(s_xta, PT // PAIRS * 2 + 2)
                        pe.wait_ge(s_xtv, PT // PAIRS * 2 + 2)
                    else:
                        pe.wait_ge(s_v, PT * 2)
                elif first and j < 5:
                    pe.wait_ge(s_rope, PT * 4 + j)
                elif j in (3, 4):
                    pe.wait_ge(s_rope, PT * 4 + (1 if j == 3 else 4))
                elif j == 5:
                    pe.wait_ge(s_v, PT * 2 + 1)
                if j < 4:
                    for k in range(KT):
                        last = pe.matmul(proj_bank(j, first), wbuf[:, u, k, (j // 2) * P:(j // 2 + 1) * P],
                                         xT[:, k, HALF * (j % 2):HALF * (j % 2 + 1)], start=k == 0, stop=k == KT - 1)
                else:
                    for i in range(4):
                        tt = 4 * (j - 4) + i
                        for k in range(KT):
                            last = pe.matmul(pj[:, P * i:P * (i + 1)], xT[:, k, P * tt:P * (tt + 1)],
                                             wbuf[:, u, k, 2 * P:3 * P], start=k == 0, stop=k == KT - 1)
                last.then_inc(s_pj, 1)

            def scores(PB, u, n):
                _, qi, hh = unit(n)
                if n >= 2:
                    pe.wait_ge(s_exp, PB * UNITS + n - 1)
                q = stk[:, u, hh, 0, qi * P:(qi + 1) * P]
                for c, w in score_chunks(qi):
                    out = sc[:, 2 * (n % 2) + c // HALF, 0:w]
                    diag = c <= qi * P < c + HALF
                    pe.matmul(out, q, stk[:, u, hh, 1, c:c + w], start=True, stop=False)
                    last = pe.matmul(out, q, stk[:, u, hh, 2, c:c + w], start=False, stop=not diag)
                    if diag:
                        o = qi * P - c
                        last = pe.matmul(sc[:, 2 * (n % 2) + c // HALF, o:o + P], ident_b[:], causal_b[:],
                                         start=False, stop=True)
                last.then_inc(s_s, 1)

            def reuse(PB, idx):
                if idx >= 2:
                    eng, count = CHUNKS[idx - 2][3:]
                    pe.wait_ge(s_ev[eng], PB * EVACS[eng] + count)

            def transposes(PB, n):
                pe.wait_ge(s_exp, PB * UNITS + n + 1)
                for idx, (m, c, tiles, _, _) in enumerate(CHUNKS):
                    if m == n:
                        reuse(PB, idx)
                        for i in range(tiles):
                            last = pe.transpose(tb[idx % 2][:, P * i:P * (i + 1)],
                                                probs[:, n % PROBS, (c + i) * P:(c + i + 1) * P], ident[:])
                        last.then_inc(s_t, 1)

            def finish_group(PB, u, g):
                idx = next(i for i, ch in enumerate(CHUNKS) if ch[0] == "sums" and ch[1] == g)
                reuse(PB, idx)
                pe.wait_ge(s_rinv, PB * 2 + g + 1)
                for i in range(4):
                    last = pe.transpose(tb[idx % 2][:, P * i:P * (i + 1)],
                                        rinv[:, 2 * i:2 * i + 2, :].rearrange("p h d -> p (h d)"), ident[:])
                last.then_inc(s_t, 1)
                if g == 0:
                    scores(PB, u, AHEAD + 1)
                for eng in ("dve", "act"):
                    pe.wait_ge(s_ev[eng], PB * EVACS[eng] + max(c[4] for c in CHUNKS[:idx] if c[3] == eng))
                pe.wait_ge(s_v, (PB + 1) * 2)
                tiles = 4 * (g + 1)
                for kt in range(tiles):
                    q0 = max(0, kt - 4 * g) * P
                    for hh in range(2):
                        last = pe.matmul(ob[DH * hh:DH * (hh + 1), q0:HALF], v[:, u, kt, DH * hh:DH * (hh + 1)],
                                         pt[:, hh, kt, q0:HALF], start=kt == 0, stop=kt == tiles - 1)
                last.then_inc(s_pv, 1)

            def x_transposes(b, c, bank):
                k, half = c // 2, c % 2
                for i in range(4):
                    last = pe.transpose(bank[:, P * i:P * (i + 1)], xn[:, 4 * half + i, P * k:P * (k + 1)], ident[:])
                last.then_inc(s_xt, 1)

            pe.wait_ge(s_ident, 16 * 3)
            pe.wait_ge(s_xn, 1)
            for c in range(4):
                x_transposes(0, c, sc[:, c, :])
            for j in range(6):
                proj(0, 0, j, True)
            def first_scores(PB, u, use):
                pe.wait_ge(s_stk[u], (use + 1) * (24 * 16))
                for n in range(2):
                    scores(PB, u, n)

            for b in range(BATCH):
                def body(PB, pair, pair2, u, use, nxt, nxt2, first):
                    at = FIRST_PROJ_AT if first else PROJ_AT
                    for k in range(STEPS):
                        if k in (UNITS // 2, UNITS // 2 + 1) and nxt and not first:
                            pe.wait_ge(s_rope, (PB + 1) * 4 + (k - UNITS // 2 + 2))
                        if 2 <= k < UNITS and k not in (AHEAD, AHEAD + 1):
                            scores(PB, u, k)
                        late = k in GROUP_END
                        if late:
                            transposes(PB, k - LAG)
                        if nxt and first and k in XT_AT:
                            c = XT_AT[k]
                            if c == 0:
                                pe.wait_ge(s_xn, b + 2)
                                pe.wait_ge(s_v, (PB + 1) * 2)
                            else:
                                pe.wait_ge(s_xtv if c <= 2 else s_xta, 2 * (b + 1) + (c if c <= 2 else c - 2))
                            x_transposes(b + 1, c, pj)
                        if nxt and k in at:
                            proj(PB + 1, 1 - u, at[k], first)
                        if k >= LAG and not late:
                            transposes(PB, k - LAG)
                        if k == AHEAD - 1:
                            scores(PB, u, AHEAD)
                        if k == STEPS - 1 and nxt and not first:
                            first_scores(PB + 1, 1 - u, use + u)
                        if late:
                            finish_group(PB, u, GROUP_END[k])
                first_scores(b * PAIRS, 0, b * (PAIRS // 2))
                pairs(pe, b, body)
                pe.wait_ge(s_wo, 16 * 3)
                if b < BATCH - 1:
                    pe.wait_ge(s_v, (b + 1) * (2 * PAIRS) + 2)
                pe.wait_ge(s_ot, (b + 1) * (2 * PAIRS))

                def hidden_T(c, m):
                    for k in range(PAIRS):
                        last = pe.matmul(sc[:, 2 * c + m, :], wo1[:, k, P * m:P * (m + 1)],
                                         oT[:, k, HALF * c:HALF * (c + 1)], start=k == 0, stop=k == PAIRS - 1)
                    last.then_inc(s_h1, 1)

                def outputs(c):
                    pe.wait_ge(s_h1a, b * 4 + 2 * (c + 1))
                    for i in range(4 * c, 4 * c + 4):
                        for k in range(KT):
                            last = pe.matmul(ps[i // 2][:, DIM * (i % 2):DIM * (i % 2 + 1)], h1T[:, k, P * i:P * (i + 1)],
                                             wo2[:, k, :], start=k == 0, stop=k == KT - 1)
                    last.then_inc(s_o2, 1)

                hidden_T(0, 0)
                hidden_T(0, 1)
                hidden_T(1, 0)
                outputs(0)
                hidden_T(1, 1)
                outputs(1)
                if b < BATCH - 1:
                    pe.wait_ge(s_x1, b + 1)

            pe.wait_ge(s_c2, 16 * 9)

            def transpose_sequence(b, k):
                pe.wait_ge(s_ln, b * 2 + k)
                for h in range(2):
                    for kt in range(KT):
                        for i in range(CHUNK):
                            last = pe.transpose(sc[:, 2 * h + kt, P * i:P * (i + 1)],
                                                x3[:, CHUNK * h + i, P * kt:P * (kt + 1)], ident[:])
                        last.then_inc(s_tr2, 1)
                pe.wait_ge(s_trv, b * 4 + 2 * k)
                pe.wait_ge(s_tra, b * 4 + 2 * k)

            with pe.Fori(0, BATCH) as b:
                pe.wait_ge(s_slot, b + 1)
                pe.wait_ge(s_ctx, b * 16 + 16)
                for m in range(KT):
                    for k in range(KT):
                        pe.matmul(tb[0][:, SK * m:SK * (m + 1)], wx[:, 1, k, P * m:P * (m + 1)], ctxT[:, k, :], start=k == 0, stop=k == KT - 1)
                for k in range(KT):
                    last = pe.matmul(tb[1][0:SK, 0:DIM], ctxT[:, k, :], wx[:, 2, k, :], start=k == 0, stop=k == KT - 1)
                last.then_inc(s_kv, 1)
                transpose_sequence(b, 1)
                for h in range(2):
                    if h == 1:
                        pe.wait_ge(s_kvd, b + 1)
                    for m in range(KT):
                        for k in range(KT):
                            last = pe.matmul(q_bank[2 * h + m][:], wx[:, 0, k, P * m:P * (m + 1)], xTc[:, k, HALF * h:HALF * (h + 1)],
                                             start=k == 0, stop=k == KT - 1)
                        last.then_inc(s_q2, 1)
                pe.wait_ge(s_qd, b * 4 + 4)

                def head_scores(u):
                    i, m = u // 2, u % 2
                    if u >= 2:
                        pe.wait_ge(s_sub, b * UX + u - 1)
                    for j in range(2):
                        out = sc[:, 2 * m + j, 0:4 * SK]
                        pe.matmul(out, qT[:, m, P * i:P * (i + 1)],
                                  kblk[:, m, 4 * j:4 * j + 4, :].rearrange("p h s -> p (h s)"), start=True, stop=False)
                        last = pe.matmul(out, ident_b[:], mbias[:, i, :].unsqueeze(1).to_broadcast([P, 4, SK]),
                                         start=False, stop=True)
                    last.then_inc(s_sx, 1)

                def probs_T(u):
                    pe.wait_ge(s_ex, b * UX + u + 1)
                    for j in range(2):
                        if u >= 1:
                            pe.wait_ge(s_pxa if j else s_pxv, b * UX + u)
                        for h in range(4):
                            last = pe.transpose(tb[j][0:SK, P * h:P * (h + 1)], sx[:, u % SXBUFS, 4 * j + h, :], ident[:])
                        last.then_inc(s_px, 1)

                def head_out(h, m, out, total):
                    pe.wait_ge(s_pxv, b * UX + last_unit(h, m) + 1)
                    pe.wait_ge(s_pxa, b * UX + last_unit(h, m) + 1)
                    if (h, m) in ((0, 1), (1, 0)):
                        pe.wait_ge(s_ovd, b * 4 + 2 * h + m)
                    for odd in range(2):
                        for g in range(4):
                            head = 8 * m + 2 * g + odd
                            rows = slice(32 * g, 32 * (g + 1))
                            pe.matmul(out[rows, :], vz[:, head, :], ptx[0:SK, head, :], start=odd == 0, stop=odd == 1)
                    for odd in range(2):
                        for g in range(4):
                            head = 8 * m + 2 * g + odd
                            rows = slice(32 * g, 32 * (g + 1))
                            last = pe.matmul(total[rows, :], onez[:, odd, :], ptx[0:SK, head, :], start=odd == 0, stop=odd == 1)
                    last.then_inc(s_ov, 1)

                def project(h):
                    pe.wait_ge(s_ovd, b * 4 + 2 * (h + 1))
                    for i in range(CHUNK * h, CHUNK * (h + 1)):
                        for k in range(KT):
                            last = pe.matmul(sc[:, i // 2, DIM * (i % 2):DIM * (i % 2 + 1)], oTc[:, k, P * i:P * (i + 1)],
                                             wx[:, 3, k, :], start=k == 0, stop=k == KT - 1)
                    last.then_inc(s_wox, 1)

                for u in range(UX + LAG):
                    if u < UX:
                        head_scores(u)
                    if u >= LAG:
                        probs_T(u - LAG)
                    if u in HEADS_OUT_AT:
                        head_out(*HEADS_OUT_AT[u], ob, pj)
                pe.wait_ge(s_sub, b * UX + UX)
                project(0)
                head_out(1, 1, tb[0], tb[1])
                project(1)
                transpose_sequence(b, 2)
                for i in range(TT):
                    for k in range(KT):
                        last = pe.matmul(ob[:, EXPERTS * i:EXPERTS * (i + 1)], xTc[:, k, P * i:P * (i + 1)], sel_w[:, k, :],
                                         start=k == 0, stop=k == KT - 1)
                last.then_inc(s_lg, 1)
                pe.wait_ge(s_mch, b + 1)
                for i in range(TT):
                    out = pj[:, EXPERTS * i:EXPERTS * (i + 1)]
                    pe.matmul(out, tri_b[:], mch[:, i, :], start=True, stop=False)
                    for j in range(i):
                        pe.matmul(out, ones_b[:], mch[:, j, :], start=False, stop=False)
                    last = pe.matmul(out, ones_b[:], macc[:], start=False, stop=True)
                last.then_inc(s_rk, 1)

            pe.wait_ge(s_slot, BATCH + 1)
            pe.matmul(tb[0][0:EXPERTS, 0:P], macc[:], ones_b[:], start=True, stop=True).then_inc(s_m, 1)
            pe.wait_ge(s_mv, 1)
            pe.matmul(tb[1][0:EXPERTS, 0:P], tri_b[0:EXPERTS, 0:EXPERTS], tiles_b[:], start=True, stop=True)
            pe.matmul(ob[:, 0:EXPERTS], tiles_b[:], tri_b[0:EXPERTS, 0:EXPERTS], start=True, stop=True).then_inc(s_m, 1)
            pe.wait_ge(s_mv, 2)
            pe.matmul(sc[:, 0, 0:P], owner[:], blockf[:], start=True, stop=True)
            pe.matmul(sc[:, 1, 0:MOE_TILES], iota_ee[:], owner[:], start=True, stop=True).then_inc(s_m, 1)
            pe.wait_ge(s_tab, 16)
            pe.transpose(sc[:, 2, 0:MOE_TILES], table_t[:], ident[:]).then_inc(s_m, 1)

            pe.sem_inc(s_t3, RING)
            pe.wait_ge(s_map, 1)

            def tile_T(n, s, use):
                pe.wait_ge(s_g[s % RING], use * 16 + 16)
                for k in range(KT):
                    last = pe.transpose(tb[s % 2][:, P * k:P * (k + 1)], xin[:, s % RING, P * k:P * (k + 1)], ident[:])
                last.then_inc(s_t3, 1)

            def tile_keys(n, s):
                pe.wait_ge(s_xg, n + 1)
                for k in range(KT):
                    last = pe.matmul(sc[:, s % 2, 0:P], ksel[:, s % 4, HID * k:HID * (k + 1)], xgT[:, s % 2, P * k:P * (k + 1)],
                                     start=k == 0, stop=k == KT - 1)
                last.then_inc(s_f1, 1)

            def tile_values(n, s):
                pe.wait_ge(s_h, n + 1)
                pe.matmul(sc[:, 2 + s % 2, 0:DIM], hT[:, s % 2, :], vsel[:, s % 2, :],
                          start=True, stop=True).then_inc(s_f2, 1)

            tile_T(0, 0, 0)
            tile_T(1, 1, 0)
            tile_keys(0, 0)
            with pe.Fori(0, MOE_TILES // RING - 1) as it:
                for i in range(RING):
                    s = i + 2
                    n = it * RING + s
                    tile_T(n, s, it + s // RING)
                    tile_keys(n - 1, s - 1)
                    tile_values(n - 2, s - 2)
            for n in range(MOE_TILES - RING + 2, MOE_TILES + 2):
                if n < MOE_TILES:
                    tile_T(n, n, n // RING)
                if n - 1 < MOE_TILES:
                    tile_keys(n - 1, n - 1)
                tile_values(n - 2, n - 2)

        @block.scalar
        def _(act):
            def exps(PB, n):
                _, qi, _ = unit(n)
                act.wait_ge(s_mx, PB * UNITS + n + 1)
                if n >= PROBS:
                    done = sum(1 for c in CHUNKS if c[0] != "sums" and c[0] <= n - PROBS or c[0] == "sums" and n - PROBS >= TT * (c[1] + 1))
                    act.wait_ge(s_t, PB * len(CHUNKS) + done)
                w = (qi + 1) * P
                src = sc[:, 2 * (n % 2):2 * (n % 2) + 2, :].rearrange("p a b -> p (a b)")[:, 0:w]
                act.activation(probs[:, n % PROBS, 0:w], src, ACT.Exp, bias=nmax[:, n:n + 1],
                               accum_out=rs[:, n:n + 1]).then_inc(s_exp, 1)

            def evac(PB, what):
                evac_chunks(act, "act", PB, what, lambda o, i: act.activation(o, i, ACT.Copy))

            def hi(PT, j):
                act.wait_ge(s_rot, PT * 4 + j + 1)
                act.activation(qk_hi[:, j // 2, HALF * (j % 2):HALF * (j % 2 + 1)], rot[:, j % 2], ACT.Copy).then_inc(s_hi, 1)

            def v_out(PT, u, j):
                act.wait_ge(s_pj, PT * 6 + j + 1)
                act.activation(v[:, u, 4 * (j - 4):4 * (j - 3), :], pj[:].rearrange("p (t d) -> p t d", t=4), ACT.Copy).then_inc(s_v, 1)

            def x_T(b, c, bank):
                act.wait_ge(s_xt, b * 4 + c + 1)
                act.activation(xT[:, 1, HALF * (c % 2):HALF * (c % 2 + 1)], bank, ACT.Copy).then_inc(s_xta, 1)

            def deviation(k):
                act.wait_ge(s_var, k)
                act.activation(std[:], veps[:], ACT.Sqrt).then_inc(s_std, 1)

            deviation(1)
            for c in (2, 3):
                x_T(0, c, sc[:, c, :])
            for j in range(4):
                hi(0, j)
            for j in (4, 5):
                v_out(0, 0, j)
            for b in range(BATCH):
                def body(PB, pair, pair2, u, use, nxt, nxt2, first):
                    at = FIRST_PROJ_AT if first else PROJ_AT
                    for k in range(STEPS):
                        if k < UNITS:
                            exps(PB, k)
                        if nxt and first and k == 1:
                            deviation(2 * b + 2)
                        if nxt and at.get(k - 3, 9) < 4:
                            hi(PB + 1, at[k - 3])
                        if k >= LAG:
                            evac(PB, k - LAG)
                        if nxt and first and XT_AT.get(k, 0) >= 2:
                            x_T(b + 1, XT_AT[k], pj[:])
                        if nxt and at.get(k, 0) >= 4:
                            v_out(PB + 1, 1 - u, at[k])
                        if k in GROUP_END:
                            evac(PB, ("sums", GROUP_END[k]))
                pairs(act, b, body)
                def relu(c, m):
                    act.wait_ge(s_h1, b * 4 + 2 * c + m + 1)
                    act.activation(h1T[:, m, HALF * c:HALF * (c + 1)], sc[:, 2 * c + m, :], ACT.Relu).then_inc(s_h1a, 1)

                relu(0, 0)
                relu(0, 1)
                relu(1, 0)
                deviation(last_ln(b, 0))
                relu(1, 1)
                deviation(last_ln(b, 1))

            def ln_and_transposes(b, k):
                act.wait_ge(s_var2, b * 2 + k)
                act.activation(std[:], veps[:], ACT.Sqrt).then_inc(s_std2, 1)
                for h in range(2):
                    act.wait_ge(s_tr2, b * 8 + 4 * (k - 1) + 2 * h + 2)
                    act.activation(xTc[:, 1, HALF * h:HALF * (h + 1)], sc[:, 2 * h + 1, :], ACT.Copy).then_inc(s_tra, 1)

            with act.Fori(0, BATCH) as b:
                ln_and_transposes(b, 1)
                for u in range(UX + LAG):
                    if u < UX:
                        act.wait_ge(s_sub, b * UX + u + 1)
                        act.activation(sx[:, u % SXBUFS], sx[:, u % SXBUFS], ACT.Exp).then_inc(s_ex, 1)
                    if u >= LAG:
                        taken(act, "act", b, u - LAG)
                ln_and_transposes(b, 2)
                act.wait_ge(s_lg, b + 1)
                act.activation(el[:], ob[:].rearrange("p (t e) -> p t e", t=TT), ACT.Exp, scale=-1.0).then_inc(s_el, 1)

            act.wait_ge(s_map, 1)
            act.wait_ge(s_keys, 16 * BATCH)
            def keys_of(n, s):
                e = act.value_load(etile[0:1, bass.ds(n, 1)], min_val=0, max_val=EXPERTS - 1)
                act.activation(ksel[:, s % 4, :], keys[:, bass.ds(e, 1), :].rearrange("p o d -> p (o d)"), ACT.Copy)

            def tile_in(n, s):
                act.wait_ge(s_t3, n + RING + 1)
                act.activation(xgT[:, s % 2, :], tb[s % 2][:, 0:KT * P], ACT.Copy).then_inc(s_xg, 1)

            keys_of(0, 0)
            with act.Fori(0, MOE_TILES // 8 - 1) as it:
                for i in range(8):
                    tile_in(it * 8 + i, i)
                    keys_of(it * 8 + (i + 1), i + 1)
            for n in range(MOE_TILES - 8, MOE_TILES):
                tile_in(n, n)
                if n + 1 < MOE_TILES:
                    keys_of(n + 1, n + 1)

        @block.vector
        def _(dve):
            chain = [0]

            def link(ins):
                chain[0] += 1
                ins.then_inc(s_lnv, 1)
                dve.wait_ge(s_lnv, chain[0])
                apart(dve)

            def ln_stats(src, tiles=range(TT)):
                for i in tiles:
                    last = dve.bn_stats(stats[:, i, :], src(i))
                link(last)
                for i in tiles:
                    last = dve.bn_aggr(mv[:, i, :], stats[:, i, :])
                link(last)
                dve.tensor_scalar(veps[:], mv[:, :, 1], EPS, None, ALU.add).then_inc(s_var, 1)

            def ln_inverse(k):
                dve.wait_ge(s_std, k)
                link(dve.reciprocal(rstd[:], std[:]))

            def x_normalised():
                for i in range(TT):
                    last = dve.tensor_scalar(xn[:, i, :], xn[:, i, :], mv[:, i, 0:1], rstd[:, i:i + 1], ALU.subtract, ALU.mult)
                last.then_inc(s_xn, 1)

            def x_T(b, c, bank):
                dve.wait_ge(s_xt, b * 4 + c + 1)
                dve.tensor_copy(xT[:, 0, HALF * c:HALF * (c + 1)], bank).then_inc(s_xtv, 1)

            def rope(PT, j, first):
                dve.wait_ge(s_pj, PT * 6 + j + 1)
                if j >= 2:
                    dve.wait_ge(s_rot, PT * 4 + j - 1)
                cols = slice(HALF * (j % 2), HALF * (j % 2 + 1))
                bank = proj_bank(j, first)
                dve.tensor_tensor(t1[:, j % 2], bank, cos_t[:, cols], ALU.mult)
                dve.tensor_tensor(t2[0:64, j % 2], bank[64:128], sin_t[64:128, cols], ALU.mult)
                dve.tensor_tensor(t2[64:128, j % 2], bank[0:64], sin_t[0:64, cols], ALU.mult).then_inc(s_rope, 1)

            def row_max(PB, n):
                _, qi, _ = unit(n)
                w = (qi + 1) * P
                dve.wait_ge(s_s, PB * UNITS + n + 1)
                src = sc[:, 2 * (n % 2):2 * (n % 2) + 2, :].rearrange("p a b -> p (a b)")[:, 0:w]
                dve.tensor_reduce(nmax[:, n:n + 1], src, axis=AX, op=ALU.max, negate=True).then_inc(s_mx, 1)

            def inverse_sums(PB, g):
                dve.wait_ge(s_exp, PB * UNITS + TT * (g + 1))
                dve.reciprocal(rsi[:], rs[:, TT * g:TT * (g + 1)]).then_inc(s_rsi, 1)
                dve.wait_ge(s_rsi, PB * 2 + g + 1)
                dve.tensor_copy(rinv[:], rsi[:, :].unsqueeze(2).to_broadcast([P, TT, DH])).then_inc(s_rinv, 1)

            def out_T(PB, pair, g):
                dve.wait_ge(s_pv, PB * 2 + g + 1)
                count = next(c[4] for c in CHUNKS if c[0] == "sums" and c[1] == g)
                dve.wait_ge(s_ev["act"], PB * EVACS["act"] + count)
                dst = oT[:, bass.ds(pair, 1), HALF * g:HALF * (g + 1)].rearrange("p o s -> p (o s)")
                dve.tensor_tensor(dst, ob[:], inv_b[:], ALU.mult).then_inc(s_ot, 1)

            dve.wait_ge(s_x, 16)
            apart(dve)
            ln_stats(lambda i: xn[:, i, :])
            ln_inverse(1)
            x_normalised()
            for c in (0, 1):
                x_T(0, c, sc[:, c, :])
            dve.wait_ge(s_angle, 16 * 2)
            for j in range(4):
                rope(0, j, True)
            for b in range(BATCH):
                def body(PB, pair, pair2, u, use, nxt, nxt2, first):
                    at = FIRST_PROJ_AT if first else PROJ_AT
                    for k in range(STEPS):
                        if 2 <= k < UNITS and k != AHEAD + 1:
                            row_max(PB, k)
                        if k == AHEAD:
                            row_max(PB, AHEAD + 1)
                        if nxt and first and k == 1:
                            dve.wait_ge(s_x, 16 * (b + 2))
                            apart(dve)
                            ln_stats(lambda i: xn[:, i, :])
                        if nxt and first and k == 2:
                            ln_inverse(2 * b + 2)
                            x_normalised()
                        late = k in GROUP_END
                        if late:
                            inverse_sums(PB, GROUP_END[k])
                            evac_chunks(dve, "dve", PB, k - LAG, dve.tensor_copy)
                        if nxt and first and XT_AT.get(k, 9) < 2:
                            x_T(b + 1, XT_AT[k], pj[:])
                        if k >= LAG and not late:
                            evac_chunks(dve, "dve", PB, k - LAG, dve.tensor_copy)
                        if nxt and at.get(k, 9) < 4:
                            rope(PB + 1, at[k], first)
                        if k == 11:
                            out_T(PB, pair, 0)
                    if nxt and not first:
                        for n in range(2):
                            row_max(PB + 1, n)
                    out_T(PB, pair, 1)
                for n in range(2):
                    row_max(b * PAIRS, n)
                pairs(dve, b, body)
                for h in range(2):
                    tiles = range(4 * h, 4 * h + 4)
                    half = slice(4 * h, 4 * h + 4)
                    dve.wait_ge(s_o2, b * 2 + h + 1)
                    apart(dve)
                    o2 = lambda i: ps[i // 2][:, DIM * (i % 2):DIM * (i % 2 + 1)]
                    ln_stats(o2, tiles)
                    ln_inverse(last_ln(b, h))
                    for i in tiles:
                        last = dve.tensor_scalar(on[:, i, :], o2(i), mv[:, i, 0:1], rstd[:, i:i + 1], ALU.subtract, ALU.mult)
                    link(last)
                    dve.wait_ge(s_wo, 16 * 3)
                    link(dve.tensor_tensor(on[:, half], on[:, half], gamma[:, :].unsqueeze(1).to_broadcast([P, 4, DIM]), ALU.mult))
                    dve.wait_ge(s_xr, 16 * (b + 1))
                    last = dve.tensor_tensor(xb[:, half, :], xb[:, half, :], on[:, half], ALU.add)
                last.then_inc(s_x1, 1)

            steps = [0]

            def then(ins, b):
                steps[0] += 1
                ins.then_inc(s_cd, 1)
                dve.wait_ge(s_cd, b * CHAIN_PER_SEQUENCE + steps[0])
                apart(dve)

            def layer_norm(b, k, src):
                for i in range(TT):
                    last = dve.bn_stats(stats[:, i, :], src(i))
                then(last, b)
                for i in range(TT):
                    last = dve.bn_aggr(mv[:, i, :], stats[:, i, :])
                then(last, b)
                dve.tensor_scalar(veps[:], mv[:, :, 1], EPS, None, ALU.add).then_inc(s_var2, 1)
                dve.wait_ge(s_std2, b * 2 + k)
                then(dve.reciprocal(rstd[:], std[:]), b)
                dve.wait_ge(s_st, 16 * BATCH)
                apart(dve)
                for i in range(TT):
                    last = dve.tensor_scalar(x3[:, i, :], src(i), mv[:, i, 0:1], rstd[:, i:i + 1], ALU.subtract, ALU.mult)
                last.then_inc(s_ln, 1)

            def transposes_out(b, k):
                for h in range(2):
                    dve.wait_ge(s_tr2, b * 8 + 4 * (k - 1) + 2 * h + 1)
                    dve.tensor_copy(xTc[:, 0, HALF * h:HALF * (h + 1)], sc[:, 2 * h, :]).then_inc(s_trv, 1)

            dve.wait_ge(s_x1, BATCH)
            apart(dve)
            dve.wait_ge(s_c2, 16 * 9)
            dve.memset(vz[:], 0.0)
            for odd in range(2):
                dve.memset(onez[:, odd, DX * odd:DX * (odd + 1)], 1.0)
                dve.memset(onez[:, odd, DX * (1 - odd):DX * (2 - odd)], 0.0)
            dve.memset(macc[:], 0.0).then_inc(s_slot, 1)
            with dve.Fori(0, BATCH) as b:
                steps[0] = 0
                dve.wait_ge(s_x1c, b * 16 + 16)
                apart(dve)
                layer_norm(b, 1, lambda i: x1c[:, i, :])
                dve.wait_ge(s_mask, b * 16 + 16)
                dve.tensor_scalar(mbias[:], maskc[:], NEG, None, ALU.mult)
                transposes_out(b, 1)
                dve.wait_ge(s_kv, b + 1)
                for m in range(KT):
                    last = dve.tensor_scalar(kT[:, m, :], tb[0][:, SK * m:SK * (m + 1)], bqk[:, 1, m:m + 1], None, ALU.add)
                then(last, b)
                for m in range(KT):
                    dve.tensor_tensor(kblk[:, m], kT[:, m, :].unsqueeze(1).to_broadcast([P, HEADS // 2, SK]),
                                      headm[:, :].unsqueeze(2).to_broadcast([P, HEADS // 2, SK]), ALU.mult)
                for odd in range(2):
                    last = dve.tensor_tensor(vz[:].rearrange("s (g o) d -> s g o d", o=2)[:, :, odd, DX * odd:DX * (odd + 1)],
                                             tb[1][0:SK, 0:DIM].rearrange("s (g o d) -> s g o d", o=2, d=DX)[:, :, odd, :],
                                             bvo[0:SK, 0, :].rearrange("s (g o d) -> s g o d", o=2, d=DX)[:, :, odd, :], ALU.add)
                last.then_inc(s_kvd, 1)
                for n in range(4):
                    h, m = n // 2, n % 2
                    dve.wait_ge(s_q2, b * 4 + n + 1)
                    dve.tensor_scalar(qT[:, m, HALF * h:HALF * (h + 1)], q_bank[n][:], bqk[:, 0, m:m + 1], DX ** -0.5,
                                      ALU.add, ALU.mult).then_inc(s_qd, 1)

                def score_max(u):
                    m = u % 2
                    dve.wait_ge(s_sx, b * UX + u + 1)
                    dve.tensor_reduce(mx[:, m, :].rearrange("p (j h) -> p j h", j=2),
                                      sc[:, 2 * m:2 * m + 2, 0:4 * SK].rearrange("p j (h k) -> p j h k", h=4),
                                      axis=AX, op=ALU.max).then_inc(s_mxx, 1)

                def score_shift(u):
                    m = u % 2
                    if u >= SXBUFS:
                        dve.wait_ge(s_px, b * (2 * UX) + 2 * (u - SXBUFS + 1))
                    dve.wait_ge(s_mxx, b * UX + u + 1)
                    dve.tensor_tensor(sx[:, u % SXBUFS].rearrange("p (j h) k -> p j h k", j=2),
                                      sc[:, 2 * m:2 * m + 2, 0:4 * SK].rearrange("p j (h k) -> p j h k", h=4),
                                      mx[:, m, :].rearrange("p (j h) -> p j h", j=2).unsqueeze(3).to_broadcast([P, 2, 4, SK]),
                                      ALU.subtract).then_inc(s_sub, 1)

                def normalised(n, out, total):
                    dve.wait_ge(s_ov, b * 4 + n + 1)
                    dve.reciprocal(itotal[:, n % 2], total[:]).then_inc(s_tot, 1)
                    dve.wait_ge(s_tot, b * 4 + n + 1)
                    h, m = n // 2, n % 2
                    dve.tensor_tensor(oTc[:, m, HALF * h:HALF * (h + 1)], out[:], itotal[:, n % 2], ALU.mult).then_inc(s_ovd, 1)

                for u in range(UX + LAG):
                    if u < UX:
                        score_max(u)
                        score_shift(u)
                    if u >= LAG:
                        taken(dve, "dve", b, u - LAG)
                    if u in NORMALISED_AT:
                        normalised(NORMALISED_AT[u], ob, pj)
                dve.wait_ge(s_bo, b + 1)
                for i in range(4):
                    if i == 2:
                        normalised(3, tb[0], tb[1])
                    dve.wait_ge(s_wox, b * 2 + i // 2 + 1)
                    last = dve.tensor_tensor(x2[:, bass.ds(b * TT + 2 * i, 2), :], sc[:, i, :].rearrange("p (t d) -> p t d", t=2),
                                             x1c[:, 2 * i:2 * i + 2, :], ALU.add)
                last.then_inc(s_x2, 1)
                dve.wait_ge(s_x2, b + 1)
                apart(dve)
                layer_norm(b, 2, lambda i: x2[:, bass.ds(b * TT + i, 1), :].rearrange("p o d -> p (o d)"))
                transposes_out(b, 2)
                dve.wait_ge(s_el, b + 1)
                then(dve.tensor_scalar(el[:], el[:], 1.0, None, ALU.add), b)
                then(dve.reciprocal(sel[:], el[:]), b)
                for i in range(TT):
                    last = dve.max(top[:, i, :], sel[:, i, :])
                then(last, b)
                for i in range(TT):
                    last = dve.max_index(topi[:, i, :], top[:, i, :], sel[:, i, :])
                then(last, b)
                cols = bass.ts(b, NOTES)
                dve.tensor_copy(gate[:, cols].rearrange("p (t j) -> p t j", t=TT), top[:, :, 0:TOPK])
                then(dve.tensor_copy(expert[:, cols].rearrange("p (t j) -> p t j", t=TT), topi[:, :, 0:TOPK]), b)
                then(dve.tensor_tensor(chose[:, cols, :], iota_e[:, :].unsqueeze(1).to_broadcast([P, NOTES, EXPERTS]),
                                       expert[:, cols].unsqueeze(2).to_broadcast([P, NOTES, EXPERTS]), ALU.is_equal), b)
                with nc.allow_low_precision(reason="sums of zeros and ones, exact in bfloat16"):
                    dve.tensor_reduce(mch[:], chose[:, cols, :].rearrange("p (t j) e -> p t e j", t=TT), axis=AX, op=ALU.add).then_inc(s_mch, 1)
                dve.wait_ge(s_rk, b + 1)
                for i in range(TT):
                    last = dve.tensor_tensor(prod[:, TOPK * i:TOPK * (i + 1), :], chose[:, bass.ds(b * NOTES + TOPK * i, TOPK), :],
                                             pj[:, EXPERTS * i:EXPERTS * (i + 1)].unsqueeze(1).to_broadcast([P, TOPK, EXPERTS]), ALU.mult)
                then(last, b)
                dve.tensor_reduce(msum[:], mch[:].rearrange("p t e -> p e t"), axis=AX, op=ALU.add)
                then(dve.tensor_reduce(rank[:, cols], prod[:], axis=AX, op=ALU.add), b)
                dve.tensor_tensor(macc[:], macc[:], msum[:], ALU.add)
                then(dve.scalar_tensor_tensor(slotf[:], expert[:, cols], float(PLACES), rank[:, cols], ALU.mult, ALU.add), b)
                dve.tensor_copy(tokens[:], tokid[:, bass.ts(b, TT)])
                dve.tensor_copy(slots[:], slotf[:]).then_inc(s_slot, 1)
            assert steps[0] == CHAIN_PER_SEQUENCE, steps

            made = [0]

            def do(ins):
                made[0] += 1
                ins.then_inc(s_md, 1)
                dve.wait_ge(s_md, made[0])

            dve.wait_ge(s_c3, 16 * 3)
            dve.wait_ge(s_m, 1)
            do(dve.tensor_copy(cnt[:], tb[0][0:EXPERTS, 0:P]))
            do(dve.tensor_scalar(cnti[:, 0], cnt[:], float(P - 1), None, ALU.add))
            do(dve.tensor_scalar(cnti[:, 1], cnti[:, 0], P.bit_length() - 1, None, ALU.arith_shift_right))
            dve.tensor_copy(tiles_f[:], cnti[:, 1])
            dve.tensor_copy(tiles_b[:], cnti[:, 1]).then_inc(s_mv, 1)
            dve.wait_ge(s_m, 2)
            dve.tensor_copy(first_b[:], ob[:, 0:EXPERTS])
            do(dve.tensor_copy(first[:], tb[1][0:EXPERTS, 0:P]))
            do(dve.tensor_tensor(after[:], first[:, 0:1], tiles_f[:, 0:1], ALU.add))
            dve.tensor_scalar(begun[:, 0], iota_t[:], first[:, 0:1], None, ALU.is_ge)
            do(dve.tensor_scalar(begun[:, 1], iota_t[:], after[:, 0:1], None, ALU.is_ge))
            do(dve.scalar_tensor_tensor(blockf[:], iota_ee[:], float(PLACES // P), first[:], ALU.mult, ALU.subtract))
            dve.tensor_tensor(owner[:], begun[:, 0], begun[:, 1], ALU.subtract).then_inc(s_mv, 1)
            dve.wait_ge(s_m, 3)
            dve.tensor_tensor(block_i[:], sc[:, 0, 0:1], iota_pt[:, 0:1], ALU.add).then_inc(s_blk, 1)
            dve.tensor_copy(etile[:], sc[:, 1, 0:MOE_TILES])
            for q in range(BATCH):
                cols = slice(NOTES * q, NOTES * (q + 1))
                do(dve.tensor_tensor(prod3, chose[:, cols, :], first_b[:, :].unsqueeze(1).to_broadcast([P, NOTES, EXPERTS]), ALU.mult))
                do(dve.tensor_reduce(ybase[:, cols], prod3, axis=AX, op=ALU.add))
            do(dve.scalar_tensor_tensor(ybase[:], ybase[:], float(P), rank[:], ALU.mult, ALU.add))
            do(dve.tensor_copy(yslot[:], ybase[:]))
            dve.wait_ge(s_m, 4)
            do(dve.tensor_copy(rowidx[:], sc[:, 2, 0:MOE_TILES]))
            dve.sem_inc(s_map, 1)

            dve.wait_ge(s_vals, 16)

            def hidden(n, s):
                e = dve.value_load(etile[0:1, bass.ds(n, 1)], min_val=0, max_val=EXPERTS - 1)
                dve.tensor_copy(vsel[:, s % 2, :], vals[:, bass.ds(e, 1), :].rearrange("p o d -> p (o d)"))
                dve.wait_ge(s_f1, n + 1)
                dve.tensor_scalar(hT[:, s % 2, :], sc[:, s % 2, 0:P], 0.0, None, ALU.max).then_inc(s_h, 1)

            def result(n, s):
                dve.wait_ge(s_f2, n + 1)
                if not isinstance(n, int) or n >= 4:
                    dve.wait_ge(s_ys[s % 4], (n - s % 4) * 4)
                dve.tensor_copy(ysb[:, s % 4, :], sc[:, 2 + s % 2, 0:DIM]).then_inc(s_y, 1)

            for n in range(5):
                hidden(n, n)
                if n >= 1:
                    result(n - 1, n - 1)
            with dve.Fori(0, (MOE_TILES - 8) // 8) as it:
                for i in range(8):
                    hidden(it * 8 + 5 + i, 5 + i)
                    result(it * 8 + 4 + i, 4 + i)
            for n in range(MOE_TILES - 3, MOE_TILES + 1):
                if n < MOE_TILES:
                    hidden(n, n)
                result(n - 1, n - 1)
            dve.sem_inc(s_comb, RING)
            with dve.Fori(0, TILES_IN * TOPK // RING) as it:
                for i in range(RING):
                    dve.wait_ge(s_cg[i], it * 16 + 16)
                    row = x2[:, bass.ds(it * (RING // TOPK) + i // TOPK, 1), :].rearrange("p o d -> p (o d)")
                    dve.scalar_tensor_tensor(row, xin[:, i, :], gate[:, bass.ds(it * RING + i, 1)], row, ALU.mult, ALU.add).then_inc(s_comb, 1)
                    dve.wait_ge(s_comb, it * RING + (i + 1 + RING))

CHAIN_PER_SEQUENCE = 16


def constants():
    inv = (1.0 / 10000.0 ** (np.arange(0, DH, 2, dtype=np.float32) / DH)).astype(np.float32)
    ang = np.arange(SEQ, dtype=np.float32)[:, None] * inv[None, :]
    cos, sin = np.cos(ang).T.astype(np.float32), np.sin(ang).T.astype(np.float32)
    bf = np.dtype("bfloat16")
    eye = np.eye(P, dtype=np.float32)
    i = np.arange(P)
    return {
        "cos": np.ascontiguousarray(np.tile(cos, (4, 1))),
        "sin": np.ascontiguousarray(np.concatenate([sin, sin, -sin, -sin])),
        "ident": eye,
        "tri_b": (i[:, None] < i[None, :]).astype(bf),
        "ones_b": np.ones((P, P), bf),
        "tokid": (P * np.arange(TILES_IN)[None, :] + i[:, None]).astype(np.float32),
        "headm": (i[:, None] // DX == np.arange(HEADS // 2)[None, :]).astype(np.float32),
        "iota_e": np.tile(np.arange(EXPERTS, dtype=np.float32), (P, 1)),
        "iota_t": np.tile(np.arange(MOE_TILES, dtype=np.float32), (EXPERTS, 1)),
        "iota_ee": np.tile(np.arange(EXPERTS, dtype=np.float32)[:, None], (1, P)),
        "iota_pt": (P * np.arange(MOE_TILES)[None, :] + i[:, None]).astype(np.float32),
        "ident_b": eye.astype(bf),
        "causal_b": np.where(i[None, :] > i[:, None], np.float32(NEG), np.float32(0)).astype(bf),
    }


def layout(inputs):
    a = {k: np.asarray(v) for k, v in inputs.items()}
    out = dict(constants())
    out["x"] = a["x"]
    w = a["L0_attn_W_qkv"].reshape(KT, P, 3, PAIRS, 2, 2, DH // 2)
    q, k, v = w[:, :, 0], w[:, :, 1], w[:, :, 2]
    perm = lambda z: z.transpose(2, 1, 0, 4, 3, 5).reshape(PAIRS, P, KT, P)
    out["wqkv"] = np.concatenate([perm(q), perm(k), v.transpose(2, 1, 0, 3, 4, 5).reshape(PAIRS, P, KT, P)], axis=3)
    out["wo1"] = a["L0_attn_W_o1"].reshape(PAIRS, P, DIM).transpose(1, 0, 2)
    out["wo2"] = a["L0_attn_W_o2"].reshape(KT, P, DIM).transpose(1, 0, 2)
    out["gamma"] = np.broadcast_to(a["L0_attn_gamma"], (P, DIM))
    lay = lambda w: w.T.reshape(KT, P, -1).transpose(1, 0, 2)
    out["wx"] = np.stack([lay(a["L0_xattn_" + n]) for n in ("Wq", "Wk", "Wv", "Wo")], axis=1)
    out["bqk"] = np.stack([a["L0_xattn_" + n].reshape(KT, P).T for n in ("bq", "bk")], axis=1)
    out["bvo"] = np.stack([np.broadcast_to(a["L0_xattn_" + n], (P, DIM)) for n in ("bv", "bo")], axis=1)
    out["ctxT"] = a["ctx_1024"].reshape(BATCH, SK, KT, P).transpose(0, 3, 2, 1)
    out["mask"] = a["mask_BxSxS2_bk1"].reshape(BATCH, TT, P, SK).transpose(0, 2, 1, 3)
    out["sel_w"] = lay(a["L0_ffn_expert_sel"])
    out["keys"] = a["L0_ffn_keys"].reshape(EXPERTS, KT, P, HID).transpose(2, 0, 1, 3).reshape(P, EXPERTS, KT * HID)
    out["vals"] = a["L0_ffn_values"].transpose(1, 0, 2)
    return {k: np.ascontiguousarray(v) for k, v in out.items()}


def make(nc, arrays):
    t = {}
    for name, arr in arrays.items():
        t[name] = nc.dram_tensor("in_" + name, arr.shape, mybir.dt.from_np(arr.dtype), kind="ExternalInput").ap()
    t["x1"] = nc.dram_tensor("x1", (BATCH, SEQ, DIM), F32, kind="Internal").ap()
    t["x3"] = nc.dram_tensor("x3_rows", (BATCH, SEQ, DIM), F32, kind="Internal").ap()
    t["table"] = nc.dram_tensor("table", (EXPERTS * PLACES, 1), F32, kind="Internal").ap()
    t["yg"] = nc.dram_tensor("yg", (MOE_TILES * P, DIM), F32, kind="Internal").ap()
    t["out"] = nc.dram_tensor("out", (BATCH * SEQ, DIM), F32, kind="ExternalOutput").ap()
    build_program(nc, t)


def kernel(**inputs):
    import concourse.bacc as bacc
    from concourse.bass_utils import run_bass_kernel_spmd

    nc = bacc.Bacc("TRN2", target_bir_lowering=False, num_devices=1)
    arrays = layout(inputs)
    make(nc, arrays)
    result = run_bass_kernel_spmd(nc, [{"in_" + k: v for k, v in arrays.items()}], core_ids=[0])
    return result.results[0]["out"].reshape(BATCH, SEQ, DIM)
```
